# Optimizing a Trainium2 kernel written in Bass

```python
import numpy as np
import jax
import jax.numpy as jnp

def _softmax(x, axis=-1):
    return jax.nn.softmax(x, axis=axis)

def _gelu(x):
    return jax.nn.gelu(x, approximate=True)

def _silu(x):
    return jax.nn.silu(x)

def _sigmoid(x):
    return jax.nn.sigmoid(x)

def _layernorm(x, axis=-1, eps=1e-05):
    m = jnp.mean(x, axis=axis, keepdims=True)
    v = jnp.var(x, axis=axis, keepdims=True)
    return (x - m) / jnp.sqrt(v + eps)

def _scatter_add(tgt, idx, src, axis=0):
    return tgt.at[idx].add(src)

def _segment_sum(src, seg, n):
    return jax.ops.segment_sum(src, seg, n)
kernel_name = 'mk_gps_d1_gnn_r8_a6d8d4'

def setup_inputs(seed: int=0):
    np.random.seed(seed)
    _w = jnp.asarray

    def _rec_inputs():
        import jax
        import jax.numpy as jnp
        _gk = jax.random.key(seed)
        x = -0.0002117 + 1 * jax.random.normal(jax.random.fold_in(_gk, 1), (6250, 256), jnp.float32)
        src = jax.random.randint(jax.random.fold_in(_gk, 2), (200000,), 0, 6250, jnp.int32)
        dst = jax.random.randint(jax.random.fold_in(_gk, 3), (200000,), 0, 6250, jnp.int32)
        _o = jnp.argsort(dst, stable=True)
        src = src[_o]
        dst = dst[_o]
        return (x, src, dst)
    x, src, dst = _rec_inputs()

    def _L0_gnn_setup():
        import jax, jax.numpy as jnp
        import numpy as np
        key = jax.random.key(seed)
        k0, k1, k2 = jax.random.split(key, 3)
        N, E, C_IN, C_HID = (12500, 200000, 256, 256)
        x = jax.random.normal(k0, (N, C_IN), dtype=jnp.float32)
        edge_index = jax.random.randint(k1, (2, E), 0, N, dtype=jnp.int64)
        W = jax.random.normal(k2, (C_IN, C_HID), dtype=jnp.float32) / np.sqrt(C_IN).astype(np.float32)
        b = jnp.zeros((C_HID,), dtype=jnp.float32)
        prelu_a = jnp.full((C_HID,), 0.25, dtype=jnp.float32)
        return {'x': x, 'edge_index': edge_index, 'k_centers': 7, 'W': W, 'b': b, 'prelu_a': prelu_a}
    _L0_gnn_all = _L0_gnn_setup()
    _L0_gnn_in = {k: v for k, v in _L0_gnn_all.items() if k in ('W', 'b', 'prelu_a')}
    del _L0_gnn_all

    def _L0_mix_setup():
        import jax, jax.numpy as jnp
        import numpy as np
        HEADS = 4
        DIM_HEAD = 32
        key = jax.random.key(seed)
        k1, k2, k3 = jax.random.split(key, 3)
        B, L, D = (16, 1024, 256)
        hidden = HEADS * DIM_HEAD
        x = jax.random.normal(k1, (B, L, D), dtype=jnp.float32)
        W_qkv = jax.random.normal(k2, (D, 3 * hidden), dtype=jnp.float32) * D ** (-0.5)
        W_out = jax.random.normal(k3, (hidden, D), dtype=jnp.float32) * hidden ** (-0.5)
        b_out = jnp.zeros((D,), dtype=jnp.float32)
        return {'x': x, 'W_qkv': W_qkv, 'W_out': W_out, 'b_out': b_out}
    _L0_mix_all = _L0_mix_setup()
    _L0_mix_in = {k: v for k, v in _L0_mix_all.items() if k in ('W_qkv', 'W_out', 'b_out')}
    del _L0_mix_all

    def _L0_ffn_setup():
        import jax, jax.numpy as jnp
        import numpy as np
        D_MODEL = 256
        EXPERT_DIM = 512
        NUM_EXPERTS = 8
        TOP_K = 2
        SEQ_LEN = 256
        BATCH = 2
        key = jax.random.key(seed)
        ks = jax.random.split(key, 8)
        s = 0.02
        x = jax.random.normal(ks[0], (SEQ_LEN, BATCH, D_MODEL), dtype=jnp.float32)
        Wg = jax.random.normal(ks[1], (D_MODEL, NUM_EXPERTS), dtype=jnp.float32) * s
        bg = jax.random.normal(ks[2], (NUM_EXPERTS,), dtype=jnp.float32) * s
        bias = jnp.zeros((NUM_EXPERTS,), dtype=jnp.float32)
        W1 = jax.random.normal(ks[3], (NUM_EXPERTS, D_MODEL, EXPERT_DIM), dtype=jnp.float32) * s
        b1 = jax.random.normal(ks[4], (NUM_EXPERTS, EXPERT_DIM), dtype=jnp.float32) * s
        W2 = jax.random.normal(ks[5], (NUM_EXPERTS, EXPERT_DIM, D_MODEL), dtype=jnp.float32) * s
        b2 = jax.random.normal(ks[6], (NUM_EXPERTS, D_MODEL), dtype=jnp.float32) * s
        return {'x': x, 'Wg': Wg, 'bg': bg, 'bias': bias, 'W1': W1, 'b1': b1, 'W2': W2, 'b2': b2}
    _L0_ffn_all = _L0_ffn_setup()
    _L0_ffn_in = {k: v for k, v in _L0_ffn_all.items() if k in ('Wg', 'bg', 'bias', 'W1', 'b1', 'W2', 'b2')}
    del _L0_ffn_all
    return {'x': x, 'src': src, 'dst': dst, 'L0_gnn_W': _L0_gnn_in['W'], 'L0_gnn_b': _L0_gnn_in['b'], 'L0_gnn_prelu_a': _L0_gnn_in['prelu_a'], 'L0_mix_W_qkv': _L0_mix_in['W_qkv'], 'L0_mix_W_out': _L0_mix_in['W_out'], 'L0_mix_b_out': _L0_mix_in['b_out'], 'L0_ffn_Wg': _L0_ffn_in['Wg'], 'L0_ffn_bg': _L0_ffn_in['bg'], 'L0_ffn_bias': _L0_ffn_in['bias'], 'L0_ffn_W1': _L0_ffn_in['W1'], 'L0_ffn_b1': _L0_ffn_in['b1'], 'L0_ffn_W2': _L0_ffn_in['W2'], 'L0_ffn_b2': _L0_ffn_in['b2']}

def reference(x, src, dst, L0_gnn_W, L0_gnn_b, L0_gnn_prelu_a, L0_mix_W_qkv, L0_mix_W_out, L0_mix_b_out, L0_ffn_Wg, L0_ffn_bg, L0_ffn_bias, L0_ffn_W1, L0_ffn_b1, L0_ffn_W2, L0_ffn_b2):
    import jax
    import jax.numpy as jnp

    def _L0_gnn_ref(x, edge_index, k_centers, W, b, prelu_a):
        import jax, jax.numpy as jnp
        import numpy as np
        N = x.shape[0]
        loop = jnp.arange(N, dtype=edge_index.dtype)
        src = jnp.concatenate([edge_index[0], loop])
        dst = jnp.concatenate([edge_index[1], loop])
        deg = jax.ops.segment_sum(jnp.ones_like(dst, dtype=x.dtype), dst, num_segments=N)
        dinv = jnp.where(deg > 0, jax.lax.rsqrt(deg), jnp.zeros_like(deg))
        norm = dinv[src] * dinv[dst]
        h = x @ W
        out = jax.ops.segment_sum(h[src] * norm[:, None], dst, num_segments=N) + b
        return jnp.where(out > 0, out, prelu_a * out)

    def _L0_mix_ref(x, W_qkv, W_out, b_out):
        import jax, jax.numpy as jnp
        import numpy as np
        HEADS = 4
        DIM_HEAD = 32
        B, L, D = x.shape
        scale = DIM_HEAD ** (-0.5)
        qkv = jnp.einsum('bld,df->blf', x, W_qkv)
        qkv = qkv.reshape(B, L, 3, HEADS, DIM_HEAD)
        q = jnp.transpose(qkv[:, :, 0], (0, 2, 1, 3)) * scale
        k = jax.nn.softmax(jnp.transpose(qkv[:, :, 1], (0, 2, 1, 3)), axis=2)
        v = jnp.transpose(qkv[:, :, 2], (0, 2, 1, 3))
        context = jnp.einsum('bhld,bhle->bhde', k, v)
        out = jnp.einsum('bhde,bhld->bhle', context, q)
        out = jnp.transpose(out, (0, 2, 1, 3)).reshape(B, L, HEADS * DIM_HEAD)
        return jnp.einsum('blf,fd->bld', out, W_out) + b_out

    def _L0_ffn_ref(x, Wg, bg, bias, W1, b1, W2, b2):
        import jax, jax.numpy as jnp
        import numpy as np
        D_MODEL = 256
        EXPERT_DIM = 512
        NUM_EXPERTS = 8
        TOP_K = 2
        SEQ_LEN = 256
        BATCH = 2
        x_flat = x.reshape(-1, D_MODEL)
        gate_logits = x_flat @ Wg + bg + bias
        topk_vals, topk_idx = jax.lax.top_k(gate_logits, TOP_K)
        topk_w = jax.nn.softmax(topk_vals, axis=-1)
        combine = (jax.nn.one_hot(topk_idx, NUM_EXPERTS, dtype=x.dtype) * topk_w[..., None]).sum(axis=1)
        h = jax.nn.relu(jnp.einsum('td,edh->teh', x_flat, W1) + b1)
        y = jnp.einsum('teh,ehd->ted', h, W2) + b2
        out = jnp.einsum('ted,te->td', y, combine)
        return out.reshape(x.shape)
    edge_index = jnp.stack([src, dst])
    xn = _layernorm(x, axis=-1)
    x = x + _L0_gnn_ref(xn, edge_index, 7, L0_gnn_W, L0_gnn_b, L0_gnn_prelu_a) + _L0_mix_ref(xn[None], L0_mix_W_qkv, L0_mix_W_out, L0_mix_b_out)[0]
    x = x + _L0_ffn_ref(_layernorm(x, axis=-1)[None], L0_ffn_Wg, L0_ffn_bg, L0_ffn_bias, L0_ffn_W1, L0_ffn_b1, L0_ffn_W2, L0_ffn_b2)[0]
    return x

_drawn_inputs = setup_inputs


def setup_inputs(seed=0):
    import zlib

    import numpy as np

    out = dict(_drawn_inputs(seed))
    spreads = {'L0_gnn_b': (0.0, 0.1),
     'L0_gnn_prelu_a': (0.25, 0.6),
     'L0_mix_b_out': (0.0, 0.1),
     'L0_ffn_bias': (0.0, 0.1)}
    factors = {'L0_ffn_bg': 4.146, 'L0_ffn_b1': 8.0, 'L0_ffn_b2': 3.982}
    for name, (base, spread) in spreads.items():
        noise = np.random.default_rng([zlib.crc32(name.encode()), seed]).standard_normal(out[name].shape)
        drawn = base * np.exp(spread * noise) if base else spread * noise
        out[name] = jnp.asarray(drawn.astype(out[name].dtype))
    for name, factor in factors.items():
        out[name] = (out[name] * factor).astype(out[name].dtype)
    return out
```

```python
from contextlib import ExitStack

import concourse.bass as bass
from concourse import mybir

F32 = mybir.dt.float32
BF16 = mybir.dt.bfloat16
I32 = mybir.dt.int32
U32 = mybir.dt.uint32
ALU = mybir.AluOpType
ACT = mybir.ActivationFunctionType
AX_X = mybir.AxisListType.X

P = 128
NODES, D = 6250, 256
EDGES = 200000
KC = D // P
HEADS, HEAD = 4, 32
HID = HEADS * HEAD
EXPERTS, EXPERT_DIM = 8, 512
FC = EXPERT_DIM // P
EPS = 1e-5

BLOCKS = -(-NODES // P)
LAST_ROWS = NODES - (BLOCKS - 1) * P
GROUP = 8
GROUPS = 4
STEP_TILES = GROUP * GROUPS
TILES = BLOCKS * STEP_TILES
FULL_TILES = EDGES // P
LAST_EDGES = EDGES - FULL_TILES * P
CHUNKS = -(-TILES // P)
COLS = CHUNKS * P
WINDOW = 64
ACC_COLS = BLOCKS * P + WINDOW
PAIRS = (BLOCKS - 3) // 2
OFF_GRID = 1.0e6


def gps_layer(nc, x, src, dst, w_gnn, b_gnn, prelu_a, w_qkv, w_out, b_out, w_gate, b_gate, gate_bias,
              w1, b1, w2, b2, out, table, xnt):
    assert EDGES <= TILES * P and GROUPS == 4 and BLOCKS % 2 == 1

    with ExitStack() as ctx:
        def sb(name, shape, dt=F32):
            return ctx.enter_context(nc.sbuf_tensor(name, shape, dt))

        def sem(name):
            return ctx.enter_context(nc.semaphore(name))

        def wait(eng, semaphore, value):
            if isinstance(value, int) and value <= 0:
                return
            eng.wait_ge(semaphore, value)

        s_passed = {name: sem(f"s_passed_{name}") for name in ("act", "dve", "pool", "pe")}

        def passed(eng, name):
            eng.sem_inc(s_passed[name], 1)

        psum = [ctx.enter_context(nc.psum_tensor(f"bank{n}", [P, 512], F32)) for n in range(8)]

        src_t = sb("src_t", [P, COLS], I32)
        dst_t = sb("dst_t", [P, COLS])
        rel = sb("rel", [P, COLS])
        base = sb("base", [1, COLS // GROUP], I32)
        ident = sb("ident", [P, P])
        ones = sb("ones", [P, P])
        iota_b = sb("iota_b", [P, P], BF16)
        iota_w = sb("iota_w", [P, WINDOW])
        iota_n = sb("iota_n", [P, P])
        iota_e = sb("iota_e", [P, EXPERTS])
        dinv = sb("dinv", [P, BLOCKS])
        flag = sb("flag", [P, 4])
        flag_i = sb("flag_i", [1, 1], I32)
        wgnn_sb = sb("wgnn_sb", [P, KC, D])
        wqkv_sb = sb("wqkv_sb", [P, KC, 3 * HID])
        wout_sb = sb("wout_sb", [P, D])
        mix_w = sb("mix_w", [P, KC, D])
        wgate_sb = sb("wgate_sb", [P, KC, EXPERTS])
        b1_t = sb("b1_t", [P, EXPERTS * FC])
        b2_sb = sb("b2_sb", [EXPERTS, D])
        rows = sb("rows", [1, 3 * D + 2 * EXPERTS])
        bgnn_bc = sb("bgnn_bc", [P, D])
        prelu_bc = sb("prelu_bc", [P, D])
        bout_bc = sb("bout_bc", [P, D])
        gate_bc = sb("gate_bc", [P, EXPERTS])
        eps_sb = sb("eps_sb", [P, 1])

        acc_region = sb("acc_region", [P, 2 * ACC_COLS])
        w_region = sb("w_region", [P, 2 * EXPERTS * FC * D])
        g_region = sb("g_region", [P, STEP_TILES * D])

        acc_t = acc_region[:, :].rearrange("p (c n) -> p c n", c=KC)
        k_t = acc_region[:, 0:BLOCKS * P]
        v_all = acc_region[:, BLOCKS * P:2 * BLOCKS * P].rearrange("p (b e) -> p b e", e=P)
        x_all = w_region[:, 0:BLOCKS * D].rearrange("p (b d) -> p b d", d=D)
        w1_sb = w_region[:, 0:EXPERTS * FC * D].rearrange("p (e k f) -> p e k f", e=EXPERTS, k=KC)
        w2_sb = w_region[:, EXPERTS * FC * D:].rearrange("p (e f d) -> p e f d", e=EXPERTS, f=FC)
        gathered = g_region[:, :].rearrange("p (t d) -> p t d", d=D)
        raw_i = acc_region[:, 0:2 * COLS].bitcast(I32)
        raw_f = acc_region[:, 2 * COLS:4 * COLS]
        check = acc_region[:, 4 * COLS:7 * COLS]
        digit_a = g_region[:, 0:COLS]
        digit_b = g_region[:, COLS:2 * COLS]
        dst_i = g_region[:, 2 * COLS:3 * COLS].bitcast(I32)
        hot_b = g_region[:, 3 * COLS:3 * COLS + GROUP * P].bitcast(BF16).rearrange(
            "p (r t n) -> p r t n", r=2, t=GROUP)
        spare = 3 * COLS + GROUP * P
        hot_a = g_region[:, spare:spare + GROUP * BLOCKS].bitcast(BF16).rearrange(
            "p (r t n) -> p r t n", r=2, t=GROUP)
        spare += GROUP * BLOCKS
        xn_buf = g_region[:, spare:spare + 2 * D].rearrange("p (r d) -> p r d", r=2)
        spare += 2 * D
        assert spare <= STEP_TILES * D

        hot_w = sb("hot_w", [P, 2, GROUP, WINDOW])
        index = sb("index", [P, STEP_TILES], I32)
        x_ld = sb("x_ld", [P, 2, D])
        xt_ld = sb("xt_ld", [P, 2, KC, P])
        h_ld = sb("h_ld", [P, 2, D])
        agg_t = sb("agg_t", [P, KC, P])
        tmp = sb("tmp", [P, 2, D])
        acc = sb("acc", [P, 2, D])
        stats = sb("stats", [P, 6])
        mv = sb("mv", [P, 4])
        xn2 = sb("xn2", [P, D])
        x2_t = sb("x2_t", [P, 2, KC, P])
        gate = sb("gate", [P, 8, EXPERTS])
        gate_i = sb("gate_i", [P, EXPERTS], U32)
        comb = sb("comb", [P, 2, EXPERTS])
        comb_t = sb("comb_t", [EXPERTS, P])
        hid_t = sb("hid_t", [P, 2, FC, P])
        xt_buf = x_ld[:, :, :].rearrange("p r (k n) -> p r k n", k=KC)
        stat6 = hid_t[:, 0, :, :].rearrange("p f n -> p (f n)")[:, 0:BLOCKS * 6].rearrange(
            "p (b s) -> p b s", s=6)
        ln = hid_t[:, 1, :, :].rearrange("p f n -> p (f n)")[:, 0:8 * BLOCKS].rearrange(
            "p (r b) -> p r b", r=8)
        b1_rows = agg_t[0:EXPERTS * FC, 0, :]
        exp_t = xt_ld[:, :, :, :].rearrange("p r k n -> p (r k n)")
        exp_n = h_ld[:, :, :].rearrange("p r d -> p (r d)")
        kmax = mv[:, 0:1]
        ctx_m = tmp[:, 0, 0:P]
        ctx_mt = tmp[:, 0, P:2 * P]
        ctx_w = tmp[:, 1, :]
        wq_t = hid_t[:, 1, 0:KC, :]
        shifted = gate[:, 0, :]

        s_pad = sem("s_pad")
        s_edges = sem("s_edges")
        s_x = sem("s_x")
        s_w = sem("s_w")
        s_const = sem("s_const")
        s_rawf = sem("s_rawf")
        s_turned = sem("s_turned")
        s_dv = sem("s_dv")
        s_basebc = sem("s_basebc")
        s_bad = sem("s_bad")
        s_badsum = sem("s_badsum")
        s_var = sem("s_var")
        s_std = sem("s_std")
        s_bn = sem("s_bn")
        s_idc = sem("s_idc")

        with nc.Block() as block:
            @block.sync
            def _(sp):
                sp.wait_ge(s_pad, 4)
                whole = (CHUNKS - 1) * P * P
                rest = FULL_TILES - (CHUNKS - 1) * P
                for n, edges in ((0, src), (1, dst)):
                    raw = raw_i[:, n * COLS:(n + 1) * COLS].rearrange("t (c e) -> t c e", e=P)
                    sp.dma_start(raw[:, 0:CHUNKS - 1, :],
                                 edges[0:whole].rearrange("(c t e) -> t c e", t=P, e=P)).then_inc(s_edges, 16)
                    sp.dma_start(raw[0:rest, CHUNKS - 1, :],
                                 edges[whole:FULL_TILES * P].rearrange("(t e) -> t e", e=P)).then_inc(s_edges, 16)
                    sp.dma_start(raw[rest:rest + 1, CHUNKS - 1, 0:LAST_EDGES],
                                 edges[FULL_TILES * P:EDGES].rearrange("(a e) -> a e", a=1)).then_inc(s_edges, 16)
                for b in range(0, BLOCKS - 1, 12):
                    sp.dma_start(x_all[:, b:b + 12, :],
                                 x[b * P:(b + 12) * P, :].rearrange("(b p) d -> p b d", p=P)).then_inc(s_x, 16)
                sp.dma_start(x_all[0:LAST_ROWS, BLOCKS - 1, :], x[(BLOCKS - 1) * P:NODES, :]).then_inc(s_x, 16)
                sp.dma_start(wgnn_sb[:], w_gnn.rearrange("(k p) d -> p k d", p=P)).then_inc(s_w, 16)
                sp.dma_start(wqkv_sb[:], w_qkv.rearrange("(k p) d -> p k d", p=P)).then_inc(s_w, 16)
                sp.dma_start(wout_sb[:], w_out).then_inc(s_w, 16)
                sp.dma_start(wgate_sb[:], w_gate.rearrange("(k p) d -> p k d", p=P)).then_inc(s_w, 16)
                sp.dma_start(b1_rows, b1.rearrange("e (f n) -> (e f) n", n=P)).then_inc(s_w, 16)
                sp.dma_start(b2_sb[:], b2).then_inc(s_w, 16)
                at = 0
                for row in (b_gnn, prelu_a, b_out, b_gate, gate_bias):
                    n = row.shape[0]
                    sp.dma_start(rows[0:1, at:at + n], row.rearrange("(a n) -> a n", a=1)).then_inc(s_w, 16)
                    at += n
                sp.wait_ge(s_w, 11 * 16)

            @block.gpsimd
            def _(pool):
                last = (CHUNKS - 1) * P
                pool.memset(raw_i[:, last:COLS], 0).then_inc(s_pad, 1)
                pool.memset(raw_i[:, COLS + last:2 * COLS], -1).then_inc(s_pad, 1)
                pool.memset(x_all[:, BLOCKS - 1, :], 0.0).then_inc(s_pad, 1)
                pool.memset(eps_sb[:], EPS).then_inc(s_pad, 1)
                pool.memset(ident[:], 0.0).then_inc(s_idc, 1)
                pool.memset(ones[:], 1.0).then_inc(s_const, 1)
                pool.wait_ge(s_idc, 1)
                pool.affine_select(out=ident[:], in_=ident[:], compare_op=ALU.not_equal, fill=1.0, base=0,
                                   pattern=[[-1, P]], channel_multiplier=1).then_inc(s_const, 1)
                pool.memset(check[:, COLS:COLS + 16], 0.0).then_inc(s_const, 1)
                pool.iota(check[:, COLS + 16:COLS + 16 + TILES], [[P, BLOCKS], [0, STEP_TILES]], base=0,
                          channel_multiplier=0, allow_small_or_imprecise_dtypes=True).then_inc(s_const, 1)
                pool.iota(iota_b[:], [[1, P]], base=0, channel_multiplier=0,
                          allow_small_or_imprecise_dtypes=True).then_inc(s_const, 1)
                pool.iota(iota_n[:], [[1, P]], base=0, channel_multiplier=0,
                          allow_small_or_imprecise_dtypes=True).then_inc(s_const, 1)
                pool.iota(iota_w[:], [[1, WINDOW]], base=0, channel_multiplier=0,
                          allow_small_or_imprecise_dtypes=True).then_inc(s_const, 1)
                pool.iota(iota_e[:], [[1, EXPERTS]], base=0, channel_multiplier=0,
                          allow_small_or_imprecise_dtypes=True).then_inc(s_const, 1)

            @block.tensor
            def _(pe):
                pe.wait_ge(s_const, 8)
                for n in range(2):
                    pe.wait_ge(s_rawf, n + 1)
                    for c in range(CHUNKS):
                        last = pe.transpose(psum[4 * n + c // 4][:, c % 4 * P:(c % 4 + 1) * P],
                                            raw_f[:, n * COLS + c * P:n * COLS + (c + 1) * P], ident[:])
                    last.then_inc(s_turned, 1)
                pe.wait_ge(s_dv, 2)
                pe.matmul(psum[0][:, 0:COLS // GROUP], ones[0:1, :],
                          dst_t[0:1, :].rearrange("p (g t) -> p g t", t=GROUP)[:, :, 0],
                          start=True, stop=True).then_inc(s_basebc, 1)
                pe.wait_ge(s_bad, 1)
                pe.matmul(psum[1][:, 0:1], ones[:], flag[:, 0:1], start=True, stop=True).then_inc(s_badsum, 1)

            @block.scalar
            def _(act):
                act.wait_ge(s_pad, 4)
                act.wait_ge(s_var, 1)
                act.activation(ln[:, 4, :], ln[:, 3, :], ACT.Sqrt, bias=eps_sb[:, 0:1]).then_inc(s_std, 1)

            @block.vector
            def _(dve):
                chain = [0]

                def link(ins):
                    chain[0] += 1
                    ins.then_inc(s_bn, 1)
                    dve.wait_ge(s_bn, chain[0])

                dve.wait_ge(s_edges, 6 * 16)
                for n in range(2):
                    dve.tensor_copy(raw_f[:, n * COLS:(n + 1) * COLS],
                                    raw_i[:, n * COLS:(n + 1) * COLS]).then_inc(s_rawf, 1)
                for n, to in ((0, src_t), (1, dst_t)):
                    dve.wait_ge(s_turned, n + 1)
                    for b in range(4):
                        m = min(512, COLS - 512 * b)
                        last = dve.tensor_copy(to[:, 512 * b:512 * b + m], psum[4 * n + b][:, 0:m])
                    last.then_inc(s_dv, 1)
                dve.wait_ge(s_dv, 2)
                link(dve.tensor_copy(dst_i, dst_t[:]))
                dve.tensor_copy(base[:], dst_i[0:1, :].rearrange("p (g t) -> p g t", t=GROUP)[:, :, 0])
                spare_i = check[:, 0:COLS].bitcast(I32)
                link(dve.tensor_scalar(spare_i, dst_i, 7, None, ALU.arith_shift_right))
                link(dve.tensor_copy(digit_a, spare_i))
                link(dve.tensor_scalar(spare_i, dst_i, P - 1, None, ALU.bitwise_and))
                link(dve.tensor_copy(digit_b, spare_i))
                dve.wait_ge(s_basebc, 1)
                groups = "p (g t) -> p g t"
                link(dve.tensor_tensor(rel[:].rearrange(groups, t=GROUP), dst_t[:].rearrange(groups, t=GROUP),
                                       psum[0][:, 0:COLS // GROUP].unsqueeze(2).to_broadcast(
                                           [P, COLS // GROUP, GROUP]), ALU.subtract))
                slack = check[:, 0:FULL_TILES + 1]
                bound = check[:, COLS:COLS + FULL_TILES + 1]
                other = check[:, 2 * COLS:2 * COLS + FULL_TILES + 1]
                real = slice(0, FULL_TILES + 1)
                link(dve.tensor_scalar(slack, rel[:, real], -1.0, float(WINDOW - 1), ALU.mult, ALU.add))
                link(dve.tensor_tensor(slack, slack, rel[:, real], ALU.min))
                dve.wait_ge(s_const, 8)
                link(dve.tensor_tensor(other, dst_t[:, real], bound, ALU.subtract))
                link(dve.tensor_tensor(slack, slack, other, ALU.min))
                link(dve.tensor_scalar(slack, slack, 0.0, None, ALU.is_lt))
                link(dve.memset(check[LAST_EDGES:P, FULL_TILES:FULL_TILES + 1], 0.0))
                dve.tensor_reduce(flag[:, 0:1], slack, AX_X, ALU.add).then_inc(s_bad, 1)
                dve.wait_ge(s_badsum, 1)
                link(dve.tensor_scalar(flag[:, 1:2], psum[1][:, 0:1], 1.0, None, ALU.min))
                link(dve.tensor_copy(flag_i[:], flag[0:1, 1:2]))
                link(dve.tensor_scalar(flag[:, 2:3], flag[:, 1:2], OFF_GRID, None, ALU.mult))
                link(dve.tensor_scalar(rel[:], rel[:], flag[:, 2:3], None, ALU.subtract))

                dve.wait_ge(s_x, 5 * 16)
                with dve.Fori(0, BLOCKS) as b:
                    dve.bn_stats(stat6[:, bass.ds(b, 1), :].rearrange("p a s -> p (a s)"),
                                 x_all[:, bass.ds(b, 1), :].rearrange("p a d -> p (a d)")).then_inc(s_bn, 1)
                chain[0] += BLOCKS
                dve.wait_ge(s_bn, chain[0])
                st = lambda n: stat6[:, :, n]
                link(dve.tensor_tensor(ln[:, 0, :], st(1), st(4), ALU.add))
                link(dve.tensor_scalar(ln[:, 0, :], ln[:, 0, :], 0.5, None, ALU.mult))
                link(dve.tensor_tensor(ln[:, 1, :], st(1), st(4), ALU.subtract))
                link(dve.tensor_scalar(ln[:, 1, :], ln[:, 1, :], 0.5, None, ALU.mult))
                link(dve.tensor_tensor(ln[:, 1, :], ln[:, 1, :], ln[:, 1, :], ALU.mult))
                link(dve.tensor_tensor(ln[:, 2, :], st(2), st(5), ALU.add))
                link(dve.scalar_tensor_tensor(out=ln[:, 3, :], in0=ln[:, 2, :], scalar=1.0 / D,
                                              in1=ln[:, 1, :], op0=ALU.mult, op1=ALU.add))
                dve.sem_inc(s_var, 1)
                dve.wait_ge(s_std, 1)
                link(dve.reciprocal(ln[:, 5, :], ln[:, 4, :]))
                link(dve.scalar_tensor_tensor(out=ln[:, 6, :], in0=ln[:, 0, :], scalar=-1.0, in1=ln[:, 5, :],
                                              op0=ALU.mult, op1=ALU.mult))

        s_xn = sem("s_xn")
        s_tr = sem("s_tr")
        s_xt = sem("s_xt")
        s_hv = sem("s_hv")
        s_kept = sem("s_kept")
        s_spill = [sem(f"s_spill{r}") for r in range(2)]
        s_hot_b = sem("s_hot_b")
        s_hot_a = sem("s_hot_a")
        s_hist = sem("s_hist")
        hist = psum[0]
        ps_tr = [psum[1], psum[2]]
        ps_hv = [psum[3], psum[4]]

        def over_blocks(eng, body):
            body(0, 0)
            body(1, 1)
            with eng.Fori(0, PAIRS) as pair:
                for parity in range(2):
                    body(pair * 2 + (2 + parity), parity)
            body(BLOCKS - 1, 0)

        with nc.Block() as block:
            @block.scalar
            def _(act):
                def normalise(b, r):
                    wait(act, s_tr, b - 1)
                    passed(act, "act")
                    act.activation(xn_buf[:, r, :], x_all[:, bass.ds(b, 1), :].rearrange("p a d -> p (a d)"),
                                   ACT.Identity, scale=ln[:, 5, bass.ds(b, 1)],
                                   bias=ln[:, 6, bass.ds(b, 1)]).then_inc(s_xn, 1)

                def body(b, r):
                    act.wait_ge(s_tr, b + 1)
                    wait(act, s_hv, b - 1)
                    if not (isinstance(b, int) and b < 2):
                        act.wait_ge(s_spill[r], (b - r) * 8)
                    act.copy(xt_buf[:, r, :, :].rearrange("p k n -> p (k n)"), ps_tr[r][:, 0:D]).then_inc(s_xt, 1)
                    if not (isinstance(b, int) and b == BLOCKS - 1):
                        normalise(b + 1, 1 - r)
                    act.wait_ge(s_hv, b + 1)
                    passed(act, "act")
                    act.copy(x_all[:, bass.ds(b, 1), :].rearrange("p a d -> p (a d)"), ps_hv[r][:, 0:D])
                    act.copy(v_all[:, bass.ds(b, 1), :].rearrange("p a d -> p (a d)"), ps_hv[r][:, D:D + P])
                    act.copy(k_t[:, bass.ds(b * P, P)], ps_hv[r][:, D + P:D + 2 * P]).then_inc(s_kept, 1)

                normalise(0, 0)
                over_blocks(act, body)

            @block.vector
            def _(dve):
                def body(b, r):
                    for q in range(GROUPS):
                        wait(dve, s_hist, b * GROUPS + q - 1)
                        for t in range(GROUP):
                            last = dve.tensor_scalar(hot_b[:, q % 2, t, :], iota_b[:],
                                                     digit_b[:, bass.ds((b * GROUPS + q) * GROUP + t, 1)],
                                                     None, ALU.is_equal)
                        last.then_inc(s_hot_b, 1)
                        tiles = digit_a[:, bass.ds((b * GROUPS + q) * GROUP, GROUP)]
                        dve.tensor_tensor(hot_a[:, q % 2, :, :],
                                          iota_n[:, 0:BLOCKS].unsqueeze(1).to_broadcast([P, GROUP, BLOCKS]),
                                          tiles.unsqueeze(2).to_broadcast([P, GROUP, BLOCKS]),
                                          ALU.is_equal).then_inc(s_hot_a, 1)

                over_blocks(dve, body)

            @block.tensor
            def _(pe):
                def count(b, q):
                    pe.wait_ge(s_hot_b, b * GROUPS + q + 1)
                    pe.wait_ge(s_hot_a, b * GROUPS + q + 1)
                    for t in range(GROUP):
                        first = isinstance(b, int) and b == 0 and q == 0 and t == 0
                        final = isinstance(b, int) and b == BLOCKS - 1 and q == GROUPS - 1 and t == GROUP - 1
                        last = pe.matmul(hist[:, 0:BLOCKS], hot_b[:, q % 2, t, :], hot_a[:, q % 2, t, :],
                                         start=first, stop=final, skip_group_check=True)
                    last.then_inc(s_hist, 1)

                def body(b, r):
                    pe.wait_ge(s_xn, b + 1)
                    wait(pe, s_xt, b - 1)
                    for k in range(KC):
                        last = pe.transpose(ps_tr[r][:, k * P:(k + 1) * P], xn_buf[:, r, k * P:(k + 1) * P],
                                            ident[:])
                    last.then_inc(s_tr, 1)
                    count(b, 0)
                    count(b, 1)
                    pe.wait_ge(s_xt, b + 1)
                    wait(pe, s_kept, b - 1)
                    for k in range(KC):
                        pe.matmul(ps_hv[r][:, 0:D], xt_buf[:, r, k, :], wgnn_sb[:, k, :],
                                  start=(k == 0), stop=(k == KC - 1))
                    for k in range(KC):
                        pe.matmul(ps_hv[r][:, D:D + P], xt_buf[:, r, k, :], wqkv_sb[:, k, 2 * HID:3 * HID],
                                  start=(k == 0), stop=(k == KC - 1))
                    for k in range(KC):
                        last = pe.matmul(ps_hv[r][:, D + P:D + 2 * P], wqkv_sb[:, k, HID:2 * HID],
                                         xt_buf[:, r, k, :], start=(k == 0), stop=(k == KC - 1))
                    last.then_inc(s_hv, 1)
                    count(b, 2)
                    count(b, 3)

                over_blocks(pe, body)

            @block.sync
            def _(sp):
                def body(b, r):
                    sp.wait_ge(s_xt, b + 1)
                    sp.dma_start(xnt[bass.ds(b, 1), :, :].rearrange("a p n -> (a p) n"),
                                 xt_buf[:, r, :, :].rearrange("p k n -> p (k n)")).then_inc(s_spill[r], 16)

                over_blocks(sp, body)
                sp.wait_ge(s_spill[0], 16 * (BLOCKS // 2 + 1))
                sp.wait_ge(s_spill[1], 16 * (BLOCKS // 2))

        s_deg = sem("s_deg")
        s_root = sem("s_root")
        s_dinv = sem("s_dinv")
        s_scaled = sem("s_scaled")
        s_scaled_p = sem("s_scaled_p")
        s_table = sem("s_table")
        s_tchain = sem("s_tchain")
        s_kmax = sem("s_kmax")
        s_exp = sem("s_exp")
        s_exp_tr = sem("s_exp_tr")
        s_exp_n = sem("s_exp_n")
        s_ctx = sem("s_ctx")
        s_cm = sem("s_cm")
        s_cmt = sem("s_cmt")
        s_c = sem("s_c")
        s_cev = sem("s_cev")
        s_bc = sem("s_bc")
        SEVENTH = BLOCKS // 7
        QUAD = 4 * P
        QUADS = (BLOCKS - 1) // 4

        with nc.Block() as block:
            @block.vector
            def _(dve):
                chain = [0]

                def link(ins):
                    chain[0] += 1
                    ins.then_inc(s_tchain, 1)
                    dve.wait_ge(s_tchain, chain[0])

                dve.tensor_scalar(dinv[:], hist[:, 0:BLOCKS], 1.0, None, ALU.add).then_inc(s_deg, 1)
                dve.tensor_reduce(kmax, k_t[:, 0:NODES], AX_X, ALU.max, negate=True).then_inc(s_kmax, 1)
                dve.wait_ge(s_root, 1)
                dve.reciprocal(dinv[:], dinv[:]).then_inc(s_dinv, 1)
                dve.wait_ge(s_dinv, 1)
                for n in range(5):
                    h = x_all[:, n * SEVENTH:(n + 1) * SEVENTH, :]
                    dve.tensor_tensor(h, h, dinv[:, n * SEVENTH:(n + 1) * SEVENTH].unsqueeze(2).to_broadcast(
                        [P, SEVENTH, D]), ALU.mult).then_inc(s_scaled, 1)
                with dve.Fori(0, QUADS) as n:
                    dve.wait_ge(s_exp_tr, n + 1)
                    dve.tensor_copy(exp_n, psum[1][:, 0:QUAD]).then_inc(s_exp_n, 1)
                dve.wait_ge(s_exp_tr, QUADS + 1)
                dve.tensor_copy(exp_n[0:LAST_ROWS, 0:P], psum[1][0:LAST_ROWS, 0:P]).then_inc(s_exp_n, 1)

                link(dve.memset(ctx_m, 0.0))
                dve.wait_ge(s_ctx, 1)
                link(dve.reciprocal(flag[:, 3:4], psum[3][:, 0:1]))
                for h in range(HEADS):
                    at = slice(h * HEAD, (h + 1) * HEAD)
                    last = dve.tensor_scalar(ctx_m[at, at], psum[2][at, at], flag[at, 3:4], HEAD ** -0.5,
                                             ALU.mult, ALU.mult)
                last.then_inc(s_cm, 1)
                dve.wait_ge(s_c, 1)
                dve.tensor_copy(ctx_mt, psum[4][:, 0:P]).then_inc(s_cev, 1)
                dve.wait_ge(s_c, 2)
                dve.tensor_copy(wq_t.rearrange("p k n -> p (k n)"), psum[5][:, 0:D]).then_inc(s_cev, 1)
                dve.wait_ge(s_c, 3)
                dve.tensor_copy(ctx_w, psum[4][:, P:P + D]).then_inc(s_cev, 1)
                dve.wait_ge(s_c, 4)
                dve.tensor_copy(mix_w[:].rearrange("p k n -> p (k n)"), psum[6][:, :])

            @block.gpsimd
            def _(pool):
                pool.wait_ge(s_dinv, 1)
                for n in range(5, 7):
                    h = x_all[:, n * SEVENTH:(n + 1) * SEVENTH, :]
                    pool.tensor_tensor(h, h, dinv[:, n * SEVENTH:(n + 1) * SEVENTH].unsqueeze(2).to_broadcast(
                        [P, SEVENTH, D]), ALU.mult).then_inc(s_scaled_p, 1)

            @block.sync
            def _(sp):
                def store(n):
                    sp.dma_start(table[n * SEVENTH * P:(n + 1) * SEVENTH * P, :].rearrange(
                        "(b p) d -> p b d", p=P), x_all[:, n * SEVENTH:(n + 1) * SEVENTH, :]).then_inc(s_table, 16)

                for n in range(3):
                    sp.wait_ge(s_scaled, n + 1)
                    store(n)
                sp.wait_ge(s_scaled_p, 1)
                store(5)
                for n in range(3, 5):
                    sp.wait_ge(s_scaled, n + 1)
                    store(n)
                sp.wait_ge(s_scaled_p, 2)
                store(6)
                sp.wait_ge(s_table, 7 * 16)

            @block.scalar
            def _(act):
                act.wait_ge(s_deg, 1)
                act.activation(dinv[:], dinv[:], ACT.Sqrt).then_inc(s_root, 1)
                act.wait_ge(s_kmax, 1)
                act.activation(exp_t, k_t[:, 0:QUAD], ACT.Exp, bias=kmax).then_inc(s_exp, 1)
                with act.Fori(1, QUADS) as n:
                    act.wait_ge(s_exp_n, n)
                    passed(act, "act")
                    act.activation(exp_t, k_t[:, bass.ds(n * QUAD, QUAD)], ACT.Exp, bias=kmax).then_inc(s_exp, 1)
                act.wait_ge(s_exp_n, QUADS)
                act.activation(exp_t[:, 0:LAST_ROWS], k_t[:, QUADS * QUAD:NODES], ACT.Exp,
                               bias=kmax).then_inc(s_exp, 1)
                act.wait_ge(s_bc, 1)
                act.copy(bgnn_bc[:], psum[4][:, 0:D])
                act.copy(prelu_bc[:], psum[4][:, D:2 * D])
                act.copy(bout_bc[:], psum[5][:, 0:D])
                act.copy(b1_t[:], psum[5][:, D:D + EXPERTS * FC])
                act.copy(gate_bc[:], psum[5][:, 3 * P:3 * P + EXPERTS]).then_inc(s_bc, 1)

            @block.tensor
            def _(pe):
                def sums(n, rows_of):
                    for j, m in enumerate(rows_of):
                        first = isinstance(n, int) and n == 0 and j == 0
                        final = m < P
                        e = exp_n[0:m, j * P:(j + 1) * P]
                        pe.matmul(psum[2][:, 0:P], e, v_all[0:m, bass.ds(n * 4 + j, 1), :].rearrange(
                            "p a e -> p (a e)"), start=first, stop=final, skip_group_check=True)
                        last = pe.matmul(psum[3][:, 0:1], e, ones[0:m, 0:1], start=first, stop=final,
                                         skip_group_check=True)
                    return last

                def turn(n):
                    pe.wait_ge(s_exp, n + 1)
                    for j in range(4):
                        last = pe.transpose(psum[1][:, j * P:(j + 1) * P], exp_t[:, j * P:(j + 1) * P], ident[:])
                    last.then_inc(s_exp_tr, 1)
                    pe.wait_ge(s_exp_n, n + 1)

                pe.matmul(psum[4][:, 0:2 * D], ones[0:1, :], rows[0:1, 0:2 * D], start=True, stop=True)
                pe.matmul(psum[5][:, 0:D], ones[0:1, :], rows[0:1, 2 * D:3 * D], start=True, stop=True)
                pe.transpose(psum[5][:, D:D + EXPERTS * FC], b1_rows, ident[0:EXPERTS * FC, 0:EXPERTS * FC])
                for n in range(2):
                    last = pe.matmul(psum[5][:, 3 * P:3 * P + EXPERTS], ones[0:1, :],
                                     rows[0:1, 3 * D + n * EXPERTS:3 * D + (n + 1) * EXPERTS],
                                     start=(n == 0), stop=(n == 1))
                last.then_inc(s_bc, 1)
                turn(0)
                sums(0, [P] * 4)
                with pe.Fori(1, QUADS) as n:
                    turn(n)
                    sums(n, [P] * 4)
                pe.wait_ge(s_exp, QUADS + 1)
                pe.transpose(psum[1][0:LAST_ROWS, 0:P], exp_t[:, 0:LAST_ROWS], ident[:]).then_inc(s_exp_tr, 1)
                pe.wait_ge(s_exp_n, QUADS + 1)
                sums(QUADS, [LAST_ROWS]).then_inc(s_ctx, 1)

                pe.wait_ge(s_bc, 2)
                pe.wait_ge(s_cm, 1)
                pe.transpose(psum[4][:, 0:P], ctx_m, ident[:]).then_inc(s_c, 1)
                for k in range(KC):
                    last = pe.transpose(psum[5][:, k * P:(k + 1) * P], wqkv_sb[:, k, 0:HID], ident[:])
                last.then_inc(s_c, 1)
                pe.wait_ge(s_cev, 1)
                pe.matmul(psum[4][:, P:P + D], ctx_mt, wout_sb[:], start=True, stop=True).then_inc(s_c, 1)
                pe.wait_ge(s_cev, 3)
                for k in range(KC):
                    last = pe.matmul(psum[6][:, k * D:(k + 1) * D], wq_t[:, k, :], ctx_w, start=True, stop=True)
                last.then_inc(s_c, 1)

        s_zero = sem("s_zero")
        g_idx = sem("g_idx")
        g_in = sem("g_in")
        g_shift = sem("g_shift")
        g_hot = sem("g_hot")
        g_mm = sem("g_mm")
        g_add = sem("g_add")
        hot_g = g_region[:, GROUP * D:GROUP * (D + P)].rearrange("p (t n) -> p t n", n=P)
        ps_gen = psum[0][:, 0:KC * P].rearrange("p (c n) -> p c n", c=KC)
        ALL_GROUPS = TILES // GROUP

        with nc.Block() as block:
            @block.vector
            def _(dve):
                dve.memset(acc_region[:], 0.0).then_inc(s_zero, 1)
                dve.wait_ge(s_zero, 1)
                with dve.If(dve.value_load(flag_i[0:1, 0:1], min_val=0, max_val=1) > 0):
                    with dve.Fori(0, ALL_GROUPS) as g:
                        dve.tensor_copy(index[:, 0:GROUP], src_t[:, bass.ds(g * GROUP, GROUP)]).then_inc(g_idx, 1)
                        dve.tensor_copy(shifted, dst_t[:, bass.ds(g * GROUP, GROUP)]).then_inc(g_shift, 1)
                        with dve.Fori(0, BLOCKS) as b:
                            dve.wait_ge(g_shift, g * (BLOCKS + 1) + b + 1)
                            dve.tensor_tensor(hot_g, iota_n[:].unsqueeze(1).to_broadcast([P, GROUP, P]),
                                              shifted.unsqueeze(2).to_broadcast([P, GROUP, P]),
                                              ALU.is_equal).then_inc(g_hot, 1)
                            dve.wait_ge(g_hot, g * BLOCKS + b + 1)
                            dve.tensor_scalar(shifted, shifted, float(P), None, ALU.subtract).then_inc(g_shift, 1)
                            dve.wait_ge(g_mm, g * BLOCKS + b + 1)
                            dve.tensor_tensor(acc_t[:, :, bass.ds(b * P, P)], acc_t[:, :, bass.ds(b * P, P)],
                                              ps_gen, ALU.add).then_inc(g_add, 1)
                            dve.wait_ge(g_add, g * BLOCKS + b + 1)

            @block.gpsimd
            def _(pool):
                with pool.If(pool.value_load(flag_i[0:1, 0:1], min_val=0, max_val=1) > 0):
                    with pool.Fori(0, ALL_GROUPS) as g:
                        pool.wait_ge(g_idx, g + 1)
                        passed(pool, "pool")
                        for t in range(GROUP):
                            pool.indirect_dma_start(
                                out=gathered[:, t, :], out_offset=None, in_=table[:, :],
                                in_offset=bass.IndirectOffsetOnAxis(ap=index[:, t:t + 1], axis=0)
                            ).then_inc(g_in, 16)

            @block.tensor
            def _(pe):
                with pe.If(pe.value_load(flag_i[0:1, 0:1], min_val=0, max_val=1) > 0):
                    with pe.Fori(0, ALL_GROUPS) as g:
                        pe.wait_ge(g_in, (g + 1) * (16 * GROUP))
                        passed(pe, "pe")
                        with pe.Fori(0, BLOCKS) as b:
                            pe.wait_ge(g_hot, g * BLOCKS + b + 1)
                            for c in range(KC):
                                for t in range(GROUP):
                                    last = pe.matmul(ps_gen[:, c, :], gathered[:, t, c * P:(c + 1) * P],
                                                     hot_g[:, t, :], start=(t == 0), stop=(t == GROUP - 1))
                            last.then_inc(g_mm, 1)

        s_w1 = sem("s_w1")
        s_w2 = sem("s_w2")
        s_idx = sem("s_idx")
        s_gath = [sem(f"s_gath{q}") for q in range(GROUPS)]
        s_hot = sem("s_hot")
        s_agg = sem("s_agg")
        s_add = sem("s_add")
        s_ld = [sem(f"s_ld{r}") for r in range(2)]
        s_store = [sem(f"s_store{r}") for r in range(2)]
        s_aggt = sem("s_aggt")
        s_a2 = sem("s_a2")
        s_res = sem("s_res")
        s_moment = sem("s_moment")
        s_root2 = sem("s_root2")
        s_rstd = sem("s_rstd")
        s_xn2 = sem("s_xn2")
        s_a4 = sem("s_a4")
        s_x2t = sem("s_x2t")
        s_a6 = sem("s_a6")
        s_lg = sem("s_lg")
        s_top = sem("s_top")
        s_diff = sem("s_diff")
        s_e2 = sem("s_e2")
        s_wts = sem("s_wts")
        s_comb = sem("s_comb")
        s_a8 = sem("s_a8")
        s_combt = sem("s_combt")
        s_a9 = sem("s_a9")
        s_b2 = sem("s_b2")
        s_h1 = sem("s_h1")
        s_relu = sem("s_relu")
        s_h2 = sem("s_h2")
        s_out = sem("s_out")
        ps_agg = [psum[0], psum[1]]
        ps_h = [psum[2], psum[3]]
        ps_y = [psum[4], psum[5]]
        ps_a = psum[6]
        ps_b = psum[7]
        RES_OPS = 7

        def over_steps(eng, body):
            body(0, 0, True, False, False)
            body(1, 1, True, False, True)
            body(2, 0, True, True, True)
            body(3, 1, True, True, True)
            with eng.Fori(0, PAIRS - 1) as pair:
                for parity in range(2):
                    body(pair * 2 + (4 + parity), parity, True, True, True)
            body(BLOCKS - 1, 0, True, True, True)
            body(BLOCKS, 1, False, True, True)
            body(BLOCKS + 1, 0, False, True, False)

        with nc.Block() as block:
            @block.sync
            def _(sp):
                for e in range(EXPERTS):
                    sp.dma_start(w1_sb[:, e, :, :], w1[e].rearrange("(k p) f -> p k f", p=P)).then_inc(s_w1, 16)
                    sp.dma_start(w2_sb[:, e, :, :], w2[e].rearrange("(f p) d -> p f d", p=P)).then_inc(s_w2, 16)

                def load(b, r, n):
                    wait(sp, s_res, (b - 1) * RES_OPS)
                    at = b * P
                    sp.dma_start(x_ld[0:n, r, :], x[bass.ds(at, n), :]).then_inc(s_ld[r], 16)
                    sp.dma_start(xt_ld[:, r, :, :].rearrange("p k n -> p (k n)"),
                                 xnt[bass.ds(b, 1), :, :].rearrange("a p n -> (a p) n")).then_inc(s_ld[r], 16)
                    sp.dma_start(h_ld[:, r, :], table[bass.ds(at, P), :]).then_inc(s_ld[r], 16)

                def store(b, r, n):
                    sp.wait_ge(s_out, EXPERTS * (b + 1))
                    sp.dma_start(out[bass.ds(b * P, n), :], acc[0:n, r, :]).then_inc(s_store[r], 16)

                def body(s, r, agg, experts, stage):
                    if agg:
                        load(s, r, LAST_ROWS if isinstance(s, int) and s == BLOCKS - 1 else P)
                    if experts:
                        last = isinstance(s, int) and s == BLOCKS + 1
                        store(s - 2, r, LAST_ROWS if last else P)

                over_steps(sp, body)
                sp.wait_ge(s_store[0], 16 * (BLOCKS // 2 + 1))
                sp.wait_ge(s_store[1], 16 * (BLOCKS // 2))

            @block.gpsimd
            def _(pool):
                with pool.Fori(0, BLOCKS) as s:
                    for q in range(GROUPS):
                        pool.wait_ge(s_idx, s * GROUPS + (q + 1))
                        passed(pool, "pool")
                        for t in range(q * GROUP, (q + 1) * GROUP):
                            pool.indirect_dma_start(
                                out=gathered[:, t, :], out_offset=None, in_=table[:, :],
                                in_offset=bass.IndirectOffsetOnAxis(ap=index[:, t:t + 1], axis=0)
                            ).then_inc(s_gath[q], 16)

            @block.scalar
            def _(act):
                def body(s, r, agg, experts, stage):
                    b, rb = s - 1, 1 - r

                    def relu(e):
                        if not experts:
                            return
                        at = (s - 2) * EXPERTS + e
                        act.wait_ge(s_h1, at + 1)
                        wait(act, s_h2, at - 1)
                        for f in range(FC):
                            last = act.activation(hid_t[:, e % 2, f, :], ps_h[e % 2][:, f * P:(f + 1) * P],
                                                  ACT.Relu, bias=b1_t[:, e * FC + f:e * FC + f + 1])
                        last.then_inc(s_relu, 1)

                    for e in range(4):
                        relu(e)
                    if stage:
                        act.wait_ge(s_add, s * GROUPS + 2 if agg else BLOCKS * GROUPS)
                        wait(act, s_a2, b)
                        passed(act, "act")
                        act.copy(agg_t[:], acc_t[:, :, bass.ds(b * P, P)]).then_inc(s_aggt, 1)
                    relu(4)
                    if stage:
                        act.wait_ge(s_moment, 2 * b + 2)
                        act.activation(mv[:, 2:3], mv[:, 1:2], ACT.Sqrt, bias=eps_sb[:, 0:1]).then_inc(s_root2, 1)
                    relu(5)
                    if stage:
                        act.wait_ge(s_a4, b + 1)
                        wait(act, s_h1, (b - 1) * EXPERTS)
                        act.copy(x2_t[:, rb, :, :].rearrange("p k n -> p (k n)"),
                                 ps_b[:, 0:D]).then_inc(s_x2t, 1)
                    relu(6)
                    if stage:
                        act.wait_ge(s_diff, b + 1)
                        act.activation(gate[:, 2, 1:2], gate[:, 2, 0:1], ACT.Exp).then_inc(s_e2, 1)
                    relu(7)

                over_steps(act, body)

            @block.vector
            def _(dve):
                def one_hot(s, q):
                    tiles = rel[:, bass.ds(s * STEP_TILES + q * GROUP, GROUP)]
                    dve.tensor_tensor(hot_w[:, q % 2, :, :],
                                      iota_w[:].unsqueeze(1).to_broadcast([P, GROUP, WINDOW]),
                                      tiles.unsqueeze(2).to_broadcast([P, GROUP, WINDOW]),
                                      ALU.is_equal).then_inc(s_hot, 1)

                def fetch(s, q):
                    dve.tensor_copy(index[:, q * GROUP:(q + 1) * GROUP],
                                    src_t[:, bass.ds(s * STEP_TILES + q * GROUP, GROUP)]).then_inc(s_idx, 1)

                def add(s, q):
                    g = s * GROUPS + q
                    at = dve.value_load(base[0:1, bass.ds(g, 1)], min_val=0, max_val=NODES - 1)
                    if q < GROUPS - 1:
                        one_hot(s, q + 1)
                    else:
                        one_hot(s + 1, 0)
                    window = acc_t[:, :, bass.ds(at, WINDOW)]
                    wait(dve, s_add, g)
                    dve.wait_ge(s_agg, g + 1)
                    dve.tensor_tensor(window, window, ps_agg[q % 2][:, 0:KC * WINDOW].rearrange(
                        "p (c n) -> p c n", c=KC), ALU.add).then_inc(s_add, 1)
                    fetch(s + 1, q)

                def body(s, r, agg, experts, stage):
                    b, rb = s - 1, 1 - r
                    x1 = acc[:, rb, :]
                    t0, t1 = tmp[:, 0, :], tmp[:, 1, :]

                    def combine(e):
                        if not experts:
                            return
                        at = (s - 2) * EXPERTS + e
                        dve.wait_ge(s_h2, at + 1)
                        wait(dve, s_out, at)
                        dve.scalar_tensor_tensor(out=acc[:, r, :], in0=ps_y[e % 2][:, 0:D],
                                                 scalar=comb[:, r, e:e + 1], in1=acc[:, r, :],
                                                 op0=ALU.mult, op1=ALU.add).then_inc(s_out, 1)

                    if agg:
                        add(s, 0)
                    combine(0)
                    combine(1)
                    if agg:
                        add(s, 1)
                    combine(2)
                    if stage:
                        n = b * RES_OPS
                        if not (isinstance(b, int) and b < 2):
                            dve.wait_ge(s_store[rb], (b - rb) * 8)
                        dve.wait_ge(s_ld[rb], (b - rb) * 24 + 48)
                        dve.tensor_tensor(x1, x_ld[:, rb, :], bout_bc[:], ALU.add).then_inc(s_res, 1)
                        dve.wait_ge(s_a2, b + 1)
                        dve.tensor_tensor(t0, h_ld[:, rb, :], ps_a[:, 0:D], ALU.add).then_inc(s_res, 1)
                        dve.wait_ge(s_res, n + 2)
                        dve.tensor_tensor(x1, x1, ps_a[:, D:2 * D], ALU.add).then_inc(s_res, 1)
                        dve.scalar_tensor_tensor(out=t1, in0=t0, scalar=dinv[:, bass.ds(b, 1)], in1=bgnn_bc[:],
                                                 op0=ALU.mult, op1=ALU.add).then_inc(s_res, 1)
                        dve.wait_ge(s_res, n + 4)
                        dve.scalar_tensor_tensor(out=t0, in0=t1, scalar=0.0, in1=prelu_bc[:],
                                                 op0=ALU.min, op1=ALU.mult).then_inc(s_res, 1)
                        dve.wait_ge(s_res, n + 5)
                        dve.scalar_tensor_tensor(out=t1, in0=t1, scalar=0.0, in1=t0,
                                                 op0=ALU.max, op1=ALU.add).then_inc(s_res, 1)
                        dve.wait_ge(s_res, n + 6)
                        dve.tensor_tensor(x1, x1, t1, ALU.add).then_inc(s_res, 1)
                        dve.wait_ge(s_res, n + 7)
                        dve.bn_stats(stats[:], x1).then_inc(s_moment, 1)
                        dve.wait_ge(s_moment, 2 * b + 1)
                        passed(dve, "dve")
                        dve.bn_aggr(mv[:, 0:2], stats[:]).then_inc(s_moment, 1)
                    combine(3)
                    if agg:
                        add(s, 2)
                    if stage:
                        dve.wait_ge(s_root2, b + 1)
                        dve.reciprocal(mv[:, 3:4], mv[:, 2:3]).then_inc(s_rstd, 1)
                        dve.wait_ge(s_rstd, b + 1)
                        dve.tensor_scalar(xn2[:], x1, mv[:, 0:1], mv[:, 3:4], ALU.subtract,
                                          ALU.mult).then_inc(s_xn2, 1)
                    combine(4)
                    combine(5)
                    if agg:
                        add(s, 3)
                    if stage:
                        logits, top, small, hot1, hot2 = (gate[:, n, :] for n in (0, 1, 2, 3, 4))
                        dve.wait_ge(s_a6, b + 1)
                        dve.tensor_tensor(logits, ps_b[:, D:D + EXPERTS], gate_bc[:], ALU.add).then_inc(s_lg, 1)
                        dve.wait_ge(s_lg, b + 1)
                        passed(dve, "dve")
                        dve.max(top, logits).then_inc(s_top, 1)
                        dve.wait_ge(s_top, 3 * b + 1)
                        passed(dve, "dve")
                        dve.max_index(gate_i[:], top, logits).then_inc(s_top, 1)
                        dve.tensor_tensor(small[:, 0:1], top[:, 1:2], top[:, 0:1], ALU.subtract).then_inc(s_diff, 1)
                        dve.wait_ge(s_top, 3 * b + 2)
                        dve.tensor_copy(gate[:, 5, 0:2], gate_i[:, 0:2]).then_inc(s_top, 1)
                        dve.wait_ge(s_e2, b + 1)
                        dve.tensor_scalar(small[:, 2:3], small[:, 1:2], 1.0, None, ALU.add).then_inc(s_wts, 1)
                        dve.wait_ge(s_wts, 3 * b + 1)
                        dve.reciprocal(small[:, 3:4], small[:, 2:3]).then_inc(s_wts, 1)
                        dve.wait_ge(s_wts, 3 * b + 2)
                        dve.tensor_tensor(small[:, 4:5], small[:, 1:2], small[:, 3:4], ALU.mult).then_inc(s_wts, 1)
                        dve.wait_ge(s_wts, 3 * b + 3)
                        dve.wait_ge(s_top, 3 * b + 3)
                        dve.tensor_scalar(hot1, iota_e[:], gate[:, 5, 0:1], small[:, 3:4], ALU.is_equal,
                                          ALU.mult).then_inc(s_comb, 1)
                        dve.tensor_scalar(hot2, iota_e[:], gate[:, 5, 1:2], small[:, 4:5], ALU.is_equal,
                                          ALU.mult).then_inc(s_comb, 1)
                        dve.wait_ge(s_comb, 3 * b + 2)
                        dve.tensor_tensor(comb[:, rb, :], hot1, hot2, ALU.add).then_inc(s_comb, 1)
                    combine(6)
                    if stage:
                        dve.wait_ge(s_a8, b + 1)
                        dve.tensor_copy(comb_t[:], ps_b[0:EXPERTS, D + P:D + 2 * P]).then_inc(s_combt, 1)
                    combine(7)
                    if stage:
                        dve.wait_ge(s_a9, b + 1)
                        dve.tensor_tensor(x1, x1, ps_a[:, 0:D], ALU.add).then_inc(s_b2, 1)
                        dve.wait_ge(s_b2, b + 1)

                for q in range(GROUPS):
                    fetch(0, q)
                one_hot(0, 0)
                over_steps(dve, body)

            @block.tensor
            def _(pe):
                def body(s, r, agg, experts, stage):
                    b, rb = s - 1, 1 - r

                    def aggregate(q):
                        if not agg:
                            return
                        g = s * GROUPS + q
                        pe.wait_ge(s_hot, g + 1)
                        wait(pe, s_add, g - 1)
                        pe.wait_ge(s_gath[q], s * (16 * GROUP) + 16 * GROUP)
                        for c in range(KC):
                            for t in range(GROUP):
                                last = pe.matmul(ps_agg[q % 2][:, c * WINDOW:(c + 1) * WINDOW],
                                                 gathered[:, q * GROUP + t, c * P:(c + 1) * P],
                                                 hot_w[:, q % 2, t, :], start=(t == 0), stop=(t == GROUP - 1))
                        last.then_inc(s_agg, 1)

                    def up(e):
                        at = (s - 2) * EXPERTS + e
                        wait(pe, s_relu, at - 1)
                        if e == 0:
                            pe.wait_ge(s_w1, 16 * EXPERTS)
                        for f in range(FC):
                            for k in range(KC):
                                last = pe.matmul(ps_h[e % 2][:, f * P:(f + 1) * P],
                                                 w1_sb[:, e, k, f * P:(f + 1) * P], x2_t[:, r, k, :],
                                                 start=(k == 0), stop=(k == KC - 1))
                        last.then_inc(s_h1, 1)

                    def down(e):
                        at = (s - 2) * EXPERTS + e
                        pe.wait_ge(s_relu, at + 1)
                        wait(pe, s_out, at - 1)
                        if e == 0:
                            pe.wait_ge(s_w2, 16 * EXPERTS)
                        for f in range(FC):
                            last = pe.matmul(ps_y[e % 2][:, 0:D], hid_t[:, e % 2, f, :], w2_sb[:, e, f, :],
                                             start=(f == 0), stop=(f == FC - 1))
                        last.then_inc(s_h2, 1)

                    def sums_by_node():
                        pe.wait_ge(s_aggt, b + 1)
                        wait(pe, s_b2, b)
                        for k in range(KC):
                            pe.transpose(ps_a[:, k * P:(k + 1) * P], agg_t[:, k, :], ident[:])
                        pe.wait_ge(s_ld[rb], (b - rb) * 24 + 48)
                        for k in range(KC):
                            last = pe.matmul(ps_a[:, D:2 * D], xt_ld[:, rb, k, :], mix_w[:, k, :],
                                             start=(k == 0), stop=(k == KC - 1))
                        last.then_inc(s_a2, 1)

                    def turn_xn2():
                        pe.wait_ge(s_xn2, b + 1)
                        for k in range(KC):
                            last = pe.transpose(ps_b[:, k * P:(k + 1) * P], xn2[:, k * P:(k + 1) * P], ident[:])
                        last.then_inc(s_a4, 1)

                    def logits():
                        pe.wait_ge(s_x2t, b + 1)
                        for k in range(KC):
                            last = pe.matmul(ps_b[:, D:D + EXPERTS], x2_t[:, rb, k, :], wgate_sb[:, k, :],
                                             start=(k == 0), stop=(k == KC - 1))
                        last.then_inc(s_a6, 1)

                    def turn_weights():
                        pe.wait_ge(s_comb, 3 * b + 3)
                        pe.transpose(ps_b[0:EXPERTS, D + P:D + 2 * P], comb[:, rb, :], ident[:]).then_inc(s_a8, 1)

                    def bias2():
                        pe.wait_ge(s_combt, b + 1)
                        pe.matmul(ps_a[:, 0:D], comb_t[:], b2_sb[:], start=True, stop=True).then_inc(s_a9, 1)

                    after = {1: [lambda: aggregate(1)], 2: [sums_by_node], 3: [lambda: aggregate(2)],
                             4: [turn_xn2], 5: [lambda: aggregate(3), logits], 6: [turn_weights], 7: [bias2]}
                    work = {sums_by_node, turn_xn2, logits, turn_weights, bias2}
                    aggregate(0)
                    if experts:
                        up(0)
                    for e in range(EXPERTS):
                        if experts:
                            if e < EXPERTS - 1:
                                up(e + 1)
                            down(e)
                        for piece in after.get(e, ()):
                            if stage or piece not in work:
                                piece()

                over_steps(pe, body)


_INS = ['x', 'src', 'dst', 'L0_gnn_W', 'L0_gnn_b', 'L0_gnn_prelu_a', 'L0_mix_W_qkv', 'L0_mix_W_out',
        'L0_mix_b_out', 'L0_ffn_Wg', 'L0_ffn_bg', 'L0_ffn_bias', 'L0_ffn_W1', 'L0_ffn_b1', 'L0_ffn_W2',
        'L0_ffn_b2']


def kernel(**inputs):
    import numpy as _np
    import concourse.bacc as _bacc
    from concourse import mybir as _mybir
    from concourse.bass_utils import run_bass_kernel_spmd as _run

    nc = _bacc.Bacc("TRN2", target_bir_lowering=False, num_devices=1)
    arrays, args = {}, []
    for name in _INS:
        a = _np.ascontiguousarray(inputs[name])
        arrays[f"in_{name}"] = a
        args.append(nc.dram_tensor(f"in_{name}", a.shape, _mybir.dt.from_np(a.dtype), kind="ExternalInput").ap())
    f32 = _mybir.dt.float32
    args.append(nc.dram_tensor("out_0", (NODES, D), f32, kind="ExternalOutput").ap())
    args.append(nc.dram_tensor("table", (BLOCKS * P, D), f32, kind="Internal").ap())
    args.append(nc.dram_tensor("xnt", (BLOCKS, P, D), f32, kind="Internal").ap())
    gps_layer(nc, *args)
    r = _run(nc, [arrays], core_ids=[0])
    return r.results[0]["out_0"]
```

```python
from contextlib import ExitStack

import concourse.bass as bass
from concourse import mybir

F32 = mybir.dt.float32
BF16 = mybir.dt.bfloat16
I32 = mybir.dt.int32
U32 = mybir.dt.uint32
ALU = mybir.AluOpType
ACT = mybir.ActivationFunctionType
AX_X = mybir.AxisListType.X

P = 128
NODES, D = 6250, 256
EDGES = 200000
KC = D // P
HEADS, HEAD = 4, 32
HID = HEADS * HEAD
EXPERTS, EXPERT_DIM = 8, 512
FC = EXPERT_DIM // P
EPS = 1e-5

BLOCKS = -(-NODES // P)
LAST_ROWS = NODES - (BLOCKS - 1) * P
GROUP = 8
GROUPS = 4
STEP_TILES = GROUP * GROUPS
TILES = BLOCKS * STEP_TILES
FULL_TILES = EDGES // P
LAST_EDGES = EDGES - FULL_TILES * P
CHUNKS = -(-TILES // P)
COLS = CHUNKS * P
WINDOW = 64
ACC_COLS = BLOCKS * P + WINDOW
PARTS = 3
LO = 16
HI = 6
DEG_COLS = BLOCKS * P // LO
PER_GROUP = 2
ALL_GROUPS = TILES // GROUP
SLICE = 7
SEVENTH = BLOCKS // 7
PAIRS = (BLOCKS - 3) // 2
SPLIT = 14
QUAD = 4
QUADS = (BLOCKS - 1) // QUAD
OFF_GRID = 1.0e6


def gps_layer(nc, x, src, dst, w_gnn, b_gnn, prelu_a, w_qkv, w_out, b_out, w_gate, b_gate, gate_bias,
              w1, b1, w2, b2, out, table, xnt):
    assert EDGES <= TILES * P and GROUPS == 4 and BLOCKS % 2 == 1

    with ExitStack() as ctx:
        def sb(name, shape, dt=F32):
            return ctx.enter_context(nc.sbuf_tensor(name, shape, dt))

        def sem(name):
            return ctx.enter_context(nc.semaphore(name))

        def wait(eng, semaphore, value):
            if isinstance(value, int) and value <= 0:
                return
            eng.wait_ge(semaphore, value)

        s_passed = {name: sem(f"s_passed_{name}") for name in ("act", "dve", "pool", "pe")}

        def passed(eng, name):
            eng.sem_inc(s_passed[name], 1)

        psum = [ctx.enter_context(nc.psum_tensor(f"bank{n}", [P, 512], F32)) for n in range(8)]

        src_t = sb("src_t", [P, COLS], I32)
        rel = sb("rel", [P, COLS], BF16)
        base = sb("base", [1, COLS // GROUP], I32)
        ident = sb("ident", [P, P])
        ones = sb("ones", [P, P])
        iota_w = sb("iota_w", [P, WINDOW])
        iota_e = iota_w[:, 0:EXPERTS]
        dinv = sb("dinv", [P, BLOCKS])
        flag = sb("flag", [P, 4])
        flag_i = sb("flag_i", [1, 1], I32)
        wqkv_sb = sb("wqkv_sb", [P, KC, 3 * HID])
        wout_sb = sb("wout_sb", [P, D])
        mix_w = sb("mix_w", [P, KC, D])
        wgate_sb = sb("wgate_sb", [P, KC, EXPERTS])
        b1_t = sb("b1_t", [P, EXPERTS * FC])
        b2_sb = sb("b2_sb", [EXPERTS, D])
        bgnn_bc = sb("bgnn_bc", [P, D])
        prelu_bc = sb("prelu_bc", [P, D])
        bout_bc = sb("bout_bc", [P, D])
        gate_bc = sb("gate_bc", [P, EXPERTS])
        eps_sb = sb("eps_sb", [P, 1])
        kmax = sb("kmax", [P, 2])

        hot_w = sb("hot_w", [P, 2, GROUP, WINDOW], BF16)
        index = sb("index", [P, STEP_TILES], I32)
        x_ld = sb("x_ld", [P, 2, D])
        xt_ld = sb("xt_ld", [P, 2, KC, P])
        h_ld = sb("h_ld", [P, 2, PARTS, D], BF16)
        agg_t = sb("agg_t", [P, KC, P])
        tmp = sb("tmp", [P, D])
        acc = sb("acc", [P, 2, D])
        stats = sb("stats", [P, 6])
        mv = sb("mv", [P, 4])
        xn2 = sb("xn2", [P, D])
        x2_t = sb("x2_t", [P, 2, KC, P])
        gate = sb("gate", [P, 6, EXPERTS])
        gate_i = sb("gate_i", [P, EXPERTS], U32)
        comb = sb("comb", [P, 2, EXPERTS])
        comb_t = sb("comb_t", [EXPERTS, P])
        hid_t = sb("hid_t", [P, 2, FC, P])

        acc_region = sb("acc_region", [P, 2 * ACC_COLS])
        w_region = sb("w_region", [P, 2 * EXPERTS * FC * D])
        g_region = sb("g_region", [P, STEP_TILES * PARTS * D], BF16)

        hid_zero = hot_w[:, 0, :, :].rearrange("p t n -> p (t n)")
        acc_t = acc_region[:, :].rearrange("p (c n) -> p c n", c=KC)
        x_all = acc_region[:, 0:BLOCKS * D].rearrange("p (b d) -> p b d", d=D)
        w1_sb = w_region[:, 0:EXPERTS * FC * D].rearrange("p (e k f) -> p e k f", e=EXPERTS, k=KC)
        w2_sb = w_region[:, EXPERTS * FC * D:].rearrange("p (e f d) -> p e f d", e=EXPERTS, f=FC)
        kv_at = 2 * EXPERTS * FC * D - BLOCKS * 2 * P
        kv_all = w_region[:, kv_at:].rearrange("p (b r n) -> p b r n", r=2, n=P)
        xn_buf = w_region[:, 0:2 * D].rearrange("p (r d) -> p r d", r=2)
        rest_buf = w_region[:, 2 * D:4 * D].rearrange("p (r d) -> p r d", r=2)
        parts = w_region[:, 4 * D:4 * D + SEVENTH * PARTS * D // 2].bitcast(BF16).rearrange(
            "p (b r d) -> p b r d", b=SEVENTH, r=PARTS)
        assert 4 * D + SEVENTH * PARTS * D // 2 <= kv_at
        gathered = g_region[:, :].rearrange("p (t d) -> p t d", d=PARTS * D)

        def words(at, n, dt=F32):
            return g_region[:, 2 * at:2 * (at + n)].bitcast(dt)

        g_words = STEP_TILES * PARTS * D // 2
        raw_i, raw_f = words(0, 2 * COLS, I32), words(2 * COLS, 2 * COLS)
        digit_hi, whole_i, digit_i = words(0, COLS), words(COLS, COLS, I32), words(2 * COLS, COLS, I32)
        digit_lo = words(3 * COLS, COLS)
        small = words(4 * COLS, 512)
        slot = 4 * COLS + 512
        hot_lo = words(slot, SLICE * GROUP * LO).bitcast(BF16).rearrange(
            "p (r t n) -> p r t n", r=2, t=SLICE * GROUP)
        slot += SLICE * GROUP * LO
        hot_hi = words(slot, SLICE * GROUP * HI).bitcast(BF16).rearrange(
            "p (r t n) -> p r t n", r=2, t=SLICE * GROUP)
        slot += SLICE * GROUP * HI
        ramp = words(slot, COLS)
        assert slot + COLS <= g_words - COLS
        dst_t = words(g_words - COLS, COLS)
        select = words(0, P // LO * P)[0:LO, :].rearrange("p (h n) -> p h n", h=P // LO)
        deg_lo = words(2 * COLS, DEG_COLS)[0:LO, :]
        group_at = GROUP * PARTS * D // 2
        hot_g = words(group_at, 2 * GROUP * P // 2).bitcast(BF16).rearrange("p (r t n) -> p r t n", r=2, t=GROUP)
        iota_n = words(group_at + GROUP * P, P)
        shifted = words(group_at + GROUP * P + P, 4 * GROUP)

        xt_buf = x_ld[:, :, :].rearrange("p r (k n) -> p r k n", k=KC)
        wgnn_sb = x2_t[:, :, :, :].rearrange("p r k n -> p r (k n)")
        hid_flat = hid_t[:, :, :, :].rearrange("p r f n -> p (r f n)")
        stat6 = hid_flat[:, 0:6 * BLOCKS].rearrange("p (b s) -> p b s", s=6)
        ln = hid_flat[:, 6 * BLOCKS:14 * BLOCKS].rearrange("p (r b) -> p r b", r=8)
        b1_rows = agg_t[0:EXPERTS * FC, 0, :]
        rows = xt_ld[:, :, :, :].rearrange("p r k n -> p (r k n)")[0:1, :]
        rows2 = h_ld[:, :, :, :].rearrange("p r k n -> p (r k n)").bitcast(F32)[0:1, 0:D + 2 * EXPERTS]
        exp_t = acc[:, :, :].rearrange("p r d -> p (r d)")
        exp_n = x2_t[:, :, :, :].rearrange("p r k n -> p (r k n)")
        ctx_m, ctx_mt = tmp[:, 0:P], tmp[:, P:2 * P]
        ctx_w = xn2[:, :]
        wq_t = hid_t[:, 1, 0:KC, :]

        s_pad = sem("s_pad")
        s_edges = sem("s_edges")
        s_x = [sem(f"s_x{n}") for n in range(5)]
        s_w = sem("s_w")
        s_wb = sem("s_wb")
        s_ident = sem("s_ident")
        s_const = sem("s_const")
        s_rawf = sem("s_rawf")
        s_turned = sem("s_turned")
        s_dv = sem("s_dv")
        s_cast = sem("s_cast")
        s_base = sem("s_base")
        s_basebc = sem("s_basebc")
        s_var = sem("s_var")
        s_std = sem("s_std")
        s_ln = sem("s_ln")
        s_bn = sem("s_bn")
        s_bc = sem("s_bc")
        s_slice = sem("s_slice")
        s_counted = sem("s_counted")
        s_deg = sem("s_deg")
        s_zeros = sem("s_zeros")
        s_xn = sem("s_xn")
        s_tr = sem("s_tr")
        s_xt = sem("s_xt")
        s_hv = sem("s_hv")
        s_kept = sem("s_kept")
        s_spill = [sem(f"s_spill{r}") for r in range(2)]
        ps_tr = [psum[1], psum[2]]
        ps_hv = [psum[3], psum[4]]
        ps_count = psum[0]
        X_LOADS = [(0, 12), (12, 24), (24, 36), (36, 48), (48, 49)]

        def over_blocks(eng, body, lo, hi):
            if lo == 0:
                body(0, 0)
                body(1, 1)
                lo = 2
            with eng.Fori(0, (hi - lo) // 2) as pair:
                for parity in range(2):
                    body(pair * 2 + (lo + parity), parity)
            if (hi - lo) % 2:
                body(hi - 1, 0)

        def row(ap):
            return ap.rearrange("p a d -> p (a d)")

        def at_least(b, n):
            return not isinstance(b, int) or b >= n

        def project_act(act):
            def scale(b, r):
                wait(act, s_tr, b - 1)
                passed(act, "act")
                act.activation(xn_buf[:, r, :], row(x_all[:, bass.ds(b, 1), :]), ACT.Identity,
                               scale=ln[:, 5, bass.ds(b, 1)], bias=ln[:, 6, bass.ds(b, 1)]).then_inc(s_xn, 1)

            def turned(b, r):
                act.wait_ge(s_tr, b + 1)
                wait(act, s_hv, b - 1)
                if at_least(b, 2):
                    act.wait_ge(s_spill[r], (b - r) * 8)
                act.copy(xt_buf[:, r, :, :].rearrange("p k n -> p (k n)"), ps_tr[r][:, 0:D]).then_inc(s_xt, 1)

            def keep(b, r):
                act.wait_ge(s_hv, b + 1)
                passed(act, "act")
                act.copy(row(x_all[:, bass.ds(b, 1), :]), ps_hv[r][:, 0:D])
                act.copy(kv_all[:, bass.ds(b, 1), :, :].rearrange("p a r n -> p (a r n)"),
                         ps_hv[r][:, D:2 * D]).then_inc(s_kept, 1)

            def body(b, r):
                scale(b, r)
                if at_least(b, 1):
                    turned(b - 1, 1 - r)
                if at_least(b, 2):
                    keep(b - 2, r)

            return body, turned, keep

        def project_pe(pe):
            def products(b, r):
                pe.wait_ge(s_xt, b + 1)
                wait(pe, s_kept, b - 1)
                for k in range(KC):
                    pe.matmul(ps_hv[r][:, 0:D], xt_buf[:, r, k, :], wgnn_sb[:, k, :],
                              start=(k == 0), stop=(k == KC - 1))
                for k in range(KC):
                    pe.matmul(ps_hv[r][:, D:D + P], xt_buf[:, r, k, :], wqkv_sb[:, k, 2 * HID:3 * HID],
                              start=(k == 0), stop=(k == KC - 1))
                for k in range(KC):
                    last = pe.matmul(ps_hv[r][:, D + P:D + 2 * P], wqkv_sb[:, k, HID:2 * HID],
                                     xt_buf[:, r, k, :], start=(k == 0), stop=(k == KC - 1))
                last.then_inc(s_hv, 1)

            def body(b, r):
                pe.wait_ge(s_xn, b + 1)
                wait(pe, s_xt, b - 1)
                for k in range(KC):
                    last = pe.transpose(ps_tr[r][:, k * P:(k + 1) * P], xn_buf[:, r, k * P:(k + 1) * P], ident[:])
                last.then_inc(s_tr, 1)
                if at_least(b, 1):
                    products(b - 1, 1 - r)

            return body, products

        def spill(eng, b, r):
            eng.wait_ge(s_xt, b + 1)
            eng.dma_start(xnt[bass.ds(b, 1), :, :].rearrange("a p n -> (a p) n"),
                          xt_buf[:, r, :, :].rearrange("p k n -> p (k n)")).then_inc(s_spill[r], 16)

        with nc.Block() as block:
            @block.sync
            def _(sp):
                whole = (CHUNKS - 1) * P * P
                rest = FULL_TILES - (CHUNKS - 1) * P
                sp.wait_ge(s_pad, 3)
                for n, edges in ((0, src), (1, dst)):
                    raw = raw_i[:, n * COLS:(n + 1) * COLS].rearrange("t (c e) -> t c e", e=P)
                    sp.dma_start(raw[:, 0:CHUNKS - 1, :],
                                 edges[0:whole].rearrange("(c t e) -> t c e", t=P, e=P)).then_inc(s_edges, 16)
                    sp.dma_start(raw[0:rest, CHUNKS - 1, :],
                                 edges[whole:FULL_TILES * P].rearrange("(t e) -> t e", e=P)).then_inc(s_edges, 16)
                    sp.dma_start(raw[rest:rest + 1, CHUNKS - 1, 0:LAST_EDGES],
                                 edges[FULL_TILES * P:EDGES].rearrange("(a e) -> a e", a=1)).then_inc(s_edges, 16)
                for n, (lo, hi) in enumerate(X_LOADS[:-1]):
                    sp.dma_start(x_all[:, lo:hi, :],
                                 x[lo * P:hi * P, :].rearrange("(b p) d -> p b d", p=P)).then_inc(s_x[n], 16)
                    if n == 0:
                        sp.dma_start(wgnn_sb, w_gnn.rearrange("(k p) d -> p k d", p=P)).then_inc(s_w, 16)
                        sp.dma_start(wqkv_sb[:], w_qkv.rearrange("(k p) d -> p k d", p=P)).then_inc(s_w, 16)
                sp.dma_start(x_all[0:LAST_ROWS, BLOCKS - 1, :], x[(BLOCKS - 1) * P:NODES, :]).then_inc(s_x[4], 16)
                sp.dma_start(wout_sb[:], w_out).then_inc(s_wb, 16)
                sp.dma_start(wgate_sb[:], w_gate.rearrange("(k p) d -> p k d", p=P)).then_inc(s_wb, 16)
                sp.dma_start(b1_rows, b1.rearrange("e (f n) -> (e f) n", n=P)).then_inc(s_wb, 16)
                sp.dma_start(b2_sb[:], b2).then_inc(s_wb, 16)
                for to, bias in ((rows[:, 0:D], b_gnn), (rows[:, D:2 * D], prelu_a), (rows2[:, 0:D], b_out),
                                 (rows2[:, D:D + EXPERTS], b_gate),
                                 (rows2[:, D + EXPERTS:D + 2 * EXPERTS], gate_bias)):
                    sp.dma_start(to, bias.rearrange("(a n) -> a n", a=1)).then_inc(s_wb, 16)
                over_blocks(sp, lambda b, r: spill(sp, b, r), 0, SPLIT - 2)
                spill(sp, SPLIT - 2, 0)
                sp.wait_ge(s_wb, 9 * 16)

            @block.gpsimd
            def _(pool):
                last = (CHUNKS - 1) * P
                pool.memset(raw_i[:, last:COLS], 0).then_inc(s_pad, 1)
                pool.memset(raw_i[:, COLS + last:2 * COLS], -1).then_inc(s_pad, 1)
                pool.memset(x_all[:, BLOCKS - 1, :], 0.0).then_inc(s_pad, 1)
                pool.memset(eps_sb[:], EPS).then_inc(s_const, 1)
                pool.memset(ones[:], 1.0).then_inc(s_const, 1)
                pool.memset(ident[:], 0.0).then_inc(s_ident, 1)
                pool.wait_ge(s_ident, 1)
                pool.affine_select(out=ident[:], in_=ident[:], compare_op=ALU.not_equal, fill=1.0, base=0,
                                   pattern=[[-1, P]], channel_multiplier=1).then_inc(s_ident, 1)
                pool.iota(iota_w[:], [[1, WINDOW]], base=0, channel_multiplier=0,
                          allow_small_or_imprecise_dtypes=True).then_inc(s_const, 1)
                pool.memset(small[0:1, 256:258], 0.0).then_inc(s_const, 1)
                pool.iota(ramp, [[PER_GROUP, COLS // GROUP], [0, GROUP]], base=-PER_GROUP, channel_multiplier=0,
                          allow_small_or_imprecise_dtypes=True).then_inc(s_const, 1)
                pool.iota(small[0:1, 258:258 + ALL_GROUPS], [[P, BLOCKS], [0, GROUPS]], base=0,
                          channel_multiplier=0, allow_small_or_imprecise_dtypes=True).then_inc(s_const, 1)

            @block.tensor
            def _(pe):
                pe.wait_ge(s_ident, 2)
                for n in range(2):
                    pe.wait_ge(s_rawf, n + 1)
                    for c in range(CHUNKS):
                        last = pe.transpose(psum[4 * n + c // 4][:, c % 4 * P:(c % 4 + 1) * P],
                                            raw_f[:, n * COLS + c * P:n * COLS + (c + 1) * P], ident[:])
                    last.then_inc(s_turned, 1)
                pe.wait_ge(s_dv, 2)
                pe.wait_ge(s_w, 2 * 16)
                body, products = project_pe(pe)
                over_blocks(pe, body, 0, 6)
                pe.wait_ge(s_base, 1)
                pe.wait_ge(s_const, 6)
                pe.matmul(psum[7][:, 0:COLS // GROUP], ones[0:1, :], small[0:1, 0:COLS // GROUP],
                          start=True, stop=True).then_inc(s_basebc, 1)
                pe.wait_ge(s_wb, 9 * 16)
                pe.matmul(psum[5][:, 0:2 * D], ones[0:1, :], rows, start=True, stop=True)
                pe.matmul(psum[6][:, 0:D], ones[0:1, :], rows2[:, 0:D], start=True, stop=True)
                pe.transpose(psum[6][:, D:D + EXPERTS * FC], b1_rows, ident[0:EXPERTS * FC, 0:EXPERTS * FC])
                for n in range(2):
                    last = pe.matmul(psum[6][:, 3 * P:3 * P + EXPERTS], ones[0:1, :],
                                     rows2[:, D + n * EXPERTS:D + (n + 1) * EXPERTS],
                                     start=(n == 0), stop=(n == 1))
                last.then_inc(s_bc, 1)
                over_blocks(pe, body, 6, SPLIT)

                pe.wait_ge(s_zeros, 1)
                pe.matmul(ps_count[0:LO, :], hid_zero[:, 0:LO], hid_zero, start=True, stop=False,
                          skip_group_check=True)

                def slice_(n, r):
                    pe.wait_ge(s_slice, n + 1)
                    for g in range(SLICE):
                        window = ps_count[0:LO, bass.ds((n * SLICE + g) * PER_GROUP, HI)]
                        for t in range(g * GROUP, (g + 1) * GROUP):
                            last = pe.matmul(window, hot_lo[:, r, t, :], hot_hi[:, r, t, :],
                                             start=False, stop=False, skip_group_check=True)
                    last.then_inc(s_counted, 1)

                with pe.Fori(0, ALL_GROUPS // SLICE // 2) as pair:
                    for r in range(2):
                        slice_(pair * 2 + r, r)
                pe.matmul(ps_count[0:LO, :], hid_zero[:, 0:LO], hid_zero, start=False, stop=True,
                          skip_group_check=True).then_inc(s_counted, 1)
                pe.wait_ge(s_deg, 1)
                for h in range(P // LO):
                    pe.matmul(psum[5][:, 0:BLOCKS], select[:, h, :],
                              deg_lo.rearrange("p (b h) -> p b h", h=P // LO)[:, :, h],
                              start=(h == 0), stop=(h == P // LO - 1))
                pe.matmul(psum[6][:, 0:1], ones[0:LO, :], flag[0:LO, 0:1], start=True, stop=True)
                pe.matmul(psum[6][:, 1:2], ones[0:1, :], flag[0:1, 2:3], start=True, stop=True)
                pe.matmul(psum[6][:, 2:3], ones[:], flag[:, 3:4], start=True, stop=True).then_inc(s_deg, 1)

            @block.scalar
            def _(act):
                act.wait_ge(s_const, 6)
                body, turned, keep = project_act(act)

                def roots(n):
                    lo, hi = X_LOADS[n]
                    act.wait_ge(s_var, n + 1)
                    act.activation(ln[:, 4, lo:hi], ln[:, 3, lo:hi], ACT.Sqrt, bias=eps_sb[:, 0:1]).then_inc(s_std, 1)

                roots(0)
                act.wait_ge(s_ln, 1)
                over_blocks(act, body, 0, 6)
                for n in range(1, 5):
                    roots(n)
                act.wait_ge(s_bc, 1)
                act.copy(bgnn_bc[:], psum[5][:, 0:D])
                act.copy(prelu_bc[:], psum[5][:, D:2 * D])
                act.copy(bout_bc[:], psum[6][:, 0:D])
                act.copy(b1_t[:], psum[6][:, D:D + EXPERTS * FC])
                act.copy(gate_bc[:], psum[6][:, 3 * P:3 * P + EXPERTS])
                act.wait_ge(s_ln, 5)
                over_blocks(act, body, 6, SPLIT)

            @block.vector
            def _(dve):
                chain = [0]

                def link(ins):
                    chain[0] += 1
                    ins.then_inc(s_bn, 1)
                    dve.wait_ge(s_bn, chain[0])

                def variances(n):
                    lo, hi = X_LOADS[n]
                    dve.wait_ge(s_x[n], 16)
                    with dve.Fori(lo, hi) as b:
                        dve.bn_stats(row(stat6[:, bass.ds(b, 1), :]), row(x_all[:, bass.ds(b, 1), :])
                                     ).then_inc(s_bn, 1)
                    chain[0] += hi - lo
                    dve.wait_ge(s_bn, chain[0])
                    st = lambda m: stat6[:, lo:hi, m]
                    to = lambda m: ln[:, m, lo:hi]
                    link(dve.tensor_tensor(to(0), st(1), st(4), ALU.add))
                    link(dve.tensor_scalar(to(0), to(0), 0.5, None, ALU.mult))
                    link(dve.tensor_tensor(to(1), st(1), st(4), ALU.subtract))
                    link(dve.tensor_scalar(to(1), to(1), 0.5, None, ALU.mult))
                    link(dve.tensor_tensor(to(1), to(1), to(1), ALU.mult))
                    link(dve.tensor_tensor(to(2), st(2), st(5), ALU.add))
                    dve.scalar_tensor_tensor(out=to(3), in0=to(2), scalar=1.0 / D, in1=to(1),
                                             op0=ALU.mult, op1=ALU.add).then_inc(s_var, 1)

                def norms(n):
                    lo, hi = X_LOADS[n]
                    dve.wait_ge(s_std, n + 1)
                    link(dve.reciprocal(ln[:, 5, lo:hi], ln[:, 4, lo:hi]))
                    dve.scalar_tensor_tensor(out=ln[:, 6, lo:hi], in0=ln[:, 0, lo:hi], scalar=-1.0,
                                             in1=ln[:, 5, lo:hi], op0=ALU.mult, op1=ALU.mult).then_inc(s_ln, 1)

                dve.memset(hid_zero, 0.0).then_inc(s_zeros, 1)
                dve.wait_ge(s_const, 6)
                dve.wait_ge(s_edges, 6 * 16)
                for n in range(2):
                    dve.tensor_copy(raw_f[:, n * COLS:(n + 1) * COLS],
                                    raw_i[:, n * COLS:(n + 1) * COLS]).then_inc(s_rawf, 1)
                variances(0)
                for n, to in ((0, src_t), (1, dst_t)):
                    dve.wait_ge(s_turned, n + 1)
                    for b in range(4):
                        m = min(512, COLS - 512 * b)
                        last = dve.tensor_copy(to[:, 512 * b:512 * b + m], psum[4 * n + b][:, 0:m])
                    last.then_inc(s_dv, 1)
                dve.wait_ge(s_dv, 2)
                norms(0)
                first = small.bitcast(I32)[0:1, 0:COLS // GROUP]
                link(dve.tensor_copy(first, dst_t[0:1, :].rearrange("p (g t) -> p g t", t=GROUP)[:, :, 0]))
                link(dve.tensor_scalar(base[:], first, -LO, None, ALU.bitwise_and))
                dve.tensor_copy(small[0:1, 0:COLS // GROUP], base[:]).then_inc(s_base, 1)
                for n in range(1, 5):
                    variances(n)
                for n in range(1, 5):
                    norms(n)
                link(dve.tensor_copy(whole_i, dst_t))
                link(dve.tensor_scalar(digit_i, whole_i, LO - 1, None, ALU.bitwise_and))
                link(dve.tensor_copy(digit_lo, digit_i))
                link(dve.tensor_scalar(digit_i, whole_i, 4, None, ALU.arith_shift_right))
                link(dve.tensor_copy(digit_hi, digit_i))
                link(dve.tensor_tensor(digit_hi, digit_hi, ramp, ALU.subtract))

                def slice_(n, r, first):
                    if not first:
                        dve.wait_ge(s_counted, n - 1)
                    for digit, hot, width in ((digit_lo, hot_lo, LO), (digit_hi, hot_hi, HI)):
                        tiles = digit[:, bass.ds(n * (SLICE * GROUP), SLICE * GROUP)]
                        last = dve.tensor_tensor(
                            hot[:, r, :, :],
                            iota_w[:, 0:width].unsqueeze(1).to_broadcast([P, SLICE * GROUP, width]),
                            tiles.unsqueeze(2).to_broadcast([P, SLICE * GROUP, width]), ALU.is_equal)
                    last.then_inc(s_slice, 1)

                for r in range(2):
                    slice_(r, r, True)
                dve.wait_ge(s_basebc, 1)
                groups = "p (g t) -> p g t"
                link(dve.tensor_tensor(rel[:].rearrange(groups, t=GROUP), dst_t.rearrange(groups, t=GROUP),
                                       psum[7][:, 0:COLS // GROUP].unsqueeze(2).to_broadcast(
                                           [P, COLS // GROUP, GROUP]), ALU.subtract))
                span = small[:, 480:488]
                dve.tensor_reduce(span[:, 0:1], rel[:, 0:FULL_TILES], AX_X, ALU.min)
                link(dve.tensor_reduce(span[:, 1:2], rel[:, 0:FULL_TILES], AX_X, ALU.max))
                half = rel[0:LAST_EDGES, FULL_TILES:FULL_TILES + 1]
                dve.tensor_tensor(span[0:LAST_EDGES, 0:1], span[0:LAST_EDGES, 0:1], half, ALU.min)
                link(dve.tensor_tensor(span[0:LAST_EDGES, 1:2], span[0:LAST_EDGES, 1:2], half, ALU.max))
                dve.tensor_scalar(span[:, 2:3], span[:, 0:1], 0.0, None, ALU.is_lt)
                link(dve.tensor_scalar(span[:, 3:4], span[:, 1:2], float(WINDOW), None, ALU.is_ge))
                dve.tensor_tensor(flag[:, 3:4], span[:, 2:3], span[:, 3:4], ALU.add)
                link(dve.tensor_tensor(small[0:1, 0:ALL_GROUPS], small[0:1, 0:ALL_GROUPS],
                                       small[0:1, 256:256 + ALL_GROUPS], ALU.is_lt))
                dve.tensor_reduce(flag[0:1, 2:3], small[0:1, 0:ALL_GROUPS], AX_X, ALU.add)
                with dve.Fori(1, ALL_GROUPS // SLICE // 2) as pair:
                    for r in range(2):
                        slice_(pair * 2 + r, r, False)
                dve.wait_ge(s_counted, ALL_GROUPS // SLICE + 1)
                link(dve.tensor_copy(deg_lo, ps_count[0:LO, PER_GROUP:PER_GROUP + DEG_COLS]))
                link(dve.memset(select, 0.0))
                dve.tensor_reduce(flag[0:LO, 0:1], deg_lo, AX_X, ALU.add)
                for h in range(P // LO):
                    last = dve.tensor_copy(select[:, h, h * LO:(h + 1) * LO], ident[0:LO, 0:LO])
                last.then_inc(s_deg, 1)
                dve.wait_ge(s_deg, 2)
                dve.tensor_copy(dinv[:], psum[5][:, 0:BLOCKS])
                link(dve.tensor_scalar(flag[:, 0:1], psum[6][:, 0:1], float(EDGES), None, ALU.is_lt))
                link(dve.tensor_scalar(flag[:, 1:2], psum[6][:, 1:2], flag[:, 0:1], None, ALU.add))
                link(dve.tensor_scalar(flag[:, 1:2], psum[6][:, 2:3], flag[:, 1:2], 1.0, ALU.add, ALU.min))
                link(dve.tensor_copy(flag_i[:], flag[0:1, 1:2]))
                link(dve.tensor_scalar(flag[:, 2:3], flag[:, 1:2], OFF_GRID, None, ALU.mult))
                dve.tensor_scalar(rel[:], rel[:], flag[:, 2:3], None, ALU.subtract)

        r_digit = sem("r_digit")
        r_hot = sem("r_hot")
        r_count = sem("r_count")
        r_iota = sem("r_iota")
        hot_a = words(group_at + GROUP * P + 2 * P, GROUP * P).bitcast(BF16).rearrange(
            "p (r t n) -> p r t n", r=2, t=GROUP)
        hist = psum[5]

        with nc.Block() as block:
            @block.gpsimd
            def _(pool):
                pool.iota(iota_n, [[1, P]], base=0, channel_multiplier=0,
                          allow_small_or_imprecise_dtypes=True).then_inc(r_iota, 1)

            @block.vector
            def _(dve):
                dve.wait_ge(r_iota, 1)
                with dve.If(dve.value_load(flag_i[0:1, 0:1], min_val=0, max_val=1) > 0):
                    with dve.Fori(0, ALL_GROUPS) as g:
                        as_i = lambda n: shifted[:, n * GROUP:(n + 1) * GROUP].bitcast(I32)
                        dve.tensor_copy(as_i(0), dst_t[:, bass.ds(g * GROUP, GROUP)]).then_inc(r_digit, 1)
                        dve.wait_ge(r_digit, g * 3 + 1)
                        dve.tensor_scalar(as_i(1), as_i(0), P - 1, None, ALU.bitwise_and).then_inc(r_digit, 1)
                        dve.tensor_scalar(as_i(2), as_i(0), 7, None, ALU.arith_shift_right).then_inc(r_digit, 1)
                        dve.wait_ge(r_digit, g * 3 + 3)
                        for n, hot, width in ((1, hot_g, P), (2, hot_a, BLOCKS)):
                            dve.tensor_tensor(hot[:, 0, :, 0:width],
                                              iota_n[:, 0:width].unsqueeze(1).to_broadcast([P, GROUP, width]),
                                              as_i(n).unsqueeze(2).to_broadcast([P, GROUP, width]),
                                              ALU.is_equal).then_inc(r_hot, 1)
                        dve.wait_ge(r_count, g + 1)
                    dve.wait_ge(r_count, ALL_GROUPS + 1)
                    dve.tensor_copy(dinv[:], hist[:, 0:BLOCKS])

            @block.tensor
            def _(pe):
                with pe.If(pe.value_load(flag_i[0:1, 0:1], min_val=0, max_val=1) > 0):
                    pe.matmul(hist[:, 0:BLOCKS], hid_zero[:, 0:P], hid_zero[:, 0:BLOCKS], start=True, stop=False,
                              skip_group_check=True)
                    with pe.Fori(0, ALL_GROUPS) as g:
                        pe.wait_ge(r_hot, g * 2 + 2)
                        for t in range(GROUP):
                            last = pe.matmul(hist[:, 0:BLOCKS], hot_g[:, 0, t, :], hot_a[:, 0, t, 0:BLOCKS],
                                             start=False, stop=False, skip_group_check=True)
                        last.then_inc(r_count, 1)
                    pe.matmul(hist[:, 0:BLOCKS], hid_zero[:, 0:P], hid_zero[:, 0:BLOCKS], start=False, stop=True,
                              skip_group_check=True).then_inc(r_count, 1)

        s_self = sem("s_self")
        s_root = sem("s_root")
        s_dinv = sem("s_dinv")
        s_hi = sem("s_hi")
        s_rest = sem("s_rest")
        s_mid = sem("s_mid")
        s_low = sem("s_low")
        s_table = [sem(f"s_table{n}") for n in range(SEVENTH)]

        def over_sevenths(eng, body):
            for n in range(SEVENTH):
                body(0, n, n, n % 2)
            with eng.Fori(0, (7 - 1) // 2) as pair:
                for half in range(2):
                    for n in range(SEVENTH):
                        c = pair * 2 + (1 + half)
                        body(c, n, c * SEVENTH + n, (1 + half + n) % 2)

        with nc.Block() as block:
            @block.vector
            def _(dve):
                dve.tensor_scalar(dinv[:], dinv[:], 1.0, None, ALU.add).then_inc(s_self, 1)
                dve.wait_ge(s_root, 1)
                dve.reciprocal(dinv[:], dinv[:]).then_inc(s_dinv, 1)
                dve.wait_ge(s_dinv, 1)

                def body(c, n, b, r):
                    h, scale = row(x_all[:, bass.ds(b, 1), :]), dinv[:, bass.ds(b, 1)]
                    dve.wait_ge(s_kept, b + 1)
                    if at_least(c, 1):
                        dve.wait_ge(s_table[n], c * 16)
                    dve.tensor_scalar(parts[:, n, 0, :], h, scale, None, ALU.mult).then_inc(s_hi, 1)
                    dve.wait_ge(s_hi, b + 1)
                    wait(dve, s_low, b - 1)
                    dve.scalar_tensor_tensor(out=rest_buf[:, r, :], in0=h, scalar=scale, in1=parts[:, n, 0, :],
                                             op0=ALU.mult, op1=ALU.subtract).then_inc(s_rest, 1)
                    dve.wait_ge(s_rest, b + 1)
                    dve.tensor_copy(parts[:, n, 1, :], rest_buf[:, r, :]).then_inc(s_mid, 1)

                over_sevenths(dve, body)
                dve.wait_ge(s_kept, BLOCKS)
                k_t = kv_all[:, 0:BLOCKS - 1, 1, :]
                dve.tensor_reduce(kmax[:, 0:1], k_t, mybir.AxisListType.XY, ALU.max).then_inc(s_dinv, 1)
                dve.tensor_reduce(kmax[:, 1:2], kv_all[:, BLOCKS - 1, 1, 0:LAST_ROWS], AX_X, ALU.max
                                  ).then_inc(s_dinv, 1)
                dve.wait_ge(s_dinv, 3)
                dve.tensor_scalar(kmax[:, 0:1], kmax[:, 0:1], kmax[:, 1:2], -1.0, ALU.max, ALU.mult)

            @block.gpsimd
            def _(pool):
                def body(c, n, b, r):
                    pool.wait_ge(s_mid, b + 1)
                    pool.tensor_tensor(parts[:, n, 2, :], rest_buf[:, r, :], parts[:, n, 1, :],
                                       ALU.subtract).then_inc(s_low, 1)

                over_sevenths(pool, body)

            @block.sync
            def _(sp):
                def store(c, n, b, r):
                    sp.wait_ge(s_low, b + 1)
                    sp.dma_start(table[bass.ds(b * P, P), :],
                                 parts[:, n, :, :].rearrange("p r d -> p (r d)")).then_inc(s_table[n], 16)

                over_sevenths(sp, store)
                for n in range(SEVENTH):
                    sp.wait_ge(s_table[n], 16 * 7)

            @block.scalar
            def _(act):
                act.wait_ge(s_self, 1)
                act.activation(dinv[:], dinv[:], ACT.Sqrt).then_inc(s_root, 1)
                body, turned, keep = project_act(act)

                def with_spill(b, r):
                    body(b, r)
                    spill(act, b - 1, 1 - r)

                over_blocks(act, with_spill, SPLIT, BLOCKS)
                turned(BLOCKS - 1, 0)
                spill(act, BLOCKS - 1, 0)
                keep(BLOCKS - 2, 1)
                keep(BLOCKS - 1, 0)
                act.wait_ge(s_spill[0], 16 * (BLOCKS // 2 + 1))
                act.wait_ge(s_spill[1], 16 * (BLOCKS // 2))

            @block.tensor
            def _(pe):
                body, products = project_pe(pe)
                over_blocks(pe, body, SPLIT, BLOCKS)
                products(BLOCKS - 1, 0)

        s_zero = sem("s_zero")
        g_idx = sem("g_idx")
        g_in = sem("g_in")
        g_shift = sem("g_shift")
        g_hot = sem("g_hot")
        g_mm = sem("g_mm")
        g_add = sem("g_add")
        ps_gen = psum[0][:, 0:KC * P].rearrange("p (c n) -> p c n", c=KC)

        with nc.Block() as block:
            @block.vector
            def _(dve):
                with dve.If(dve.value_load(flag_i[0:1, 0:1], min_val=0, max_val=1) > 0):
                    dve.memset(acc_region[:], 0.0).then_inc(s_zero, 1)
                    dve.wait_ge(s_zero, 1)
                    moved = shifted[:, 0:GROUP]
                    with dve.Fori(0, ALL_GROUPS) as g:
                        dve.tensor_copy(index[:, 0:GROUP], src_t[:, bass.ds(g * GROUP, GROUP)]).then_inc(g_idx, 1)
                        dve.tensor_copy(moved, dst_t[:, bass.ds(g * GROUP, GROUP)]).then_inc(g_shift, 1)
                        with dve.Fori(0, BLOCKS) as b:
                            dve.wait_ge(g_shift, g * (BLOCKS + 1) + b + 1)
                            dve.tensor_tensor(hot_g[:, 0, :, :], iota_n.unsqueeze(1).to_broadcast([P, GROUP, P]),
                                              moved.unsqueeze(2).to_broadcast([P, GROUP, P]),
                                              ALU.is_equal).then_inc(g_hot, 1)
                            dve.wait_ge(g_hot, g * BLOCKS + b + 1)
                            dve.tensor_scalar(moved, moved, float(P), None, ALU.subtract).then_inc(g_shift, 1)
                            dve.wait_ge(g_mm, g * BLOCKS + b + 1)
                            dve.tensor_tensor(acc_t[:, :, bass.ds(b * P, P)], acc_t[:, :, bass.ds(b * P, P)],
                                              ps_gen, ALU.add).then_inc(g_add, 1)
                            dve.wait_ge(g_add, g * BLOCKS + b + 1)

            @block.gpsimd
            def _(pool):
                with pool.If(pool.value_load(flag_i[0:1, 0:1], min_val=0, max_val=1) > 0):
                    with pool.Fori(0, ALL_GROUPS) as g:
                        pool.wait_ge(g_idx, g + 1)
                        passed(pool, "pool")
                        for t in range(GROUP):
                            pool.indirect_dma_start(
                                out=gathered[:, t, :], out_offset=None, in_=table[:, :],
                                in_offset=bass.IndirectOffsetOnAxis(ap=index[:, t:t + 1], axis=0)
                            ).then_inc(g_in, 16)

            @block.tensor
            def _(pe):
                with pe.If(pe.value_load(flag_i[0:1, 0:1], min_val=0, max_val=1) > 0):
                    with pe.Fori(0, ALL_GROUPS) as g:
                        pe.wait_ge(g_in, (g + 1) * (16 * GROUP))
                        passed(pe, "pe")
                        with pe.Fori(0, BLOCKS) as b:
                            pe.wait_ge(g_hot, g * BLOCKS + b + 1)
                            for c in range(KC):
                                for n in range(PARTS * GROUP):
                                    t, part = n // PARTS, n % PARTS
                                    at = part * D + c * P
                                    last = pe.matmul(ps_gen[:, c, :], gathered[:, t, at:at + P],
                                                     hot_g[:, 0, t, :], start=(n == 0),
                                                     stop=(n == PARTS * GROUP - 1))
                            last.then_inc(g_mm, 1)

        s_w1 = [sem(f"s_w1_{e}") for e in range(EXPERTS)]
        s_w2 = [sem(f"s_w2_{e}") for e in range(EXPERTS)]
        s_idx = sem("s_idx")
        s_gath = [sem(f"s_gath{q}") for q in range(GROUPS)]
        s_hot = sem("s_hot")
        s_agg = sem("s_agg")
        s_add = sem("s_add")
        s_ld = [sem(f"s_ld{r}") for r in range(2)]
        s_store = [sem(f"s_store{r}") for r in range(2)]
        s_aggt = sem("s_aggt")
        s_a2 = sem("s_a2")
        s_res = sem("s_res")
        s_moment = sem("s_moment")
        s_root2 = sem("s_root2")
        s_rstd = sem("s_rstd")
        s_xn2 = sem("s_xn2")
        s_a4 = sem("s_a4")
        s_x2t = sem("s_x2t")
        s_a6 = sem("s_a6")
        s_lg = sem("s_lg")
        s_top = sem("s_top")
        s_diff = sem("s_diff")
        s_e2 = sem("s_e2")
        s_wts = sem("s_wts")
        s_comb = sem("s_comb")
        s_a8 = sem("s_a8")
        s_combt = sem("s_combt")
        s_a9 = sem("s_a9")
        s_b2 = sem("s_b2")
        s_h1 = sem("s_h1")
        s_relu = sem("s_relu")
        s_h2 = sem("s_h2")
        s_out = sem("s_out")
        ps_agg = [psum[0], psum[1]]
        ps_h = [psum[2], psum[3]]
        ps_y = [psum[4], psum[5]]
        ps_a = psum[6]
        ps_b = psum[7]
        RES_OPS = 9
        s_exp = sem("s_exp")
        s_exp_tr = sem("s_exp_tr")
        s_exp_n = sem("s_exp_n")
        s_ctx = sem("s_ctx")
        s_cchain = sem("s_cchain")
        s_cm = sem("s_cm")
        s_c = sem("s_c")
        s_cev = sem("s_cev")

        def over_steps(eng, body):
            body(0, 0, True, False, False)
            body(1, 1, True, False, True)
            body(2, 0, True, True, True)
            body(3, 1, True, True, True)
            with eng.Fori(0, PAIRS - 1) as pair:
                for parity in range(2):
                    body(pair * 2 + (4 + parity), parity, True, True, True)
            body(BLOCKS - 1, 0, True, True, True)
            body(BLOCKS, 1, False, True, True)
            body(BLOCKS + 1, 0, False, True, False)

        with nc.Block() as block:
            @block.sync
            def _(sp):
                def load_w1(e):
                    sp.dma_start(w1_sb[:, e, :, :], w1[e].rearrange("(k p) f -> p k f", p=P)).then_inc(s_w1[e], 16)

                def load_w2(e):
                    sp.dma_start(w2_sb[:, e, :, :], w2[e].rearrange("(f p) d -> p f d", p=P)).then_inc(s_w2[e], 16)

                def load(b, r, n):
                    wait(sp, s_res, (b - 1) * RES_OPS)
                    at = b * P
                    sp.dma_start(x_ld[0:n, r, :], x[bass.ds(at, n), :]).then_inc(s_ld[r], 16)
                    sp.dma_start(xt_ld[:, r, :, :].rearrange("p k n -> p (k n)"),
                                 xnt[bass.ds(b, 1), :, :].rearrange("a p n -> (a p) n")).then_inc(s_ld[r], 16)
                    sp.dma_start(h_ld[:, r, :, :].rearrange("p k d -> p (k d)"), table[bass.ds(at, P), :]).then_inc(s_ld[r], 16)

                def store(b, r, n):
                    sp.wait_ge(s_out, EXPERTS * (b + 1))
                    sp.dma_start(out[bass.ds(b * P, n), :], acc[0:n, r, :]).then_inc(s_store[r], 16)

                def body(s, r, agg, experts, stage):
                    if agg:
                        load(s, r, LAST_ROWS if isinstance(s, int) and s == BLOCKS - 1 else P)
                    if isinstance(s, int) and s == 0:
                        early = kv_at // (FC * D)
                        for e in range(early):
                            load_w1(e)
                        sp.wait_ge(s_ctx, 1)
                        for e in range(EXPERTS):
                            if e >= early:
                                load_w1(e)
                            load_w2(e)
                    if experts:
                        last = isinstance(s, int) and s == BLOCKS + 1
                        store(s - 2, r, LAST_ROWS if last else P)

                over_steps(sp, body)
                sp.wait_ge(s_store[0], 16 * (BLOCKS // 2 + 1))
                sp.wait_ge(s_store[1], 16 * (BLOCKS // 2))

            @block.gpsimd
            def _(pool):
                with pool.Fori(0, BLOCKS) as s:
                    for q in range(GROUPS):
                        pool.wait_ge(s_idx, s * GROUPS + (q + 1))
                        passed(pool, "pool")
                        for t in range(q * GROUP, (q + 1) * GROUP):
                            pool.indirect_dma_start(
                                out=gathered[:, t, :], out_offset=None, in_=table[:, :],
                                in_offset=bass.IndirectOffsetOnAxis(ap=index[:, t:t + 1], axis=0)
                            ).then_inc(s_gath[q], 16)

            @block.scalar
            def _(act):
                with act.If(act.value_load(flag_i[0:1, 0:1], min_val=0, max_val=1) < 1):
                    act.activation(acc_region[:, ACC_COLS:], ones[:, 0:1].to_broadcast([P, ACC_COLS]),
                                   ACT.Copy, scale=0.0).then_inc(s_zero, 1)

                def body(s, r, agg, experts, stage):
                    b, rb = s - 1, 1 - r

                    def relu(e):
                        if not experts:
                            return
                        at = (s - 2) * EXPERTS + e
                        act.wait_ge(s_h1, at + 1)
                        wait(act, s_h2, at - 1)
                        for f in range(FC):
                            last = act.activation(hid_t[:, e % 2, f, :], ps_h[e % 2][:, f * P:(f + 1) * P],
                                                  ACT.Relu, bias=b1_t[:, e * FC + f:e * FC + f + 1])
                        last.then_inc(s_relu, 1)

                    if isinstance(s, int) and s == 0:
                        def exps(q, n):
                            act.activation(exp_t.rearrange("p (b n) -> p b n", n=P),
                                           kv_all[:, bass.ds(n * QUAD, QUAD), 1, :], ACT.Exp,
                                           bias=kmax[:, 0:1]).then_inc(s_exp, 1)

                        exps(0, 0)
                        with act.Fori(1, QUADS) as n:
                            act.wait_ge(s_exp_n, n)
                            passed(act, "act")
                            exps(0, n)
                        act.wait_ge(s_exp_n, QUADS)
                        act.activation(exp_t[:, 0:LAST_ROWS], kv_all[:, BLOCKS - 1, 1, 0:LAST_ROWS], ACT.Exp,
                                       bias=kmax[:, 0:1]).then_inc(s_exp, 1)
                    for e in range(4):
                        relu(e)
                    if stage:
                        act.wait_ge(s_add, s * GROUPS + 2 if agg else BLOCKS * GROUPS)
                        wait(act, s_a2, b)
                        passed(act, "act")
                        act.copy(agg_t[:], acc_t[:, :, bass.ds(b * P, P)]).then_inc(s_aggt, 1)
                    relu(4)
                    if stage:
                        act.wait_ge(s_moment, 2 * b + 2)
                        act.activation(mv[:, 2:3], mv[:, 1:2], ACT.Sqrt, bias=eps_sb[:, 0:1]).then_inc(s_root2, 1)
                    relu(5)
                    if stage:
                        act.wait_ge(s_a4, b + 1)
                        wait(act, s_h1, (b - 1) * EXPERTS)
                        act.copy(x2_t[:, rb, :, :].rearrange("p k n -> p (k n)"),
                                 ps_b[:, 0:D]).then_inc(s_x2t, 1)
                    relu(6)
                    if stage:
                        act.wait_ge(s_diff, b + 1)
                        act.activation(gate[:, 2, 1:2], gate[:, 2, 0:1], ACT.Exp).then_inc(s_e2, 1)
                    relu(7)

                over_steps(act, body)

            @block.vector
            def _(dve):
                def one_hot(s, q):
                    tiles = rel[:, bass.ds(s * STEP_TILES + q * GROUP, GROUP)]
                    dve.tensor_tensor(hot_w[:, q % 2, :, :],
                                      iota_w[:].unsqueeze(1).to_broadcast([P, GROUP, WINDOW]),
                                      tiles.unsqueeze(2).to_broadcast([P, GROUP, WINDOW]),
                                      ALU.is_equal).then_inc(s_hot, 1)

                def fetch(s, q):
                    dve.tensor_copy(index[:, q * GROUP:(q + 1) * GROUP],
                                    src_t[:, bass.ds(s * STEP_TILES + q * GROUP, GROUP)]).then_inc(s_idx, 1)

                def add(s, q):
                    g = s * GROUPS + q
                    at = dve.value_load(base[0:1, bass.ds(g, 1)], min_val=0, max_val=NODES - 1)
                    if q < GROUPS - 1:
                        one_hot(s, q + 1)
                    else:
                        one_hot(s + 1, 0)
                    window = acc_t[:, :, bass.ds(at, WINDOW)]
                    wait(dve, s_add, g)
                    dve.wait_ge(s_agg, g + 1)
                    dve.tensor_tensor(window, window, ps_agg[q % 2][:, 0:KC * WINDOW].rearrange(
                        "p (c n) -> p c n", c=KC), ALU.add).then_inc(s_add, 1)
                    fetch(s + 1, q)

                def body(s, r, agg, experts, stage):
                    b, rb = s - 1, 1 - r
                    x1 = acc[:, rb, :]
                    t0, t1 = tmp[:], xn2[:]

                    def combine(e):
                        if not experts:
                            return
                        at = (s - 2) * EXPERTS + e
                        dve.wait_ge(s_h2, at + 1)
                        wait(dve, s_out, at)
                        dve.scalar_tensor_tensor(out=acc[:, r, :], in0=ps_y[e % 2][:, 0:D],
                                                 scalar=comb[:, r, e:e + 1], in1=acc[:, r, :],
                                                 op0=ALU.mult, op1=ALU.add).then_inc(s_out, 1)

                    first_step = isinstance(s, int) and s == 0
                    if isinstance(s, int) and s == 1:
                        attention_matrix()
                    if agg:
                        add(s, 0)
                    if first_step:
                        attention_sums(0)
                    combine(0)
                    combine(1)
                    if agg:
                        add(s, 1)
                    if first_step:
                        attention_sums(1)
                    combine(2)
                    if stage:
                        n = b * RES_OPS
                        if not (isinstance(b, int) and b < 2):
                            dve.wait_ge(s_store[rb], (b - rb) * 8)
                        dve.wait_ge(s_ld[rb], (b - rb) * 24 + 48)
                        dve.tensor_tensor(x1, x_ld[:, rb, :], bout_bc[:], ALU.add).then_inc(s_res, 1)
                        dve.wait_ge(s_a2, b + 1)
                        dve.tensor_tensor(t0, h_ld[:, rb, 2, :], ps_a[:, 0:D], ALU.add).then_inc(s_res, 1)
                        dve.wait_ge(s_res, n + 2)
                        dve.tensor_tensor(t0, t0, h_ld[:, rb, 1, :], ALU.add).then_inc(s_res, 1)
                        dve.tensor_tensor(x1, x1, ps_a[:, D:2 * D], ALU.add).then_inc(s_res, 1)
                        dve.wait_ge(s_res, n + 3)
                        dve.tensor_tensor(t0, t0, h_ld[:, rb, 0, :], ALU.add).then_inc(s_res, 1)
                        dve.wait_ge(s_res, n + 5)
                        dve.scalar_tensor_tensor(out=t1, in0=t0, scalar=dinv[:, bass.ds(b, 1)], in1=bgnn_bc[:],
                                                 op0=ALU.mult, op1=ALU.add).then_inc(s_res, 1)
                        dve.wait_ge(s_res, n + 6)
                        dve.scalar_tensor_tensor(out=t0, in0=t1, scalar=0.0, in1=prelu_bc[:],
                                                 op0=ALU.min, op1=ALU.mult).then_inc(s_res, 1)
                        dve.wait_ge(s_res, n + 7)
                        dve.scalar_tensor_tensor(out=t1, in0=t1, scalar=0.0, in1=t0,
                                                 op0=ALU.max, op1=ALU.add).then_inc(s_res, 1)
                        dve.wait_ge(s_res, n + 8)
                        dve.tensor_tensor(x1, x1, t1, ALU.add).then_inc(s_res, 1)
                        dve.wait_ge(s_res, n + 9)
                        dve.bn_stats(stats[:], x1).then_inc(s_moment, 1)
                        dve.wait_ge(s_moment, 2 * b + 1)
                        passed(dve, "dve")
                        dve.bn_aggr(mv[:, 0:2], stats[:]).then_inc(s_moment, 1)
                    combine(3)
                    if agg:
                        add(s, 2)
                    if first_step:
                        attention_sums(2)
                    if stage:
                        dve.wait_ge(s_root2, b + 1)
                        dve.reciprocal(mv[:, 3:4], mv[:, 2:3]).then_inc(s_rstd, 1)
                        dve.wait_ge(s_rstd, b + 1)
                        dve.tensor_scalar(xn2[:], x1, mv[:, 0:1], mv[:, 3:4], ALU.subtract,
                                          ALU.mult).then_inc(s_xn2, 1)
                    combine(4)
                    combine(5)
                    if agg:
                        add(s, 3)
                    if first_step:
                        attention_sums(3)
                    if stage:
                        logits, top, pair_, hot1, hot2 = (gate[:, n, :] for n in (0, 1, 2, 3, 4))
                        dve.wait_ge(s_a6, b + 1)
                        dve.tensor_tensor(logits, ps_b[:, D:D + EXPERTS], gate_bc[:], ALU.add).then_inc(s_lg, 1)
                        dve.wait_ge(s_lg, b + 1)
                        passed(dve, "dve")
                        dve.max(top, logits).then_inc(s_top, 1)
                        dve.wait_ge(s_top, 3 * b + 1)
                        passed(dve, "dve")
                        dve.max_index(gate_i[:], top, logits).then_inc(s_top, 1)
                        dve.tensor_tensor(pair_[:, 0:1], top[:, 1:2], top[:, 0:1], ALU.subtract).then_inc(s_diff, 1)
                        dve.wait_ge(s_top, 3 * b + 2)
                        dve.tensor_copy(gate[:, 5, 0:2], gate_i[:, 0:2]).then_inc(s_top, 1)
                        dve.wait_ge(s_e2, b + 1)
                        dve.tensor_scalar(pair_[:, 2:3], pair_[:, 1:2], 1.0, None, ALU.add).then_inc(s_wts, 1)
                        dve.wait_ge(s_wts, 3 * b + 1)
                        dve.reciprocal(pair_[:, 3:4], pair_[:, 2:3]).then_inc(s_wts, 1)
                        dve.wait_ge(s_wts, 3 * b + 2)
                        dve.tensor_tensor(pair_[:, 4:5], pair_[:, 1:2], pair_[:, 3:4], ALU.mult).then_inc(s_wts, 1)
                        dve.wait_ge(s_wts, 3 * b + 3)
                        dve.wait_ge(s_top, 3 * b + 3)
                        dve.tensor_scalar(hot1, iota_e, gate[:, 5, 0:1], pair_[:, 3:4], ALU.is_equal,
                                          ALU.mult).then_inc(s_comb, 1)
                        dve.tensor_scalar(hot2, iota_e, gate[:, 5, 1:2], pair_[:, 4:5], ALU.is_equal,
                                          ALU.mult).then_inc(s_comb, 1)
                        dve.wait_ge(s_comb, 3 * b + 2)
                        dve.tensor_tensor(comb[:, rb, :], hot1, hot2, ALU.add).then_inc(s_comb, 1)
                    combine(6)
                    if stage:
                        dve.wait_ge(s_a8, b + 1)
                        dve.tensor_copy(comb_t[:], ps_b[0:EXPERTS, D + P:D + 2 * P]).then_inc(s_combt, 1)
                    combine(7)
                    if stage:
                        dve.wait_ge(s_a9, b + 1)
                        dve.tensor_tensor(x1, x1, ps_a[:, 0:D], ALU.add).then_inc(s_b2, 1)
                        dve.wait_ge(s_b2, b + 1)

                def attention_sums(q):
                    with dve.Fori(3 * q, 3 * q + 3) as n:
                        dve.wait_ge(s_exp_tr, n + 1)
                        dve.tensor_copy(exp_n, ps_h[0][:, :]).then_inc(s_exp_n, 1)
                    if q == 3:
                        dve.wait_ge(s_exp_tr, QUADS + 1)
                        dve.tensor_copy(exp_n[0:LAST_ROWS, 0:P], ps_h[0][0:LAST_ROWS, 0:P]).then_inc(s_exp_n, 1)

                def attention_matrix():
                    dve.memset(ctx_m, 0.0).then_inc(s_cchain, 1)
                    dve.wait_ge(s_ctx, 1)
                    dve.reciprocal(flag[:, 3:4], ps_y[1][:, 0:1]).then_inc(s_cchain, 1)
                    dve.wait_ge(s_cchain, 2)
                    for h in range(HEADS):
                        at = slice(h * HEAD, (h + 1) * HEAD)
                        last = dve.tensor_scalar(ctx_m[at, at], ps_y[0][at, at], flag[at, 3:4], HEAD ** -0.5,
                                                 ALU.mult, ALU.mult)
                    last.then_inc(s_cm, 1)
                    dve.wait_ge(s_c, 2)
                    dve.tensor_copy(ctx_mt, ps_a[:, 0:P]).then_inc(s_cev, 1)
                    dve.tensor_copy(wq_t.rearrange("p k n -> p (k n)"), ps_b[:, 0:D]).then_inc(s_cev, 1)
                    dve.wait_ge(s_c, 3)
                    dve.tensor_copy(ctx_w, ps_a[:, P:P + D]).then_inc(s_cev, 1)
                    dve.wait_ge(s_c, 4)
                    dve.tensor_copy(mix_w[:].rearrange("p k n -> p (k n)"), ps_h[0][:, :]).then_inc(s_cev, 1)

                for q in range(GROUPS):
                    fetch(0, q)
                one_hot(0, 0)
                with dve.If(dve.value_load(flag_i[0:1, 0:1], min_val=0, max_val=1) < 1):
                    dve.memset(acc_region[:, 0:ACC_COLS], 0.0).then_inc(s_zero, 1)
                    dve.wait_ge(s_zero, 2)
                over_steps(dve, body)

            @block.tensor
            def _(pe):
                def attention_sums(q):
                    def quad(n, count_, final):
                        pe.wait_ge(s_exp, n + 1)
                        rows_of = [P] * count_ if not final else [LAST_ROWS]
                        for j, m in enumerate(rows_of):
                            last = pe.transpose(ps_h[0][0:m, j * P:(j + 1) * P], exp_t[:, j * P:j * P + m], ident[:])
                        last.then_inc(s_exp_tr, 1)
                        pe.wait_ge(s_exp_n, n + 1)
                        for j, m in enumerate(rows_of):
                            first = isinstance(n, int) and n == 0 and j == 0
                            e = exp_n[0:m, j * P:(j + 1) * P]
                            pe.matmul(ps_y[0][:, 0:P], e, row(kv_all[0:m, bass.ds(n * QUAD + j, 1), 0, :]),
                                      start=first, stop=final, skip_group_check=True)
                            last = pe.matmul(ps_y[1][:, 0:1], e, ones[0:m, 0:1], start=first, stop=final,
                                             skip_group_check=True)
                        return last

                    lo = 3 * q
                    if q == 0:
                        quad(0, QUAD, False)
                        lo = 1
                    with pe.Fori(lo, 3 * q + 3) as n:
                        quad(n, QUAD, False)
                    if q == 3:
                        quad(QUADS, 1, True).then_inc(s_ctx, 1)

                def attention_matrix():
                    for k in range(KC):
                        last = pe.transpose(ps_b[:, k * P:(k + 1) * P], wqkv_sb[:, k, 0:HID], ident[:])
                    last.then_inc(s_c, 1)
                    pe.wait_ge(s_cm, 1)
                    pe.transpose(ps_a[:, 0:P], ctx_m, ident[:]).then_inc(s_c, 1)
                    pe.wait_ge(s_cev, 1)
                    pe.matmul(ps_a[:, P:P + D], ctx_mt, wout_sb[:], start=True, stop=True).then_inc(s_c, 1)
                    pe.wait_ge(s_cev, 3)
                    for k in range(KC):
                        last = pe.matmul(ps_h[0][:, k * D:(k + 1) * D], wq_t[:, k, :], ctx_w,
                                         start=True, stop=True)
                    last.then_inc(s_c, 1)
                    pe.wait_ge(s_cev, 4)

                def body(s, r, agg, experts, stage):
                    b, rb = s - 1, 1 - r

                    def aggregate(q):
                        if not agg:
                            return
                        g = s * GROUPS + q
                        pe.wait_ge(s_hot, g + 1)
                        wait(pe, s_add, g - 1)
                        pe.wait_ge(s_gath[q], s * (16 * GROUP) + 16 * GROUP)
                        for c in range(KC):
                            for n in range(PARTS * GROUP):
                                t, at = n // PARTS, n % PARTS * D + c * P
                                last = pe.matmul(ps_agg[q % 2][:, c * WINDOW:(c + 1) * WINDOW],
                                                 gathered[:, q * GROUP + t, at:at + P], hot_w[:, q % 2, t, :],
                                                 start=(n == 0), stop=(n == PARTS * GROUP - 1))
                        last.then_inc(s_agg, 1)

                    def up(e):
                        at = (s - 2) * EXPERTS + e
                        wait(pe, s_relu, at - 1)
                        if isinstance(s, int) and s == 2:
                            pe.wait_ge(s_w1[e], 16)
                        for f in range(FC):
                            for k in range(KC):
                                last = pe.matmul(ps_h[e % 2][:, f * P:(f + 1) * P],
                                                 w1_sb[:, e, k, f * P:(f + 1) * P], x2_t[:, r, k, :],
                                                 start=(k == 0), stop=(k == KC - 1))
                        last.then_inc(s_h1, 1)

                    def down(e):
                        at = (s - 2) * EXPERTS + e
                        pe.wait_ge(s_relu, at + 1)
                        wait(pe, s_out, at - 1)
                        if isinstance(s, int) and s == 2:
                            pe.wait_ge(s_w2[e], 16)
                        for f in range(FC):
                            last = pe.matmul(ps_y[e % 2][:, 0:D], hid_t[:, e % 2, f, :], w2_sb[:, e, f, :],
                                             start=(f == 0), stop=(f == FC - 1))
                        last.then_inc(s_h2, 1)

                    def sums_by_node():
                        pe.wait_ge(s_aggt, b + 1)
                        wait(pe, s_b2, b)
                        for k in range(KC):
                            pe.transpose(ps_a[:, k * P:(k + 1) * P], agg_t[:, k, :], ident[:])
                        pe.wait_ge(s_ld[rb], (b - rb) * 24 + 48)
                        for k in range(KC):
                            last = pe.matmul(ps_a[:, D:2 * D], xt_ld[:, rb, k, :], mix_w[:, k, :],
                                             start=(k == 0), stop=(k == KC - 1))
                        last.then_inc(s_a2, 1)

                    def turn_xn2():
                        pe.wait_ge(s_xn2, b + 1)
                        for k in range(KC):
                            last = pe.transpose(ps_b[:, k * P:(k + 1) * P], xn2[:, k * P:(k + 1) * P], ident[:])
                        last.then_inc(s_a4, 1)

                    def logits():
                        pe.wait_ge(s_x2t, b + 1)
                        for k in range(KC):
                            last = pe.matmul(ps_b[:, D:D + EXPERTS], x2_t[:, rb, k, :], wgate_sb[:, k, :],
                                             start=(k == 0), stop=(k == KC - 1))
                        last.then_inc(s_a6, 1)

                    def turn_weights():
                        pe.wait_ge(s_comb, 3 * b + 3)
                        pe.transpose(ps_b[0:EXPERTS, D + P:D + 2 * P], comb[:, rb, :], ident[:]).then_inc(s_a8, 1)

                    def bias2():
                        pe.wait_ge(s_combt, b + 1)
                        pe.matmul(ps_a[:, 0:D], comb_t[:], b2_sb[:], start=True, stop=True).then_inc(s_a9, 1)

                    after = {1: [lambda: aggregate(1)], 2: [sums_by_node], 3: [lambda: aggregate(2)],
                             4: [turn_xn2], 5: [lambda: aggregate(3), logits], 6: [turn_weights], 7: [bias2]}
                    work = {sums_by_node, turn_xn2, logits, turn_weights, bias2}
                    if isinstance(s, int) and s == 0:
                        for q in range(GROUPS):
                            aggregate(q)
                            attention_sums(q)
                        return
                    if isinstance(s, int) and s == 1:
                        attention_matrix()
                    aggregate(0)
                    if experts:
                        up(0)
                    for e in range(EXPERTS):
                        if experts:
                            if e < EXPERTS - 1:
                                up(e + 1)
                            down(e)
                        for piece in after.get(e, ()):
                            if stage or piece not in work:
                                piece()

                over_steps(pe, body)


_INS = ['x', 'src', 'dst', 'L0_gnn_W', 'L0_gnn_b', 'L0_gnn_prelu_a', 'L0_mix_W_qkv', 'L0_mix_W_out',
        'L0_mix_b_out', 'L0_ffn_Wg', 'L0_ffn_bg', 'L0_ffn_bias', 'L0_ffn_W1', 'L0_ffn_b1', 'L0_ffn_W2',
        'L0_ffn_b2']


def kernel(**inputs):
    import numpy as _np
    import concourse.bacc as _bacc
    from concourse import mybir as _mybir
    from concourse.bass_utils import run_bass_kernel_spmd as _run

    nc = _bacc.Bacc("TRN2", target_bir_lowering=False, num_devices=1)
    arrays, args = {}, []
    for name in _INS:
        a = _np.ascontiguousarray(inputs[name])
        arrays[f"in_{name}"] = a
        args.append(nc.dram_tensor(f"in_{name}", a.shape, _mybir.dt.from_np(a.dtype), kind="ExternalInput").ap())
    f32 = _mybir.dt.float32
    args.append(nc.dram_tensor("out_0", (NODES, D), f32, kind="ExternalOutput").ap())
    args.append(nc.dram_tensor("table", (BLOCKS * P, PARTS * D), _mybir.dt.bfloat16, kind="Internal").ap())
    args.append(nc.dram_tensor("xnt", (BLOCKS, P, D), f32, kind="Internal").ap())
    gps_layer(nc, *args)
    r = _run(nc, [arrays], core_ids=[0])
    return r.results[0]["out_0"]
```

```python
from contextlib import ExitStack

import concourse.bass as bass
from concourse import mybir

F32 = mybir.dt.float32
BF16 = mybir.dt.bfloat16
I32 = mybir.dt.int32
U32 = mybir.dt.uint32
ALU = mybir.AluOpType
ACT = mybir.ActivationFunctionType
AX_X = mybir.AxisListType.X

P = 128
NODES, D = 6250, 256
EDGES = 200000
KC = D // P
HEADS, HEAD = 4, 32
HID = HEADS * HEAD
EXPERTS, EXPERT_DIM = 8, 512
FC = EXPERT_DIM // P
EPS = 1e-5

BLOCKS = -(-NODES // P)
LAST_ROWS = NODES - (BLOCKS - 1) * P
GROUP = 8
GROUPS = 4
STEP_TILES = GROUP * GROUPS
TILES = BLOCKS * STEP_TILES
FULL_TILES = EDGES // P
LAST_EDGES = EDGES - FULL_TILES * P
CHUNKS = -(-TILES // P)
COLS = CHUNKS * P
WINDOW = 64
ACC_COLS = BLOCKS * P + WINDOW
FIRST_COLS = 4 * P
PARTS = 3
PAIRS_OF_PARTS = PARTS * PARTS
LO = 16
HI = 6
DEG_COLS = BLOCKS * P // LO
PER_GROUP = 2
ALL_GROUPS = TILES // GROUP
SLICE = 7
SEVENTH = BLOCKS // 7
PAIRS = (BLOCKS - 3) // 2
STACK = 4
SECTION = 4
SECTIONS = ALL_GROUPS // SLICE // SECTION
SPAN = SECTION * SLICE * PER_GROUP
REACH = SPAN + HI - PER_GROUP
HALF_BANK = 256
BEFORE_COUNT = 20
AFTER_COUNT = 1
SPLIT = BEFORE_COUNT + 2 * SECTIONS + AFTER_COUNT
PER_SEVENTH = (BLOCKS - SPLIT) // 7
QUAD = 4
QUADS = (BLOCKS - 1) // QUAD
OFF_GRID = 1.0e6


def gps_layer(nc, x, src, dst, w_gnn, b_gnn, prelu_a, w_qkv, w_out, b_out, w_gate, b_gate, gate_bias,
              w1, b1, w2, b2, out, table, xnt):
    assert EDGES <= TILES * P and GROUPS == 4 and BLOCKS % 2 == 1

    with ExitStack() as ctx:
        def sb(name, shape, dt=F32):
            return ctx.enter_context(nc.sbuf_tensor(name, shape, dt))

        def sem(name):
            return ctx.enter_context(nc.semaphore(name))

        def wait(eng, semaphore, value):
            if isinstance(value, int) and value <= 0:
                return
            eng.wait_ge(semaphore, value)

        s_passed = {name: sem(f"s_passed_{name}") for name in ("act", "dve", "pool", "pe")}

        def passed(eng, name):
            eng.sem_inc(s_passed[name], 1)

        psum_all = ctx.enter_context(nc.psum_tensor("psum_all", [P, 8 * 512], F32))
        psum = [psum_all[:, n * 512:(n + 1) * 512] for n in range(8)]

        src_t = sb("src_t", [P, COLS], I32)
        rel = sb("rel", [P, COLS], BF16)
        base = sb("base", [1, COLS // GROUP], I32)
        ident = sb("ident", [P, P])
        ones = sb("ones", [P, P])
        iota_w = sb("iota_w", [P, WINDOW])
        iota_e = iota_w[:, 0:EXPERTS]
        dinv = sb("dinv", [P, BLOCKS])
        flag = sb("flag", [P, 4])
        flag_i = sb("flag_i", [1, 1], I32)
        wqkv_sb = sb("wqkv_sb", [P, KC, 3 * HID])
        wout_sb = sb("wout_sb", [P, D])
        mix_w = sb("mix_w", [P, KC, D])
        wgate_sb = sb("wgate_sb", [P, KC, EXPERTS])
        wgate_parts = sb("wgate_parts", [P, KC, PARTS, EXPERTS], BF16)
        wgate_rest = sb("wgate_rest", [P, KC, EXPERTS])
        b1_t = sb("b1_t", [P, EXPERTS * FC])
        b2_parts = sb("b2_parts", [PAIRS_OF_PARTS * EXPERTS, D], BF16)
        ident_b = sb("ident_b", [P, P], BF16)
        bgnn_bc = sb("bgnn_bc", [P, D])
        prelu_bc = sb("prelu_bc", [P, D])
        bout_bc = sb("bout_bc", [P, D])
        gate_bc = sb("gate_bc", [P, EXPERTS])
        eps_sb = sb("eps_sb", [P, 1])
        kmax = sb("kmax", [P, 2])

        hot_w = sb("hot_w", [P, 2, GROUP, WINDOW], BF16)
        index = sb("index", [P, STEP_TILES], I32)
        x_ld = sb("x_ld", [P, 2, D])
        xt_ld = sb("xt_ld", [P, 2, KC, P])
        h_ld = sb("h_ld", [P, 2, PARTS, D], BF16)
        agg_t = sb("agg_t", [P, KC, P])
        tmp = sb("tmp", [P, D])
        acc = sb("acc", [P, 2, D])
        stats = sb("stats", [P, 6])
        mv = sb("mv", [P, 4])
        xn2 = sb("xn2", [P, D])
        x2_t = sb("x2_t", [P, 2, KC, P])
        gate = sb("gate", [P, 6, EXPERTS])
        gate_i = sb("gate_i", [P, EXPERTS], U32)
        comb = sb("comb", [P, 2, EXPERTS])
        comb_parts = sb("comb_parts", [P, PARTS, PARTS, EXPERTS], BF16)
        comb_rest = sb("comb_rest", [P, 2, EXPERTS])
        comb_t = sb("comb_t", [PAIRS_OF_PARTS * EXPERTS, P], BF16)
        hid_t = sb("hid_t", [P, 2, FC, P])

        acc_region = sb("acc_region", [P, 2 * ACC_COLS])
        w_region = sb("w_region", [P, 2 * EXPERTS * FC * D])
        g_region = sb("g_region", [P, STEP_TILES * PARTS * D], BF16)

        hid_zero = hot_w[:, 0, :, :].rearrange("p t n -> p (t n)")
        acc_t = acc_region[:, :].rearrange("p (c n) -> p c n", c=KC)
        x_all = acc_region[:, 0:BLOCKS * D].rearrange("p (b d) -> p b d", d=D)
        w1_sb = w_region[:, 0:EXPERTS * FC * D].rearrange("p (e k f) -> p e k f", e=EXPERTS, k=KC)
        w2_sb = w_region[:, EXPERTS * FC * D:].rearrange("p (e f d) -> p e f d", e=EXPERTS, f=FC)
        kv_at = 2 * EXPERTS * FC * D - BLOCKS * 2 * P
        kv_all = w_region[:, kv_at:].rearrange("p (b r n) -> p b r n", r=2, n=P)
        xn_buf = w_region[:, 0:2 * D].rearrange("p (r d) -> p r d", r=2)
        parts = w_region[:, 4 * D:4 * D + SEVENTH * PARTS * D // 2].bitcast(BF16).rearrange(
            "p (b r d) -> p b r d", b=SEVENTH, r=PARTS)
        assert 4 * D + SEVENTH * PARTS * D // 2 <= kv_at
        gathered = g_region[:, :].rearrange("p (t d) -> p t d", d=PARTS * D)

        base_bc = w_region[:, 2 * D:2 * D + COLS // GROUP]

        def words(at, n, dt=F32):
            return g_region[:, 2 * at:2 * (at + n)].bitcast(dt)

        g_words = STEP_TILES * PARTS * D // 2
        raw_i, raw_f = words(0, 2 * COLS, I32), words(2 * COLS, 2 * COLS)
        digit_hi, whole_i, digit_i = words(0, COLS), words(COLS, COLS, I32), words(2 * COLS, COLS, I32)
        digit_lo = words(3 * COLS, COLS, I32)
        small = words(4 * COLS, 512)
        slot = 4 * COLS + 512
        hot_lo = words(slot, SLICE * GROUP * LO).bitcast(BF16).rearrange(
            "p (r t n) -> p r t n", r=2, t=SLICE * GROUP)
        slot += SLICE * GROUP * LO
        hot_hi = words(slot, SLICE * GROUP * HI).bitcast(BF16).rearrange(
            "p (r t n) -> p r t n", r=2, t=SLICE * GROUP)
        slot += SLICE * GROUP * HI
        ramp = words(slot, COLS)
        assert slot + COLS <= g_words - COLS
        dst_t = words(g_words - COLS, COLS)
        rest_buf = words(0, SEVENTH * D).rearrange("p (n d) -> p n d", d=D)
        select = words(COLS, P // LO * P)[0:STACK * LO, :].rearrange("p (h n) -> p h n", h=P // LO)
        own = words(COLS + P // LO * P, STACK)[0:STACK * LO, :]
        low = words(COLS + P // LO * P + STACK, LO)[0:STACK * LO, :]
        counts = words(2 * COLS, SECTIONS * STACK * REACH)[0:STACK * LO, :].rearrange(
            "p (s t c) -> p s t c", s=SECTIONS, t=STACK)
        by_section = words(0, SECTIONS * REACH)[0:STACK * LO, :].rearrange("p (s c) -> p s c", s=SECTIONS)
        deg_lo = words(512, SECTIONS * SPAN + REACH - SPAN)[0:STACK * LO, :]
        assert SECTIONS * STACK * REACH <= 2 * COLS and SECTIONS * REACH <= 512
        b2_f, b2_rest = tmp[0:EXPERTS, :], xn2[0:EXPERTS, :]
        b2_split = acc[:, :, :].rearrange("p r d -> p (r d)")[0:EXPERTS, 0:PARTS * D // 2].bitcast(BF16).rearrange(
            "p (j d) -> p j d", j=PARTS)
        group_at = GROUP * PARTS * D // 2
        hot_g = words(group_at, 2 * GROUP * P // 2).bitcast(BF16).rearrange("p (r t n) -> p r t n", r=2, t=GROUP)
        iota_n = words(group_at + GROUP * P, P)
        shifted = words(group_at + GROUP * P + P, 4 * GROUP)

        xt_buf = [x_ld[:, r, :].rearrange("p (k n) -> p k n", k=KC) for r in range(2)] + [
            xt_ld[:, r, :, :] for r in range(2)]
        wgnn_sb = x2_t[:, :, :, :].rearrange("p r k n -> p r (k n)")
        hid_flat = hid_t[:, :, :, :].rearrange("p r f n -> p (r f n)")
        stat6 = hid_flat[:, 0:6 * BLOCKS].rearrange("p (b s) -> p b s", s=6)
        ln = hid_flat[:, 6 * BLOCKS:14 * BLOCKS].rearrange("p (r b) -> p r b", r=8)
        b1_rows = agg_t[0:EXPERTS * FC, 0, :]
        rows = xt_ld[:, :, :, :].rearrange("p r k n -> p (r k n)")[0:1, :]
        rows2 = h_ld[:, :, :, :].rearrange("p r k n -> p (r k n)").bitcast(F32)[0:1, 0:D + 2 * EXPERTS]
        exp_t = [acc[:, :, :].rearrange("p r d -> p (r d)"), hid_flat[:, 0:QUAD * P]]
        exp_n = [x2_t[:, :, :, :].rearrange("p r k n -> p (r k n)"), hid_flat[:, QUAD * P:2 * QUAD * P]]
        x2_parts = [agg_t[:, n, :].bitcast(BF16) for n in range(2)] + [xn2[:, 0:P].bitcast(BF16)]
        kmax7 = gate[:, 0, :]
        ctx_m, ctx_mt = tmp[:, 0:P], tmp[:, P:2 * P]
        ctx_w = xn2[:, :]
        wq_t = hid_t[:, 1, 0:KC, :]

        s_pad = sem("s_pad")
        s_edges = [sem("s_edges_src"), sem("s_edges_dst")]
        s_x = [sem(f"s_x{n}") for n in range(-(-BLOCKS // 4))]
        s_w = sem("s_w")
        s_wb = sem("s_wb")
        s_split = sem("s_split")
        s_ident = sem("s_ident")
        s_const = sem("s_const")
        s_rawf = sem("s_rawf")
        s_turned = sem("s_turned")
        s_src = sem("s_src")
        s_dst = sem("s_dst")
        s_base = sem("s_base")
        s_basebc = sem("s_basebc")
        s_var = sem("s_var")
        s_std = sem("s_std")
        s_ln = sem("s_ln")
        s_bn = sem("s_bn")
        s_bc = sem("s_bc")
        s_slice = sem("s_slice")
        s_counted = sem("s_counted")
        s_bccopied = sem("s_bccopied")
        s_deg = sem("s_deg")
        s_zeros = sem("s_zeros")
        s_xn = sem("s_xn")
        s_tr = sem("s_tr")
        s_xt = sem("s_xt")
        s_hv = sem("s_hv")
        s_kept = sem("s_kept")
        s_spill = [sem(f"s_spill{r}") for r in range(2)]
        s_spilled = [sem(f"s_spilled{r}") for r in range(4)]
        ps_tr = [psum[0], psum[1]]
        ps_hv = [psum[2], psum[3]]
        ps_count = psum_all[0:STACK * LO, 4 * 512:4 * 512 + SECTIONS * HALF_BANK]
        assert STACK * REACH <= HALF_BANK and SECTIONS * HALF_BANK <= 4 * 512
        assert (BLOCKS - SPLIT) % 7 == 0 and PER_SEVENTH == 2 and SPLIT % 2 == 1
        X_LOADS = [(0, 4), (4, 12), (12, 24), (24, 36), (36, 48), (48, 49)]

        def over_blocks(eng, body, lo, hi, by_four=False):
            if lo == 0:
                body(0, 0)
                body(1, 1)
                lo = 2
            fours = (hi - lo) // 4
            if fours > 1:
                with eng.Fori(0, fours) as four:
                    for n in range(4):
                        turn = ((lo + n - 1) % 4,) if by_four else ()
                        body(four * 4 + (lo + n), (lo + n) % 2, *turn)
                lo += 4 * fours
            for b in range(lo, hi):
                body(b, b % 2, *(((b - 1) % 4,) if by_four else ()))

        def row(ap):
            return ap.rearrange("p a d -> p (a d)")

        def first_of(turn):
            return SPLIT - 1 + (turn - SPLIT + 1) % 4

        def at_least(b, n):
            return not isinstance(b, int) or b >= n

        def project_act(act, in_table):
            def scale(b, r):
                wait(act, s_tr, b - 1)
                passed(act, "act")
                act.activation(xn_buf[:, r, :], row(x_all[:, bass.ds(b, 1), :]), ACT.Identity,
                               scale=ln[:, 5, bass.ds(b, 1)], bias=ln[:, 6, bass.ds(b, 1)]).then_inc(s_xn, 1)

            def turned(b, r, turn=None):
                act.wait_ge(s_tr, b + 1)
                wait(act, s_hv, b - 1)
                if in_table:
                    if at_least(b, SPLIT + 3):
                        act.wait_ge(s_spilled[turn], (b - first_of(turn)) * 4)
                elif at_least(b, 2):
                    act.wait_ge(s_spill[r], (b - r) * 8)
                to = xt_buf[turn] if in_table else xt_buf[r]
                act.copy(to.rearrange("p k n -> p (k n)"), ps_tr[r][:, 0:D]).then_inc(s_xt, 1)

            def keep(b, r):
                act.wait_ge(s_hv, b + 1)
                passed(act, "act")
                act.copy(row(x_all[:, bass.ds(b, 1), :]), ps_hv[r][:, 0:D])
                act.copy(kv_all[:, bass.ds(b, 1), :, :].rearrange("p a r n -> p (a r n)"),
                         ps_hv[r][:, D:2 * D]).then_inc(s_kept, 1)

            def body(b, r, turn=None):
                scale(b, r)
                if at_least(b, 1):
                    turned(b - 1, 1 - r, turn)
                if at_least(b, 2):
                    keep(b - 2, r)

            return body, turned, keep

        def project_pe(pe, in_table):
            def products(b, r, turn=None):
                x_t = xt_buf[turn] if in_table else xt_buf[r]
                pe.wait_ge(s_xt, b + 1)
                wait(pe, s_kept, b - 1)
                for k in range(KC):
                    pe.matmul(ps_hv[r][:, 0:D], x_t[:, k, :], wgnn_sb[:, k, :],
                              start=(k == 0), stop=(k == KC - 1))
                for k in range(KC):
                    pe.matmul(ps_hv[r][:, D:D + P], x_t[:, k, :], wqkv_sb[:, k, 2 * HID:3 * HID],
                              start=(k == 0), stop=(k == KC - 1))
                for k in range(KC):
                    last = pe.matmul(ps_hv[r][:, D + P:D + 2 * P], wqkv_sb[:, k, HID:2 * HID],
                                     x_t[:, k, :], start=(k == 0), stop=(k == KC - 1))
                last.then_inc(s_hv, 1)

            def body(b, r, turn=None):
                pe.wait_ge(s_xn, b + 1)
                wait(pe, s_xt, b - 1)
                for k in range(KC):
                    last = pe.transpose(ps_tr[r][:, k * P:(k + 1) * P], xn_buf[:, r, k * P:(k + 1) * P], ident[:])
                last.then_inc(s_tr, 1)
                if at_least(b, 1):
                    products(b - 1, 1 - r, turn)

            return body, products

        def spill(eng, semaphores, b, r):
            eng.wait_ge(s_xt, b + 1)
            eng.dma_start(xnt[bass.ds(b, 1), :, :].rearrange("a p n -> (a p) n"),
                          xt_buf[r].rearrange("p k n -> p (k n)")).then_inc(semaphores[r], 16)

        with nc.Block() as block:
            @block.sync
            def _(sp):
                whole = (CHUNKS - 1) * P * P
                rest = FULL_TILES - (CHUNKS - 1) * P
                sp.wait_ge(s_pad, 3)
                for n, edges in ((1, dst), (0, src)):
                    raw = raw_i[:, n * COLS:(n + 1) * COLS].rearrange("t (c e) -> t c e", e=P)
                    sp.dma_start(raw[:, 0:CHUNKS - 1, :],
                                 edges[0:whole].rearrange("(c t e) -> t c e", t=P, e=P)).then_inc(s_edges[n], 16)
                    sp.dma_start(raw[0:rest, CHUNKS - 1, :],
                                 edges[whole:FULL_TILES * P].rearrange("(t e) -> t e", e=P)).then_inc(s_edges[n], 16)
                    sp.dma_start(raw[rest:rest + 1, CHUNKS - 1, 0:LAST_EDGES],
                                 edges[FULL_TILES * P:EDGES].rearrange("(a e) -> a e", a=1)).then_inc(s_edges[n], 16)
                under_way = []
                for n, (lo, hi) in enumerate(X_LOADS[:-1]):
                    for at in range(lo, hi, 4):
                        if len(under_way) >= 2:
                            sp.wait_ge(*under_way.pop(0))
                        sp.dma_start(x_all[:, at:at + 4, :], x[at * P:(at + 4) * P, :].rearrange(
                            "(b p) d -> p b d", p=P)).then_inc(s_x[at // 4], 16)
                        under_way.append((s_x[at // 4], 16))
                    if n == 0:
                        sp.dma_start(wgnn_sb, w_gnn.rearrange("(k p) d -> p k d", p=P)).then_inc(s_w, 16)
                        sp.dma_start(wqkv_sb[:], w_qkv.rearrange("(k p) d -> p k d", p=P)).then_inc(s_w, 16)
                sp.dma_start(x_all[0:LAST_ROWS, BLOCKS - 1, :], x[(BLOCKS - 1) * P:NODES, :]).then_inc(s_x[-1], 16)
                sp.dma_start(wout_sb[:], w_out).then_inc(s_wb, 16)
                sp.dma_start(wgate_sb[:], w_gate.rearrange("(k p) d -> p k d", p=P)).then_inc(s_wb, 16)
                sp.dma_start(b1_rows, b1.rearrange("e (f n) -> (e f) n", n=P)).then_inc(s_wb, 16)
                sp.dma_start(b2_f, b2).then_inc(s_wb, 16)
                for to, bias in ((rows[:, 0:D], b_gnn), (rows[:, D:2 * D], prelu_a), (rows2[:, 0:D], b_out),
                                 (rows2[:, D:D + EXPERTS], b_gate),
                                 (rows2[:, D + EXPERTS:D + 2 * EXPERTS], gate_bias)):
                    sp.dma_start(to, bias.rearrange("(a n) -> a n", a=1)).then_inc(s_wb, 16)
                sp.wait_ge(s_split, 5)
                for i in range(PARTS):
                    for j in range(PARTS):
                        at = (i * PARTS + j) * EXPERTS
                        sp.dma_start(b2_parts[at:at + EXPERTS, :], b2_split[:, j, :]).then_inc(s_wb, 16)
                sp.wait_ge(s_wb, (9 + PAIRS_OF_PARTS) * 16)

            @block.gpsimd
            def _(pool):
                last = (CHUNKS - 1) * P
                pool.memset(raw_i[:, last:COLS], 0).then_inc(s_pad, 1)
                pool.memset(raw_i[:, COLS + last:2 * COLS], -1).then_inc(s_pad, 1)
                pool.memset(x_all[:, BLOCKS - 1, :], 0.0).then_inc(s_pad, 1)
                pool.memset(eps_sb[:], EPS).then_inc(s_const, 1)
                pool.memset(ones[:], 1.0).then_inc(s_const, 1)
                pool.memset(ident[:], 0.0).then_inc(s_ident, 1)
                pool.wait_ge(s_ident, 1)
                pool.affine_select(out=ident[:], in_=ident[:], compare_op=ALU.not_equal, fill=1.0, base=0,
                                   pattern=[[-1, P]], channel_multiplier=1).then_inc(s_ident, 1)
                pool.iota(iota_w[:], [[1, WINDOW]], base=0, channel_multiplier=0,
                          allow_small_or_imprecise_dtypes=True).then_inc(s_const, 1)
                pool.memset(small[0:1, 256:258], 0.0).then_inc(s_const, 1)
                pool.iota(ramp, [[PER_GROUP, COLS // GROUP], [0, GROUP]], base=-PER_GROUP, channel_multiplier=0,
                          allow_small_or_imprecise_dtypes=True).then_inc(s_const, 1)
                pool.iota(small[0:1, 258:258 + ALL_GROUPS], [[P, BLOCKS], [0, GROUPS]], base=0,
                          channel_multiplier=0, allow_small_or_imprecise_dtypes=True).then_inc(s_const, 1)
                over_blocks(pool, lambda b, r: spill(pool, s_spill, b, r), 0, SPLIT - 1)

            @block.tensor
            def _(pe):
                pe.wait_ge(s_ident, 2)
                for n in (1, 0):
                    pe.wait_ge(s_rawf, 2 - n)
                    for c in range(CHUNKS):
                        last = pe.transpose(psum[4 * n + c // 4][:, c % 4 * P:(c % 4 + 1) * P],
                                            raw_f[:, n * COLS + c * P:n * COLS + (c + 1) * P], ident[:])
                    last.then_inc(s_turned, 1)
                pe.wait_ge(s_src, 1)
                pe.wait_ge(s_dst, 1)
                pe.wait_ge(s_w, 2 * 16)
                body, products = project_pe(pe, False)
                over_blocks(pe, body, 0, 6)
                pe.wait_ge(s_base, 1)
                pe.wait_ge(s_const, 6)
                pe.matmul(psum[7][:, 0:COLS // GROUP], ones[0:1, :], small[0:1, 0:COLS // GROUP],
                          start=True, stop=True).then_inc(s_basebc, 1)
                over_blocks(pe, body, 6, 8)
                pe.wait_ge(s_wb, 9 * 16)
                pe.matmul(psum[5][:, 0:2 * D], ones[0:1, :], rows, start=True, stop=True)
                pe.matmul(psum[6][:, 0:D], ones[0:1, :], rows2[:, 0:D], start=True, stop=True)
                pe.transpose(psum[6][:, D:D + EXPERTS * FC], b1_rows, ident[0:EXPERTS * FC, 0:EXPERTS * FC])
                for n in range(2):
                    last = pe.matmul(psum[6][:, 3 * P:3 * P + EXPERTS], ones[0:1, :],
                                     rows2[:, D + n * EXPERTS:D + (n + 1) * EXPERTS],
                                     start=(n == 0), stop=(n == 1))
                last.then_inc(s_bc, 1)
                over_blocks(pe, body, 8, BEFORE_COUNT)

                pe.wait_ge(s_zeros, 1)
                pe.wait_ge(s_bccopied, 2)

                def zeros(start):
                    for n in range(4, 8):
                        last = pe.matmul(psum[n][0:STACK * LO, :], hid_zero[:, 0:STACK * LO], hid_zero,
                                         start=start, stop=not start, skip_group_check=True)
                    return last

                def slice_(section, i, r):
                    pe.wait_ge(s_slice, section * SECTION + (i + 1))
                    area = ps_count[:, bass.ds(section * HALF_BANK, STACK * REACH)].rearrange(
                        "p (t c) -> p t c", t=STACK)
                    for g in range(SLICE):
                        at = (i * SLICE + g) * PER_GROUP
                        for t in range(g * GROUP, (g + 1) * GROUP, STACK):
                            last = pe.matmul(area[:, :, at:at + HI],
                                             hot_lo[:, r, t:t + STACK, :].rearrange("p t n -> p (t n)"),
                                             hot_hi[:, r, t:t + STACK, :],
                                             start=False, stop=False, skip_group_check=True)
                    last.then_inc(s_counted, 1)

                zeros(True)
                with pe.Fori(0, SECTIONS) as section:
                    for i in range(SECTION):
                        slice_(section, i, i % 2)
                        if i % 2 == 1:
                            body(section * 2 + (BEFORE_COUNT + i // 2), i // 2)
                zeros(False).then_inc(s_counted, 1)
                over_blocks(pe, body, SPLIT - AFTER_COUNT, SPLIT)
                pe.wait_ge(s_deg, 1)
                for h in range(P // LO):
                    pe.matmul(psum[5][:, 0:BLOCKS], select[:, h, :],
                              deg_lo[:, PER_GROUP:PER_GROUP + DEG_COLS].rearrange(
                                  "p (b h) -> p b h", h=P // LO)[:, :, h],
                              start=(h == 0), stop=(h == P // LO - 1))
                pe.matmul(psum[6][:, 0:1], ones[0:STACK * LO, :], flag[0:STACK * LO, 0:1], start=True, stop=True)
                pe.matmul(psum[6][:, 1:2], ones[0:1, :], flag[0:1, 2:3], start=True, stop=True)
                pe.matmul(psum[6][:, 2:3], ones[:], flag[:, 3:4], start=True, stop=True).then_inc(s_deg, 1)

            @block.scalar
            def _(act):
                act.wait_ge(s_turned, 2)
                for b in range(4):
                    m = min(512, COLS - 512 * b)
                    last = act.copy(src_t[:, 512 * b:512 * b + m], psum[b][:, 0:m])
                last.then_inc(s_src, 1)
                act.wait_ge(s_const, 6)
                body, turned, keep = project_act(act, False)

                def roots(n):
                    lo, hi = X_LOADS[n]
                    act.wait_ge(s_var, n + 1)
                    act.activation(ln[:, 4, lo:hi], ln[:, 3, lo:hi], ACT.Sqrt, bias=eps_sb[:, 0:1]).then_inc(s_std, 1)

                roots(0)
                act.wait_ge(s_ln, 1)
                over_blocks(act, body, 0, 2)
                roots(1)
                over_blocks(act, body, 2, 4)
                act.wait_ge(s_ln, 2)
                over_blocks(act, body, 4, 12)
                for n in range(2, 6):
                    roots(n)
                act.wait_ge(s_basebc, 1)
                act.copy(base_bc, psum[7][:, 0:COLS // GROUP]).then_inc(s_bccopied, 1)
                act.wait_ge(s_bc, 1)
                act.copy(bgnn_bc[:], psum[5][:, 0:D])
                act.copy(prelu_bc[:], psum[5][:, D:2 * D])
                act.copy(bout_bc[:], psum[6][:, 0:D])
                act.copy(b1_t[:], psum[6][:, D:D + EXPERTS * FC])
                act.copy(gate_bc[:], psum[6][:, 3 * P:3 * P + EXPERTS]).then_inc(s_bccopied, 1)
                act.wait_ge(s_ln, 6)
                over_blocks(act, body, 12, SPLIT)

            @block.vector
            def _(dve):
                chain = [0]

                def link(ins):
                    chain[0] += 1
                    ins.then_inc(s_bn, 1)
                    dve.wait_ge(s_bn, chain[0])

                def variances(n):
                    lo, hi = X_LOADS[n]
                    for piece in range(lo // 4, -(-hi // 4)):
                        dve.wait_ge(s_x[piece], 16)
                    moments = lambda b: dve.bn_stats(row(stat6[:, bass.ds(b, 1), :]),
                                                     row(x_all[:, bass.ds(b, 1), :])).then_inc(s_bn, 1)
                    if hi - lo > 4:
                        with dve.Fori(0, 2) as part:
                            for j in range((hi - lo) // 2):
                                moments(part * ((hi - lo) // 2) + (lo + j))
                    else:
                        for b in range(lo, hi):
                            moments(b)
                    chain[0] += hi - lo
                    dve.wait_ge(s_bn, chain[0])
                    st = lambda m: stat6[:, lo:hi, m]
                    to = lambda m: ln[:, m, lo:hi]
                    link(dve.tensor_tensor(to(0), st(1), st(4), ALU.add))
                    link(dve.tensor_scalar(to(0), to(0), 0.5, None, ALU.mult))
                    link(dve.tensor_tensor(to(1), st(1), st(4), ALU.subtract))
                    link(dve.tensor_scalar(to(1), to(1), 0.5, None, ALU.mult))
                    link(dve.tensor_tensor(to(1), to(1), to(1), ALU.mult))
                    link(dve.tensor_tensor(to(2), st(2), st(5), ALU.add))
                    dve.scalar_tensor_tensor(out=to(3), in0=to(2), scalar=1.0 / D, in1=to(1),
                                             op0=ALU.mult, op1=ALU.add).then_inc(s_var, 1)

                def norms(n):
                    lo, hi = X_LOADS[n]
                    dve.wait_ge(s_std, n + 1)
                    link(dve.reciprocal(ln[:, 5, lo:hi], ln[:, 4, lo:hi]))
                    dve.scalar_tensor_tensor(out=ln[:, 6, lo:hi], in0=ln[:, 0, lo:hi], scalar=-1.0,
                                             in1=ln[:, 5, lo:hi], op0=ALU.mult, op1=ALU.mult).then_inc(s_ln, 1)

                dve.memset(hid_zero, 0.0).then_inc(s_zeros, 1)
                dve.wait_ge(s_const, 6)
                for n in (1, 0):
                    dve.wait_ge(s_edges[n], 3 * 16)
                    dve.tensor_copy(raw_f[:, n * COLS:(n + 1) * COLS],
                                    raw_i[:, n * COLS:(n + 1) * COLS]).then_inc(s_rawf, 1)
                variances(0)
                dve.wait_ge(s_turned, 1)
                for b in range(4):
                    m = min(512, COLS - 512 * b)
                    last = dve.tensor_copy(dst_t[:, 512 * b:512 * b + m], psum[4 + b][:, 0:m])
                last.then_inc(s_dst, 1)
                norms(0)
                variances(1)
                dve.wait_ge(s_dst, 1)
                first = small.bitcast(I32)[0:1, 0:COLS // GROUP]
                link(dve.tensor_copy(first, dst_t[0:1, :].rearrange("p (g t) -> p g t", t=GROUP)[:, :, 0]))
                link(dve.tensor_scalar(base[:], first, -LO, None, ALU.bitwise_and))
                dve.tensor_copy(small[0:1, 0:COLS // GROUP], base[:]).then_inc(s_base, 1)
                norms(1)
                for n in range(2, 6):
                    variances(n)
                for n in range(2, 6):
                    norms(n)
                dve.wait_ge(s_turned, 2)
                link(dve.tensor_copy(whole_i, dst_t))
                dve.tensor_scalar(digit_lo, whole_i, LO - 1, None, ALU.bitwise_and)
                link(dve.tensor_scalar(digit_i, whole_i, 4, None, ALU.arith_shift_right))
                link(dve.tensor_tensor(digit_hi, digit_i, ramp, ALU.subtract))
                def slice_(n, r, first):
                    if not first:
                        dve.wait_ge(s_counted, n - 1)
                    for digit, hot, width in ((digit_lo, hot_lo, LO), (digit_hi, hot_hi, HI)):
                        tiles = digit[:, bass.ds(n * (SLICE * GROUP), SLICE * GROUP)]
                        last = dve.tensor_tensor(
                            hot[:, r, :, :],
                            iota_w[:, 0:width].unsqueeze(1).to_broadcast([P, SLICE * GROUP, width]),
                            tiles.unsqueeze(2).to_broadcast([P, SLICE * GROUP, width]), ALU.is_equal)
                    last.then_inc(s_slice, 1)

                for r in range(2):
                    slice_(r, r, True)
                dve.wait_ge(s_bccopied, 1)
                groups = "p (g t) -> p g t"
                link(dve.tensor_tensor(rel[:].rearrange(groups, t=GROUP), dst_t.rearrange(groups, t=GROUP),
                                       base_bc.unsqueeze(2).to_broadcast(
                                           [P, COLS // GROUP, GROUP]), ALU.subtract))
                span = small[:, 480:488]
                dve.tensor_reduce(span[:, 0:1], rel[:, 0:FULL_TILES], AX_X, ALU.min)
                link(dve.tensor_reduce(span[:, 1:2], rel[:, 0:FULL_TILES], AX_X, ALU.max))
                half = rel[0:LAST_EDGES, FULL_TILES:FULL_TILES + 1]
                dve.tensor_tensor(span[0:LAST_EDGES, 0:1], span[0:LAST_EDGES, 0:1], half, ALU.min)
                link(dve.tensor_tensor(span[0:LAST_EDGES, 1:2], span[0:LAST_EDGES, 1:2], half, ALU.max))
                dve.tensor_scalar(span[:, 2:3], span[:, 0:1], 0.0, None, ALU.is_lt)
                link(dve.tensor_scalar(span[:, 3:4], span[:, 1:2], float(WINDOW), None, ALU.is_ge))
                dve.tensor_tensor(flag[:, 3:4], span[:, 2:3], span[:, 3:4], ALU.add)
                link(dve.tensor_tensor(small[0:1, 0:ALL_GROUPS], small[0:1, 0:ALL_GROUPS],
                                       small[0:1, 256:256 + ALL_GROUPS], ALU.is_lt))
                dve.tensor_reduce(flag[0:1, 2:3], small[0:1, 0:ALL_GROUPS], AX_X, ALU.add)
                dve.wait_ge(s_ident, 2)
                corner = ident[0:STACK * LO, 0:STACK * LO]
                dve.tensor_reduce(own, corner.rearrange("p (t n) -> p t n", t=STACK), AX_X, ALU.add)
                dve.tensor_reduce(low, corner.rearrange("p (t n) -> p n t", t=STACK), AX_X, ALU.add)
                dve.tensor_copy(ident_b[:], ident[:])
                dve.wait_ge(s_wb, 9 * 16)
                split = [0]

                def part(ins):
                    split[0] += 1
                    ins.then_inc(s_split, 1)
                    dve.wait_ge(s_split, split[0])

                part(dve.tensor_copy(b2_split[:, 0, :], b2_f))
                part(dve.tensor_tensor(b2_rest, b2_f, b2_split[:, 0, :], ALU.subtract))
                part(dve.tensor_copy(b2_split[:, 1, :], b2_rest))
                part(dve.tensor_tensor(b2_rest, b2_rest, b2_split[:, 1, :], ALU.subtract))
                part(dve.tensor_copy(b2_split[:, 2, :], b2_rest))
                part(dve.tensor_copy(wgate_parts[:, :, 0, :], wgate_sb[:]))
                part(dve.tensor_tensor(wgate_rest[:], wgate_sb[:], wgate_parts[:, :, 0, :], ALU.subtract))
                part(dve.tensor_copy(wgate_parts[:, :, 1, :], wgate_rest[:]))
                dve.tensor_tensor(wgate_parts[:, :, 2, :], wgate_rest[:], wgate_parts[:, :, 1, :], ALU.subtract)
                link(dve.memset(select, 0.0))
                for h in range(P // LO):
                    dve.tensor_copy(select[:, h, h * LO:(h + 1) * LO], low)
                with dve.Fori(1, ALL_GROUPS // SLICE // 2) as pair:
                    for r in range(2):
                        slice_(pair * 2 + r, r, False)
                dve.wait_ge(s_counted, ALL_GROUPS // SLICE + 1)
                for n in range(0, SECTIONS, 2):
                    m = min(2, SECTIONS - n)
                    last = dve.tensor_tensor(
                        counts[:, n:n + m, :, :],
                        ps_count[:, n * HALF_BANK:(n + m) * HALF_BANK].rearrange(
                            "p (s c) -> p s c", s=m)[:, :, 0:STACK * REACH].rearrange(
                            "p s (t c) -> p s t c", t=STACK),
                        own.unsqueeze(1).unsqueeze(3).to_broadcast([STACK * LO, m, STACK, REACH]), ALU.mult)
                link(last)
                link(dve.tensor_reduce(by_section, counts.rearrange("p s t c -> p s c t"), AX_X, ALU.add))
                body_ = deg_lo[:, 0:SECTIONS * SPAN].rearrange("p (s c) -> p s c", s=SECTIONS)
                dve.tensor_copy(deg_lo[:, SECTIONS * SPAN:], by_section[:, SECTIONS - 1, SPAN:REACH])
                link(dve.tensor_copy(body_, by_section[:, :, 0:SPAN]))
                over = body_[:, 1:SECTIONS, 0:REACH - SPAN]
                link(dve.tensor_tensor(over, over, by_section[:, 0:SECTIONS - 1, SPAN:REACH], ALU.add))
                dve.tensor_reduce(flag[0:STACK * LO, 0:1], deg_lo, AX_X, ALU.add).then_inc(s_deg, 1)
                dve.wait_ge(s_deg, 2)
                dve.tensor_copy(dinv[:], psum[5][:, 0:BLOCKS])
                link(dve.tensor_scalar(flag[:, 0:1], psum[6][:, 0:1], float(EDGES), None, ALU.is_lt))
                link(dve.tensor_scalar(flag[:, 1:2], psum[6][:, 1:2], flag[:, 0:1], None, ALU.add))
                link(dve.tensor_scalar(flag[:, 1:2], psum[6][:, 2:3], flag[:, 1:2], 1.0, ALU.add, ALU.min))
                dve.tensor_copy(flag_i[:], flag[0:1, 1:2])

        r_digit = sem("r_digit")
        r_hot = sem("r_hot")
        r_count = sem("r_count")
        r_iota = sem("r_iota")
        hot_a = words(group_at + GROUP * P + 2 * P, GROUP * P).bitcast(BF16).rearrange(
            "p (r t n) -> p r t n", r=2, t=GROUP)
        hist = psum[5]

        s_self = sem("s_self")
        s_root = sem("s_root")
        s_dinv = sem("s_dinv")
        s_hi = sem("s_hi")
        s_rest = sem("s_rest")
        s_mid = sem("s_mid")
        s_low = sem("s_low")
        s_table = [sem(f"s_table{n}") for n in range(SEVENTH)]

        def over_sevenths(eng, body):
            for n in range(SEVENTH):
                body(0, n, n, n % 2)
            with eng.Fori(0, (7 - 1) // 2) as pair:
                for half in range(2):
                    for n in range(SEVENTH):
                        c = pair * 2 + (1 + half)
                        body(c, n, c * SEVENTH + n, (1 + half + n) % 2)

        with nc.Block() as block:
            @block.vector
            def _(dve):
                with dve.If(dve.value_load(flag_i[0:1, 0:1], min_val=0, max_val=1) > 0):
                    dve.wait_ge(r_iota, 1)
                    dve.tensor_scalar(rel[:], rel[:], OFF_GRID, None, ALU.subtract)
                    with dve.Fori(0, ALL_GROUPS) as g:
                        as_i = lambda n: shifted[:, n * GROUP:(n + 1) * GROUP].bitcast(I32)
                        dve.tensor_copy(as_i(0), dst_t[:, bass.ds(g * GROUP, GROUP)]).then_inc(r_digit, 1)
                        dve.wait_ge(r_digit, g * 3 + 1)
                        dve.tensor_scalar(as_i(1), as_i(0), P - 1, None, ALU.bitwise_and).then_inc(r_digit, 1)
                        dve.tensor_scalar(as_i(2), as_i(0), 7, None, ALU.arith_shift_right).then_inc(r_digit, 1)
                        dve.wait_ge(r_digit, g * 3 + 3)
                        for n, hot, width in ((1, hot_g, P), (2, hot_a, BLOCKS)):
                            dve.tensor_tensor(hot[:, 0, :, 0:width],
                                              iota_n[:, 0:width].unsqueeze(1).to_broadcast([P, GROUP, width]),
                                              as_i(n).unsqueeze(2).to_broadcast([P, GROUP, width]),
                                              ALU.is_equal).then_inc(r_hot, 1)
                        dve.wait_ge(r_count, g + 1)
                    dve.wait_ge(r_count, ALL_GROUPS + 1)
                    dve.tensor_copy(dinv[:], hist[:, 0:BLOCKS]).then_inc(r_digit, 1)
                    dve.wait_ge(r_digit, ALL_GROUPS * 3 + 1)
                dve.tensor_scalar(dinv[:], dinv[:], 1.0, None, ALU.add).then_inc(s_self, 1)
                dve.wait_ge(s_root, 1)
                dve.reciprocal(dinv[:], dinv[:]).then_inc(s_dinv, 1)

                def second_part(n, b):
                    dve.wait_ge(s_rest, b + 1)
                    dve.tensor_copy(parts[:, n, 1, :], rest_buf[:, n, :]).then_inc(s_mid, 1)

                def body(c, n, b, r):
                    if n == 0 and at_least(c, 1):
                        dve.tensor_reduce(kmax7[:, bass.ds(c - 1, 1)],
                                          kv_all[:, bass.ds((c - 1) * SEVENTH, SEVENTH), 1, :],
                                          mybir.AxisListType.XY, ALU.max)
                    dve.wait_ge(s_hi, b + 1)
                    wait(dve, s_low, b - (SEVENTH - 1))
                    dve.scalar_tensor_tensor(out=rest_buf[:, n, :], in0=row(x_all[:, bass.ds(b, 1), :]),
                                             scalar=dinv[:, bass.ds(b, 1)], in1=parts[:, n, 0, :],
                                             op0=ALU.mult, op1=ALU.subtract).then_inc(s_rest, 1)
                    if n > 0:
                        second_part(n - 1, b - 1)
                    if n == SEVENTH - 1:
                        second_part(n, b)

                over_sevenths(dve, body)
                last = BLOCKS - 1
                dve.tensor_reduce(kmax7[:, 6:7], kv_all[:, last - SEVENTH + 1:last, 1, :],
                                  mybir.AxisListType.XY, ALU.max)
                dve.tensor_reduce(kmax7[:, 7:8], kv_all[:, last, 1, 0:LAST_ROWS], AX_X, ALU.max
                                  ).then_inc(s_dinv, 1)
                dve.wait_ge(s_dinv, 2)
                dve.tensor_reduce(kmax[:, 1:2], kmax7, AX_X, ALU.max).then_inc(s_dinv, 1)
                dve.wait_ge(s_dinv, 3)
                dve.tensor_scalar(kmax[:, 0:1], kmax[:, 1:2], -1.0, None, ALU.mult)

            @block.gpsimd
            def _(pool):
                pool.iota(iota_n, [[1, P]], base=0, channel_multiplier=0,
                          allow_small_or_imprecise_dtypes=True).then_inc(r_iota, 1)

                def body(c, n, b, r):
                    pool.wait_ge(s_mid, b + 1)
                    pool.tensor_tensor(parts[:, n, 2, :], rest_buf[:, n, :], parts[:, n, 1, :],
                                       ALU.subtract).then_inc(s_low, 1)

                over_sevenths(pool, body)

            @block.sync
            def _(sp):
                def store(c, n, b, r):
                    sp.wait_ge(s_low, b + 1)
                    sp.dma_start(table[bass.ds(b * P, P), :],
                                 parts[:, n, :, :].rearrange("p r d -> p (r d)")).then_inc(s_table[n], 16)

                def body(c, n, b, r):
                    store(c, n, b, r)
                    if n in (2, 5):
                        m = SPLIT - 1 + (n == 5)
                        half = (r - n) % 2
                        spill(sp, s_spilled, c * PER_SEVENTH + m, (m + half * PER_SEVENTH) % 4)

                over_sevenths(sp, body)
                spill(sp, s_spilled, BLOCKS - 1, (BLOCKS - 1) % 4)

            @block.scalar
            def _(act):
                act.wait_ge(s_self, 1)
                act.activation(dinv[:], dinv[:], ACT.Sqrt).then_inc(s_root, 1)
                body, turned, keep = project_act(act, True)

                act.wait_ge(s_dinv, 1)

                for r in range(2):
                    act.wait_ge(s_spill[r], 16 * ((SPLIT - 1) // 2))

                def first_part(c, n):
                    act.wait_ge(s_kept, c * SEVENTH + (n + 1))
                    if at_least(c, 1):
                        act.wait_ge(s_table[n], c * 16)
                    passed(act, "act")
                    act.activation(parts[:, n, 0, :], row(x_all[:, bass.ds(c * SEVENTH + n, 1), :]), ACT.Copy,
                                   scale=dinv[:, bass.ds(c * SEVENTH + n, 1)]).then_inc(s_hi, 1)

                def seventh(c, parity):
                    last = isinstance(c, int) and c == 6
                    for n in range(PER_SEVENTH):
                        b, r = c * PER_SEVENTH + (SPLIT + n), (SPLIT + parity * PER_SEVENTH + n) % 2
                        body(b, r, (SPLIT - 1 + parity * PER_SEVENTH + n) % 4)
                        first_part(c, 3 * n)
                        first_part(c, 3 * n + 1)
                        if not last or n == 0:
                            first_part(c, 3 * n + 2)
                    if last:
                        turned(BLOCKS - 1, 0, (BLOCKS - 1) % 4)
                        keep(BLOCKS - 2, 1)
                        first_part(c, 5)
                        keep(BLOCKS - 1, 0)
                    first_part(c, 6)

                seventh(0, 0)
                with act.Fori(0, 2) as pair:
                    for half in range(2):
                        seventh(pair * 2 + (1 + half), (1 + half) % 2)
                seventh(5, 1)
                seventh(6, 0)

            @block.tensor
            def _(pe):
                with pe.If(pe.value_load(flag_i[0:1, 0:1], min_val=0, max_val=1) > 0):
                    pe.matmul(hist[:, 0:BLOCKS], hid_zero[:, 0:P], hid_zero[:, 0:BLOCKS], start=True, stop=False,
                              skip_group_check=True)
                    with pe.Fori(0, ALL_GROUPS) as g:
                        pe.wait_ge(r_hot, g * 2 + 2)
                        for t in range(GROUP):
                            last = pe.matmul(hist[:, 0:BLOCKS], hot_g[:, 0, t, :], hot_a[:, 0, t, 0:BLOCKS],
                                             start=False, stop=False, skip_group_check=True)
                        last.then_inc(r_count, 1)
                    pe.matmul(hist[:, 0:BLOCKS], hid_zero[:, 0:P], hid_zero[:, 0:BLOCKS], start=False, stop=True,
                              skip_group_check=True).then_inc(r_count, 1)
                body, products = project_pe(pe, True)
                over_blocks(pe, body, SPLIT, BLOCKS, True)
                products(BLOCKS - 1, 0, (BLOCKS - 1) % 4)

        s_zero = sem("s_zero")

        def table_is_stored(eng):
            for n in range(SEVENTH):
                eng.wait_ge(s_table[n], 16 * 7)

        g_idx = sem("g_idx")
        g_in = sem("g_in")
        g_shift = sem("g_shift")
        g_hot = sem("g_hot")
        g_mm = sem("g_mm")
        g_add = sem("g_add")
        ps_gen = psum[0][:, 0:KC * P].rearrange("p (c n) -> p c n", c=KC)

        s_w1 = [sem(f"s_w1_{e}") for e in range(EXPERTS)]
        s_w2 = [sem(f"s_w2_{e}") for e in range(EXPERTS)]
        s_idx = sem("s_idx")
        s_gath = [sem(f"s_gath{q}") for q in range(GROUPS)]
        s_hot = sem("s_hot")
        s_agg = sem("s_agg")
        s_add = sem("s_add")
        s_ld = [sem(f"s_ld{r}") for r in range(2)]
        s_store = [sem(f"s_store{r}") for r in range(2)]
        s_aggt = sem("s_aggt")
        s_a2 = sem("s_a2")
        s_res = sem("s_res")
        s_moment = sem("s_moment")
        s_root2 = sem("s_root2")
        s_rstd = sem("s_rstd")
        s_xn2 = sem("s_xn2")
        s_a4 = sem("s_a4")
        s_x2t = sem("s_x2t")
        s_a6 = sem("s_a6")
        s_lg = sem("s_lg")
        s_x2p = sem("s_x2p")
        s_top = sem("s_top")
        s_diff = sem("s_diff")
        s_e2 = sem("s_e2")
        s_wts = sem("s_wts")
        s_comb = sem("s_comb")
        s_a8 = sem("s_a8")
        s_combt = sem("s_combt")
        s_a9 = sem("s_a9")
        s_b2 = sem("s_b2")
        s_h1 = sem("s_h1")
        s_relu = sem("s_relu")
        s_h2 = sem("s_h2")
        s_out = sem("s_out")
        ps_agg = [psum[0], psum[1]]
        ps_h = [psum[2], psum[3]]
        ps_y = [psum[4], psum[5]]
        ps_a = psum[6]
        ps_b = psum[7]
        RES_OPS = 9
        COMB_OPS = 8
        s_cleared = sem("s_cleared")
        s_exp = sem("s_exp")
        s_exp_tr = sem("s_exp_tr")
        s_exp_n = sem("s_exp_n")
        s_exp_used = sem("s_exp_used")
        s_cchain = sem("s_cchain")
        s_cm = sem("s_cm")
        s_c = sem("s_c")
        s_cev = sem("s_cev")

        def over_steps(eng, body):
            body(0, 0, True, False, False)
            body(1, 1, True, False, True)
            body(2, 0, True, True, True)
            body(3, 1, True, True, True)
            with eng.Fori(0, PAIRS - 1) as pair:
                for parity in range(2):
                    body(pair * 2 + (4 + parity), parity, True, True, True)
            body(BLOCKS - 1, 0, True, True, True)
            body(BLOCKS, 1, False, True, True)
            body(BLOCKS + 1, 0, False, True, False)

        with nc.Block() as block:
            @block.sync
            def _(sp):
                def load_w1(e):
                    sp.dma_start(w1_sb[:, e, :, :], w1[e].rearrange("(k p) f -> p k f", p=P)).then_inc(s_w1[e], 16)

                def load_w2(e):
                    sp.dma_start(w2_sb[:, e, :, :], w2[e].rearrange("(f p) d -> p f d", p=P)).then_inc(s_w2[e], 16)

                def load(b, r, n):
                    wait(sp, s_res, (b - 1) * RES_OPS)
                    at = b * P
                    sp.dma_start(x_ld[0:n, r, :], x[bass.ds(at, n), :]).then_inc(s_ld[r], 16)
                    sp.dma_start(xt_ld[:, r, :, :].rearrange("p k n -> p (k n)"),
                                 xnt[bass.ds(b, 1), :, :].rearrange("a p n -> (a p) n")).then_inc(s_ld[r], 16)
                    sp.dma_start(h_ld[:, r, :, :].rearrange("p k d -> p (k d)"), table[bass.ds(at, P), :]).then_inc(s_ld[r], 16)

                def store(b, r, n):
                    sp.wait_ge(s_out, EXPERTS * (b + 1))
                    sp.dma_start(out[bass.ds(b * P, n), :], acc[0:n, r, :]).then_inc(s_store[r], 16)

                def body(s, r, agg, experts, stage):
                    if agg:
                        load(s, r, LAST_ROWS if isinstance(s, int) and s == BLOCKS - 1 else P)
                    if isinstance(s, int) and s == 0:
                        for e in range(2 * EXPERTS):
                            over = (e + 1) * FC * D - kv_at
                            if over > 0:
                                sp.wait_ge(s_exp_used, min(-(-over // (QUAD * 2 * P)), QUADS + 1))
                            if e < EXPERTS:
                                load_w1(e)
                            else:
                                load_w2(e - EXPERTS)
                    if experts:
                        last = isinstance(s, int) and s == BLOCKS + 1
                        store(s - 2, r, LAST_ROWS if last else P)

                for r in range(2):
                    sp.wait_ge(s_spill[r], 16 * ((SPLIT - 1) // 2))
                for turn in range(4):
                    sp.wait_ge(s_spilled[turn], 16 * ((BLOCKS - 1 - first_of(turn)) // 4 + 1))
                table_is_stored(sp)
                over_steps(sp, body)
                sp.wait_ge(s_store[0], 16 * (BLOCKS // 2 + 1))
                sp.wait_ge(s_store[1], 16 * (BLOCKS // 2))

            @block.gpsimd
            def _(pool):
                irregular = pool.value_load(flag_i[0:1, 0:1], min_val=0, max_val=1)
                table_is_stored(pool)
                with pool.If(irregular > 0):
                    with pool.Fori(0, ALL_GROUPS) as g:
                        pool.wait_ge(g_idx, g + 1)
                        passed(pool, "pool")
                        for t in range(GROUP):
                            pool.indirect_dma_start(
                                out=gathered[:, t, :], out_offset=None, in_=table[:, :],
                                in_offset=bass.IndirectOffsetOnAxis(ap=index[:, t:t + 1], axis=0)
                            ).then_inc(g_in, 16)
                    pool.wait_ge(g_add, ALL_GROUPS * BLOCKS)
                with pool.Fori(0, BLOCKS) as s:
                    for q in range(GROUPS):
                        pool.wait_ge(s_idx, s * GROUPS + (q + 1))
                        passed(pool, "pool")
                        for t in range(q * GROUP, (q + 1) * GROUP):
                            pool.indirect_dma_start(
                                out=gathered[:, t, :], out_offset=None, in_=table[:, :],
                                in_offset=bass.IndirectOffsetOnAxis(ap=index[:, t:t + 1], axis=0)
                            ).then_inc(s_gath[q], 16)

            @block.scalar
            def _(act):
                def body(s, r, agg, experts, stage):
                    b, rb = s - 1, 1 - r

                    def relu(e):
                        if not experts:
                            return
                        at = (s - 2) * EXPERTS + e
                        act.wait_ge(s_h1, at + 1)
                        wait(act, s_h2, at - 1)
                        for f in range(FC):
                            last = act.activation(hid_t[:, e % 2, f, :], ps_h[e % 2][:, f * P:(f + 1) * P],
                                                  ACT.Relu, bias=b1_t[:, e * FC + f:e * FC + f + 1])
                        last.then_inc(s_relu, 1)

                    if isinstance(s, int) and s == 0:
                        def exps(n, r):
                            act.activation(exp_t[r].rearrange("p (b n) -> p b n", n=P),
                                           kv_all[:, bass.ds(n * QUAD, QUAD), 1, :], ACT.Exp,
                                           bias=kmax[:, 0:1]).then_inc(s_exp, 1)

                        exps(0, 0)
                        exps(1, 1)
                        with act.Fori(1, QUADS // 2) as pair:
                            for r in range(2):
                                act.wait_ge(s_exp_tr, pair * 2 + (r - 1))
                                passed(act, "act")
                                exps(pair * 2 + r, r)
                        act.wait_ge(s_exp_tr, QUADS - 1)
                        act.activation(exp_t[0][:, 0:LAST_ROWS], kv_all[:, BLOCKS - 1, 1, 0:LAST_ROWS], ACT.Exp,
                                       bias=kmax[:, 0:1]).then_inc(s_exp, 1)
                        irregular = act.value_load(flag_i[0:1, 0:1], min_val=0, max_val=1)
                        with act.If(irregular < 1):
                            for c in range(KC):
                                act.activation(acc_t[:, c, FIRST_COLS:],
                                               ones[:, 0:1].to_broadcast([P, ACC_COLS - FIRST_COLS]),
                                               ACT.Copy, scale=0.0).then_inc(s_cleared, 1)
                        with act.If(irregular > 0):
                            act.sem_inc(s_cleared, KC)
                    for e in range(4):
                        relu(e)
                    if stage:
                        act.wait_ge(s_add, s * GROUPS + 2 if agg else BLOCKS * GROUPS)
                        wait(act, s_a6, b)
                        passed(act, "act")
                        act.copy(agg_t[:], acc_t[:, :, bass.ds(b * P, P)]).then_inc(s_aggt, 1)
                    relu(4)
                    if stage:
                        act.wait_ge(s_moment, 2 * b + 2)
                        act.activation(mv[:, 2:3], mv[:, 1:2], ACT.Sqrt, bias=eps_sb[:, 0:1]).then_inc(s_root2, 1)
                    relu(5)
                    if stage:
                        act.wait_ge(s_a4, b + 1)
                        wait(act, s_h1, (b - 1) * EXPERTS)
                        act.copy(x2_t[:, rb, :, :].rearrange("p k n -> p (k n)"),
                                 ps_b[:, 0:D]).then_inc(s_x2t, 1)
                    relu(6)
                    if stage:
                        act.wait_ge(s_diff, b + 1)
                        act.activation(gate[:, 2, 1:2], gate[:, 2, 0:1], ACT.Exp).then_inc(s_e2, 1)
                    relu(7)

                over_steps(act, body)

            @block.vector
            def _(dve):
                irregular = dve.value_load(flag_i[0:1, 0:1], min_val=0, max_val=1)
                with dve.If(irregular > 0):
                    dve.memset(acc_region[:], 0.0).then_inc(s_zero, 1)
                    dve.wait_ge(s_zero, 1)
                    moved = shifted[:, 0:GROUP]
                    with dve.Fori(0, ALL_GROUPS) as g:
                        dve.tensor_copy(index[:, 0:GROUP], src_t[:, bass.ds(g * GROUP, GROUP)]).then_inc(g_idx, 1)
                        dve.tensor_copy(moved, dst_t[:, bass.ds(g * GROUP, GROUP)]).then_inc(g_shift, 1)
                        with dve.Fori(0, BLOCKS) as b:
                            dve.wait_ge(g_shift, g * (BLOCKS + 1) + b + 1)
                            dve.tensor_tensor(hot_g[:, 0, :, :], iota_n.unsqueeze(1).to_broadcast([P, GROUP, P]),
                                              moved.unsqueeze(2).to_broadcast([P, GROUP, P]),
                                              ALU.is_equal).then_inc(g_hot, 1)
                            dve.wait_ge(g_hot, g * BLOCKS + b + 1)
                            dve.tensor_scalar(moved, moved, float(P), None, ALU.subtract).then_inc(g_shift, 1)
                            dve.wait_ge(g_mm, g * BLOCKS + b + 1)
                            dve.tensor_tensor(acc_t[:, :, bass.ds(b * P, P)], acc_t[:, :, bass.ds(b * P, P)],
                                              ps_gen, ALU.add).then_inc(g_add, 1)
                            dve.wait_ge(g_add, g * BLOCKS + b + 1)

                def one_hot(s, q):
                    tiles = rel[:, bass.ds(s * STEP_TILES + q * GROUP, GROUP)]
                    dve.tensor_tensor(hot_w[:, q % 2, :, :],
                                      iota_w[:].unsqueeze(1).to_broadcast([P, GROUP, WINDOW]),
                                      tiles.unsqueeze(2).to_broadcast([P, GROUP, WINDOW]),
                                      ALU.is_equal).then_inc(s_hot, 1)

                def fetch(s, q):
                    dve.tensor_copy(index[:, q * GROUP:(q + 1) * GROUP],
                                    src_t[:, bass.ds(s * STEP_TILES + q * GROUP, GROUP)]).then_inc(s_idx, 1)

                def add(s, q):
                    g = s * GROUPS + q
                    at = dve.value_load(base[0:1, bass.ds(g, 1)], min_val=0, max_val=NODES - 1)
                    if q < GROUPS - 1:
                        one_hot(s, q + 1)
                    else:
                        one_hot(s + 1, 0)
                    window = acc_t[:, :, bass.ds(at, WINDOW)]
                    wait(dve, s_add, g)
                    dve.wait_ge(s_agg, g + 1)
                    dve.tensor_tensor(window, window, ps_agg[q % 2][:, 0:KC * WINDOW].rearrange(
                        "p (c n) -> p c n", c=KC), ALU.add).then_inc(s_add, 1)
                    fetch(s + 1, q)

                def body(s, r, agg, experts, stage):
                    b, rb = s - 1, 1 - r
                    x1 = acc[:, rb, :]
                    t0, t1 = tmp[:], xn2[:]

                    def combine(e):
                        if not experts:
                            return
                        at = (s - 2) * EXPERTS + e
                        dve.wait_ge(s_h2, at + 1)
                        wait(dve, s_out, at)
                        dve.scalar_tensor_tensor(out=acc[:, r, :], in0=ps_y[e % 2][:, 0:D],
                                                 scalar=comb[:, r, e:e + 1], in1=acc[:, r, :],
                                                 op0=ALU.mult, op1=ALU.add).then_inc(s_out, 1)

                    first_step = isinstance(s, int) and s == 0
                    if isinstance(s, int) and s == 1:
                        attention_matrix()
                        dve.wait_ge(s_cleared, KC)
                    if first_step:
                        attention_sums(0)
                    if agg:
                        add(s, 0)
                    if first_step:
                        attention_sums(1)
                    combine(0)
                    combine(1)
                    if agg:
                        add(s, 1)
                    if first_step:
                        attention_sums(2)
                    combine(2)
                    if stage:
                        n = b * RES_OPS
                        if not (isinstance(b, int) and b < 2):
                            dve.wait_ge(s_store[rb], (b - rb) * 8)
                        dve.wait_ge(s_ld[rb], (b - rb) * 24 + 48)
                        dve.tensor_tensor(x1, x_ld[:, rb, :], bout_bc[:], ALU.add).then_inc(s_res, 1)
                        dve.wait_ge(s_a2, b + 1)
                        dve.tensor_tensor(t0, h_ld[:, rb, 2, :], ps_a[:, 0:D], ALU.add).then_inc(s_res, 1)
                        dve.wait_ge(s_res, n + 2)
                        dve.tensor_tensor(t0, t0, h_ld[:, rb, 1, :], ALU.add).then_inc(s_res, 1)
                        dve.tensor_tensor(x1, x1, ps_a[:, D:2 * D], ALU.add).then_inc(s_res, 1)
                        dve.wait_ge(s_res, n + 3)
                        dve.tensor_tensor(t0, t0, h_ld[:, rb, 0, :], ALU.add).then_inc(s_res, 1)
                        dve.wait_ge(s_res, n + 5)
                        dve.scalar_tensor_tensor(out=t1, in0=t0, scalar=dinv[:, bass.ds(b, 1)], in1=bgnn_bc[:],
                                                 op0=ALU.mult, op1=ALU.add).then_inc(s_res, 1)
                        dve.wait_ge(s_res, n + 6)
                        dve.scalar_tensor_tensor(out=t0, in0=t1, scalar=0.0, in1=prelu_bc[:],
                                                 op0=ALU.min, op1=ALU.mult).then_inc(s_res, 1)
                        dve.wait_ge(s_res, n + 7)
                        dve.scalar_tensor_tensor(out=t1, in0=t1, scalar=0.0, in1=t0,
                                                 op0=ALU.max, op1=ALU.add).then_inc(s_res, 1)
                        dve.wait_ge(s_res, n + 8)
                        dve.tensor_tensor(x1, x1, t1, ALU.add).then_inc(s_res, 1)
                        dve.wait_ge(s_res, n + 9)
                        dve.bn_stats(stats[:], x1).then_inc(s_moment, 1)
                        dve.wait_ge(s_moment, 2 * b + 1)
                        passed(dve, "dve")
                        dve.bn_aggr(mv[:, 0:2], stats[:]).then_inc(s_moment, 1)
                    combine(3)
                    if agg:
                        add(s, 2)
                    if stage:
                        dve.wait_ge(s_root2, b + 1)
                        dve.reciprocal(mv[:, 3:4], mv[:, 2:3]).then_inc(s_rstd, 1)
                        dve.wait_ge(s_rstd, b + 1)
                        dve.tensor_scalar(xn2[:], x1, mv[:, 0:1], mv[:, 3:4], ALU.subtract,
                                          ALU.mult).then_inc(s_xn2, 1)
                    combine(4)
                    if stage:
                        dve.wait_ge(s_x2t, b + 1)
                        x2 = x2_t[:, rb, :, :].rearrange("p k n -> p (k n)")
                        dve.tensor_copy(x2_parts[0], x2).then_inc(s_x2p, 1)
                        dve.wait_ge(s_x2p, 4 * b + 1)
                        dve.tensor_tensor(t0, x2, x2_parts[0], ALU.subtract).then_inc(s_x2p, 1)
                        dve.wait_ge(s_x2p, 4 * b + 2)
                        dve.tensor_copy(x2_parts[1], t0).then_inc(s_x2p, 1)
                        dve.wait_ge(s_x2p, 4 * b + 3)
                        dve.tensor_tensor(x2_parts[2], t0, x2_parts[1], ALU.subtract).then_inc(s_x2p, 1)
                    combine(5)
                    if stage:
                        logits, top, pair_, hot1, hot2 = (gate[:, n, :] for n in (0, 1, 2, 3, 4))
                        dve.wait_ge(s_a6, b + 1)
                        dve.tensor_reduce(logits, ps_b[:, D:D + PARTS * EXPERTS].rearrange(
                            "p (j e) -> p e j", j=PARTS), AX_X, ALU.add).then_inc(s_lg, 1)
                        dve.wait_ge(s_lg, 2 * b + 1)
                        dve.tensor_tensor(logits, logits, gate_bc[:], ALU.add).then_inc(s_lg, 1)
                        dve.wait_ge(s_lg, 2 * b + 2)
                        passed(dve, "dve")
                        dve.max(top, logits).then_inc(s_top, 1)
                        dve.wait_ge(s_top, 3 * b + 1)
                        passed(dve, "dve")
                        dve.max_index(gate_i[:], top, logits).then_inc(s_top, 1)
                        dve.tensor_tensor(pair_[:, 0:1], top[:, 1:2], top[:, 0:1], ALU.subtract).then_inc(s_diff, 1)
                        dve.wait_ge(s_top, 3 * b + 2)
                        dve.tensor_copy(gate[:, 5, 0:2], gate_i[:, 0:2]).then_inc(s_top, 1)
                        dve.wait_ge(s_e2, b + 1)
                        dve.tensor_scalar(pair_[:, 2:3], pair_[:, 1:2], 1.0, None, ALU.add).then_inc(s_wts, 1)
                        dve.wait_ge(s_wts, 3 * b + 1)
                        dve.reciprocal(pair_[:, 3:4], pair_[:, 2:3]).then_inc(s_wts, 1)
                        dve.wait_ge(s_wts, 3 * b + 2)
                        dve.tensor_tensor(pair_[:, 4:5], pair_[:, 1:2], pair_[:, 3:4], ALU.mult).then_inc(s_wts, 1)
                        dve.wait_ge(s_wts, 3 * b + 3)
                        dve.wait_ge(s_top, 3 * b + 3)
                        dve.tensor_scalar(hot1, iota_e, gate[:, 5, 0:1], pair_[:, 3:4], ALU.is_equal,
                                          ALU.mult).then_inc(s_comb, 1)
                        dve.tensor_scalar(hot2, iota_e, gate[:, 5, 1:2], pair_[:, 4:5], ALU.is_equal,
                                          ALU.mult).then_inc(s_comb, 1)
                        dve.wait_ge(s_comb, COMB_OPS * b + 2)
                        dve.tensor_tensor(comb[:, rb, :], hot1, hot2, ALU.add).then_inc(s_comb, 1)
                        three = lambda ap: ap.unsqueeze(1).to_broadcast([P, PARTS, EXPERTS])
                        dve.wait_ge(s_comb, COMB_OPS * b + 3)
                        wait(dve, s_a8, b)
                        dve.tensor_copy(comb_parts[:, 0, :, :], three(comb[:, rb, :])).then_inc(s_comb, 1)
                        dve.wait_ge(s_comb, COMB_OPS * b + 4)
                        dve.tensor_tensor(comb_rest[:, 0, :], comb[:, rb, :], comb_parts[:, 0, 0, :],
                                          ALU.subtract).then_inc(s_comb, 1)
                        dve.wait_ge(s_comb, COMB_OPS * b + 5)
                        dve.tensor_copy(comb_parts[:, 1, :, :], three(comb_rest[:, 0, :])).then_inc(s_comb, 1)
                        dve.wait_ge(s_comb, COMB_OPS * b + 6)
                        dve.tensor_tensor(comb_rest[:, 1, :], comb_rest[:, 0, :], comb_parts[:, 1, 0, :],
                                          ALU.subtract).then_inc(s_comb, 1)
                        dve.wait_ge(s_comb, COMB_OPS * b + 7)
                        dve.tensor_copy(comb_parts[:, 2, :, :], three(comb_rest[:, 1, :])).then_inc(s_comb, 1)
                    if agg:
                        add(s, 3)
                    combine(6)
                    if stage:
                        dve.wait_ge(s_a8, b + 1)
                        dve.tensor_copy(comb_t[:], ps_b[0:PAIRS_OF_PARTS * EXPERTS, D + P:D + 2 * P]).then_inc(s_combt, 1)
                    combine(7)
                    if stage:
                        dve.wait_ge(s_a9, b + 1)
                        dve.tensor_tensor(x1, x1, ps_a[:, 0:D], ALU.add).then_inc(s_b2, 1)
                        dve.wait_ge(s_b2, b + 1)

                def attention_sums(third):
                    def quad(n, r, m=P, width=QUAD * P):
                        dve.wait_ge(s_exp_tr, n + 1)
                        wait(dve, s_exp_used, n - 1)
                        dve.tensor_copy(exp_n[r][0:m, 0:width], ps_h[r][0:m, 0:width]).then_inc(s_exp_n, 1)

                    lo = third * (QUADS // 6)
                    if third == 0:
                        quad(0, 0)
                        quad(1, 1)
                        lo = 1
                    with dve.Fori(lo, (third + 1) * (QUADS // 6)) as pair:
                        for r in range(2):
                            quad(pair * 2 + r, r)
                    if third == 2:
                        quad(QUADS, 0, LAST_ROWS, P)

                def attention_matrix():
                    dve.memset(ctx_m, 0.0).then_inc(s_cchain, 1)
                    dve.wait_ge(s_exp_used, QUADS + 1)
                    dve.reciprocal(flag[:, 3:4], ps_y[1][:, 0:1]).then_inc(s_cchain, 1)
                    dve.wait_ge(s_cchain, 2)
                    for h in range(HEADS):
                        at = slice(h * HEAD, (h + 1) * HEAD)
                        last = dve.tensor_scalar(ctx_m[at, at], ps_y[0][at, at], flag[at, 3:4], HEAD ** -0.5,
                                                 ALU.mult, ALU.mult)
                    last.then_inc(s_cm, 1)
                    dve.wait_ge(s_c, 2)
                    dve.tensor_copy(ctx_mt, ps_a[:, 0:P]).then_inc(s_cev, 1)
                    dve.tensor_copy(wq_t.rearrange("p k n -> p (k n)"), ps_b[:, 0:D]).then_inc(s_cev, 1)
                    dve.wait_ge(s_c, 3)
                    dve.tensor_copy(ctx_w, ps_a[:, P:P + D]).then_inc(s_cev, 1)
                    dve.wait_ge(s_c, 4)
                    dve.tensor_copy(mix_w[:].rearrange("p k n -> p (k n)"), ps_h[0][:, :]).then_inc(s_cev, 1)

                for q in range(GROUPS):
                    fetch(0, q)
                one_hot(0, 0)
                with dve.If(irregular < 1):
                    dve.memset(acc_t[:, :, 0:FIRST_COLS], 0.0).then_inc(s_zero, 1)
                dve.wait_ge(s_zero, 1)
                over_steps(dve, body)

            @block.tensor
            def _(pe):
                with pe.If(pe.value_load(flag_i[0:1, 0:1], min_val=0, max_val=1) > 0):
                    with pe.Fori(0, ALL_GROUPS) as g:
                        pe.wait_ge(g_in, (g + 1) * (16 * GROUP))
                        passed(pe, "pe")
                        with pe.Fori(0, BLOCKS) as b:
                            pe.wait_ge(g_hot, g * BLOCKS + b + 1)
                            for c in range(KC):
                                for n in range(PARTS * GROUP):
                                    t, part = n // PARTS, n % PARTS
                                    at = part * D + c * P
                                    last = pe.matmul(ps_gen[:, c, :], gathered[:, t, at:at + P],
                                                     hot_g[:, 0, t, :], start=(n == 0),
                                                     stop=(n == PARTS * GROUP - 1))
                            last.then_inc(g_mm, 1)

                def attention_sums(third):
                    def turn(n, r, rows_of=(P,) * QUAD):
                        pe.wait_ge(s_exp, n + 1)
                        wait(pe, s_exp_n, n - 1)
                        for j, m in enumerate(rows_of):
                            last = pe.transpose(ps_h[r][0:m, j * P:(j + 1) * P], exp_t[r][:, j * P:j * P + m],
                                                ident[:])
                        last.then_inc(s_exp_tr, 1)

                    def products(n, r, rows_of=(P,) * QUAD):
                        pe.wait_ge(s_exp_n, n + 1)
                        first, final = isinstance(n, int) and n == 0, isinstance(n, int) and n == QUADS
                        for j, m in enumerate(rows_of):
                            e = exp_n[r][0:m, j * P:(j + 1) * P]
                            pe.matmul(ps_y[0][:, 0:P], e, row(kv_all[0:m, bass.ds(n * QUAD + j, 1), 0, :]),
                                      start=first and j == 0, stop=final, skip_group_check=True)
                            last = pe.matmul(ps_y[1][:, 0:1], e, ones[0:m, 0:1], start=first and j == 0,
                                             stop=final, skip_group_check=True)
                        last.then_inc(s_exp_used, 1)

                    lo = third * (QUADS // 6)
                    if third == 0:
                        turn(0, 0)
                        turn(1, 1)
                        products(0, 0)
                        lo = 1
                    with pe.Fori(lo, (third + 1) * (QUADS // 6)) as pair:
                        for r in range(2):
                            turn(pair * 2 + r, r)
                            products(pair * 2 + (r - 1), 1 - r)
                    if third == 2:
                        turn(QUADS, 0, (LAST_ROWS,))
                        products(QUADS - 1, 1)
                        products(QUADS, 0, (LAST_ROWS,))

                def attention_matrix():
                    for k in range(KC):
                        last = pe.transpose(ps_b[:, k * P:(k + 1) * P], wqkv_sb[:, k, 0:HID], ident[:])
                    last.then_inc(s_c, 1)
                    pe.wait_ge(s_cm, 1)
                    pe.transpose(ps_a[:, 0:P], ctx_m, ident[:]).then_inc(s_c, 1)
                    pe.wait_ge(s_cev, 1)
                    pe.matmul(ps_a[:, P:P + D], ctx_mt, wout_sb[:], start=True, stop=True).then_inc(s_c, 1)
                    pe.wait_ge(s_cev, 3)
                    for k in range(KC):
                        last = pe.matmul(ps_h[0][:, k * D:(k + 1) * D], wq_t[:, k, :], ctx_w,
                                         start=True, stop=True)
                    last.then_inc(s_c, 1)
                    pe.wait_ge(s_cev, 4)

                def body(s, r, agg, experts, stage):
                    b, rb = s - 1, 1 - r

                    def aggregate(q):
                        if not agg:
                            return
                        g = s * GROUPS + q
                        pe.wait_ge(s_hot, g + 1)
                        wait(pe, s_add, g - 1)
                        pe.wait_ge(s_gath[q], s * (16 * GROUP) + 16 * GROUP)
                        for c in range(KC):
                            for n in range(PARTS * GROUP):
                                t, at = n // PARTS, n % PARTS * D + c * P
                                last = pe.matmul(ps_agg[q % 2][:, c * WINDOW:(c + 1) * WINDOW],
                                                 gathered[:, q * GROUP + t, at:at + P], hot_w[:, q % 2, t, :],
                                                 start=(n == 0), stop=(n == PARTS * GROUP - 1))
                        last.then_inc(s_agg, 1)

                    def up(e, b_=None):
                        block_, x2 = (s - 2, x2_t[:, r, :, :]) if b_ is None else (b_, x2_t[:, b_ % 2, :, :])
                        at = block_ * EXPERTS + e
                        wait(pe, s_relu, at - 1)
                        if isinstance(block_, int) and block_ == 0:
                            pe.wait_ge(s_w1[e], 16)
                        for f in range(FC):
                            for k in range(KC):
                                last = pe.matmul(ps_h[e % 2][:, f * P:(f + 1) * P],
                                                 w1_sb[:, e, k, f * P:(f + 1) * P], x2[:, k, :],
                                                 start=(k == 0), stop=(k == KC - 1))
                        last.then_inc(s_h1, 1)

                    def down(e):
                        at = (s - 2) * EXPERTS + e
                        pe.wait_ge(s_relu, at + 1)
                        wait(pe, s_out, at - 1)
                        if isinstance(s, int) and s == 2:
                            pe.wait_ge(s_w2[e], 16)
                        for f in range(FC):
                            last = pe.matmul(ps_y[e % 2][:, 0:D], hid_t[:, e % 2, f, :], w2_sb[:, e, f, :],
                                             start=(f == 0), stop=(f == FC - 1))
                        last.then_inc(s_h2, 1)

                    def sums_by_node():
                        pe.wait_ge(s_aggt, b + 1)
                        wait(pe, s_b2, b)
                        for k in range(KC):
                            pe.transpose(ps_a[:, k * P:(k + 1) * P], agg_t[:, k, :], ident[:])
                        pe.wait_ge(s_ld[rb], (b - rb) * 24 + 48)
                        for k in range(KC):
                            last = pe.matmul(ps_a[:, D:2 * D], xt_ld[:, rb, k, :], mix_w[:, k, :],
                                             start=(k == 0), stop=(k == KC - 1))
                        last.then_inc(s_a2, 1)

                    def turn_xn2():
                        pe.wait_ge(s_xn2, b + 1)
                        for k in range(KC):
                            last = pe.transpose(ps_b[:, k * P:(k + 1) * P], xn2[:, k * P:(k + 1) * P], ident[:])
                        last.then_inc(s_a4, 1)

                    def logits():
                        pe.wait_ge(s_x2p, 4 * b + 4)
                        for n in range(PARTS * KC):
                            i, k = n // KC, n % KC
                            last = pe.matmul(ps_b[:, D:D + PARTS * EXPERTS], x2_parts[i][:, k * P:(k + 1) * P],
                                             wgate_parts[:, k, :, :].rearrange("p j e -> p (j e)"),
                                             start=(n == 0), stop=(n == PARTS * KC - 1))
                        last.then_inc(s_a6, 1)
                        if isinstance(s, int) and s == 1:
                            up(0, 0)
                            up(1, 0)

                    def turn_weights():
                        pe.wait_ge(s_comb, COMB_OPS * b + 8)
                        pe.matmul(ps_b[0:PAIRS_OF_PARTS * EXPERTS, D + P:D + 2 * P],
                                  comb_parts[:, :, :, :].rearrange("p i j e -> p (i j e)"), ident_b[:],
                                  start=True, stop=True).then_inc(s_a8, 1)

                    def bias2():
                        pe.wait_ge(s_combt, b + 1)
                        pe.matmul(ps_a[:, 0:D], comb_t[:], b2_parts[:], start=True, stop=True).then_inc(s_a9, 1)

                    after = {1: [lambda: aggregate(1)], 2: [sums_by_node], 3: [lambda: aggregate(2)],
                             4: [turn_xn2], 5: [logits, lambda: aggregate(3)], 6: [turn_weights], 7: [bias2]}
                    work = {sums_by_node, turn_xn2, logits, turn_weights, bias2}
                    if isinstance(s, int) and s == 0:
                        for q in range(GROUPS):
                            if q < 3:
                                attention_sums(q)
                            aggregate(q)
                        return
                    if isinstance(s, int) and s == 1:
                        attention_matrix()
                    aggregate(0)
                    ahead = 2 if isinstance(s, int) and s == 2 else 0
                    if experts and ahead == 0:
                        up(0)
                    for e in range(EXPERTS):
                        if experts:
                            if ahead <= e + 1 < EXPERTS:
                                up(e + 1)
                            down(e)
                        for piece in after.get(e, ()):
                            if stage or piece not in work:
                                piece()

                over_steps(pe, body)


_INS = ['x', 'src', 'dst', 'L0_gnn_W', 'L0_gnn_b', 'L0_gnn_prelu_a', 'L0_mix_W_qkv', 'L0_mix_W_out',
        'L0_mix_b_out', 'L0_ffn_Wg', 'L0_ffn_bg', 'L0_ffn_bias', 'L0_ffn_W1', 'L0_ffn_b1', 'L0_ffn_W2',
        'L0_ffn_b2']


def kernel(**inputs):
    import numpy as _np
    import concourse.bacc as _bacc
    from concourse import mybir as _mybir
    from concourse.bass_utils import run_bass_kernel_spmd as _run

    nc = _bacc.Bacc("TRN2", target_bir_lowering=False, num_devices=1)
    arrays, args = {}, []
    for name in _INS:
        a = _np.ascontiguousarray(inputs[name])
        arrays[f"in_{name}"] = a
        args.append(nc.dram_tensor(f"in_{name}", a.shape, _mybir.dt.from_np(a.dtype), kind="ExternalInput").ap())
    f32 = _mybir.dt.float32
    args.append(nc.dram_tensor("out_0", (NODES, D), f32, kind="ExternalOutput").ap())
    args.append(nc.dram_tensor("table", (BLOCKS * P, PARTS * D), _mybir.dt.bfloat16, kind="Internal").ap())
    args.append(nc.dram_tensor("xnt", (BLOCKS, P, D), f32, kind="Internal").ap())
    gps_layer(nc, *args)
    r = _run(nc, [arrays], core_ids=[0])
    return r.results[0]["out_0"]
```
